# Optimizing a Trainium2 kernel written in Bass

```python
import numpy as np
import jax
import jax.numpy as jnp

def _softmax(x, axis=-1):
    return jax.nn.softmax(x, axis=axis)
def _gelu(x):
    return jax.nn.gelu(x, approximate=True)
def _silu(x):
    return jax.nn.silu(x)
def _sigmoid(x):
    return jax.nn.sigmoid(x)
def _layernorm(x, axis=-1, eps=1e-5):
    m = jnp.mean(x, axis=axis, keepdims=True)
    v = jnp.var(x, axis=axis, keepdims=True)
    return (x - m) / jnp.sqrt(v + eps)
def _scatter_add(tgt, idx, src, axis=0):
    return tgt.at[idx].add(src)
def _segment_sum(src, seg, n):
    return jax.ops.segment_sum(src, seg, n)

kernel_name = 'mk_conv_preact_d2_conv_nhwc192_845b2f'

def setup_inputs(seed: int = 0):
    np.random.seed(seed)
    _w = jnp.asarray
    def _rec_inputs():
        import jax
        import jax.numpy as jnp
        _gk = jax.random.key(seed)
        x = -0.0002221 + 1 * jax.random.normal(jax.random.fold_in(_gk, 1), (8, 128, 128, 192), jnp.float32)
        return x
    x = _rec_inputs()
    def _L0_conv_setup():
        import jax, jax.numpy as jnp
        import numpy as np
        from jax import lax
        B, H, W, C = (8, 128, 128, 192)
        NUM_HEADS = 4
        EPS = 1e-12

        def _l2_normalize(x, axis=-1):
            sq = jnp.sum(x * x, axis=axis, keepdims=True)
            return x * lax.rsqrt(jnp.maximum(sq, EPS))
        key = jax.random.key(seed)
        k1, k2, k3, k4 = jax.random.split(key, 4)
        x = jax.random.normal(k1, (B, H, W, C), dtype=jnp.float32)
        qkv_w = jax.random.normal(k2, (C, 3 * C), dtype=jnp.float32) * 0.05
        dw_w = jax.random.normal(k3, (3, 3, 1, 3 * C), dtype=jnp.float32) * 0.05
        proj_w = jax.random.normal(k4, (C, C), dtype=jnp.float32) * 0.05
        temperature = jnp.ones((NUM_HEADS, 1, 1), dtype=jnp.float32)
        return {'x': x, 'qkv_w': qkv_w, 'dw_w': dw_w, 'proj_w': proj_w, 'temperature': temperature}
    _L0_conv_all = _L0_conv_setup()
    _L0_conv_in = {k: v for k, v in _L0_conv_all.items() if k in ('qkv_w', 'dw_w', 'proj_w', 'temperature', )}
    del _L0_conv_all

    def _L1_conv_setup():
        import jax, jax.numpy as jnp
        import numpy as np
        G = 16
        K = 3
        key = jax.random.key(seed)
        feature = jax.random.normal(key, (2, 128, 192, 192), dtype=jnp.float32)
        return {'feature': feature}
    _L1_conv_all = _L1_conv_setup()
    _L1_conv_in = {k: v for k, v in _L1_conv_all.items() if k in ()}
    del _L1_conv_all

    return {
        "x": x,
        "L0_conv_qkv_w": _L0_conv_in["qkv_w"],
        "L0_conv_dw_w": _L0_conv_in["dw_w"],
        "L0_conv_proj_w": _L0_conv_in["proj_w"],
        "L0_conv_temperature": _L0_conv_in["temperature"],
    }

def reference(x, L0_conv_qkv_w, L0_conv_dw_w, L0_conv_proj_w, L0_conv_temperature):
    import jax
    import jax.numpy as jnp
    def _L0_conv_ref(x, qkv_w, dw_w, proj_w, temperature):
        import jax, jax.numpy as jnp
        import numpy as np
        from jax import lax
        B, H, W, C = (8, 128, 128, 192)
        NUM_HEADS = 4
        EPS = 1e-12

        def _l2_normalize(x, axis=-1):
            sq = jnp.sum(x * x, axis=axis, keepdims=True)
            return x * lax.rsqrt(jnp.maximum(sq, EPS))
        b, h, w, c = x.shape
        heads = NUM_HEADS
        c_head = c // heads
        hw = h * w
        qkv = jnp.einsum('bhwc,cd->bhwd', x, qkv_w)
        qkv = lax.conv_general_dilated(qkv, dw_w, window_strides=(1, 1), padding='SAME', dimension_numbers=('NHWC', 'HWIO', 'NHWC'), feature_group_count=3 * c)
        q, k, v = jnp.split(qkv, 3, axis=-1)
        q = q.reshape(b, heads, c_head, hw)
        k = k.reshape(b, heads, c_head, hw)
        v = v.reshape(b, heads, c_head, hw)
        q = _l2_normalize(q, axis=-1)
        k = _l2_normalize(k, axis=-1)
        attn = jnp.einsum('bncs,bnds->bncd', q, k)
        attn = attn * temperature[None]
        attn = jax.nn.softmax(attn, axis=-1)
        out = jnp.einsum('bncd,bnds->bncs', attn, v)
        out = out.reshape(b, h, w, c)
        out = jnp.einsum('bhwc,cd->bhwd', out, proj_w)
        return out

    def _L1_conv_ref(feature):
        import jax, jax.numpy as jnp
        import numpy as np
        G = 16
        K = 3
        B, C, H, W = feature.shape
        Cg = C // G
        Hm, Wm = (H - K + 1, W - K + 1)
        L = Hm * Wm
        slices = [feature[:, :, ki:ki + Hm, kj:kj + Wm] for ki in range(K) for kj in range(K)]
        patches = jnp.stack(slices, axis=2)
        motif = patches.reshape(B, G, Cg * 9, L).reshape(B, G, 9, Cg, L)
        gram = jnp.einsum('bgjcl,bgjdl->bgjcd', motif, motif)
        sq = jnp.einsum('bgjcl,bgjcl->bgjc', motif, motif)
        d2 = sq[..., :, None] + sq[..., None, :] - 2.0 * gram
        eye = jnp.eye(Cg, dtype=bool)
        d2 = jnp.where(eye, jnp.inf, d2)
        nn_idx = jnp.argmin(d2, axis=-1)
        u_max = jnp.max(nn_idx, axis=-1)
        c_max = jnp.sum(nn_idx == u_max[..., None], axis=-1).astype(feature.dtype)
        motif_nn = jnp.take_along_axis(motif, u_max[..., None, None], axis=3)
        term = jnp.floor(motif * motif_nn * c_max[..., None, None] / Cg)
        batch_mask = (jnp.arange(B) != 0).astype(feature.dtype).reshape(B, 1, 1, 1, 1)
        out_ser = motif * batch_mask + term
        ser2 = out_ser.reshape(B, G, 9 * Cg, L).reshape(B, G, Cg, 9, Hm, Wm)
        out = jnp.zeros((B, G, Cg, H, W), feature.dtype)
        for k in range(K * K):
            ki, kj = (k // K, k % K)
            out = out.at[:, :, :, ki:ki + Hm, kj:kj + Wm].add(ser2[:, :, :, k])
        return out.reshape(B, C, H, W)

    def _gn(v, G=32, eps=1e-5):
        B_, H_, W_, C_ = v.shape
        g = v.reshape(B_, H_, W_, G, C_ // G)
        m = jnp.mean(g, axis=(1, 2, 4), keepdims=True)
        s = jnp.var(g, axis=(1, 2, 4), keepdims=True)
        return ((g - m) / jnp.sqrt(s + eps)).reshape(v.shape)

    def _ln_c(v, eps=1e-6):
        m = jnp.mean(v, axis=-1, keepdims=True)
        s = jnp.var(v, axis=-1, keepdims=True)
        return (v - m) / jnp.sqrt(s + eps)

    def _ln_t(v, eps=1e-5):
        m = jnp.mean(v, axis=-1, keepdims=True)
        s = jnp.var(v, axis=-1, keepdims=True)
        return (v - m) / jnp.sqrt(s + eps)

    def _to_tokens(v):
        B_, H_, W_, C_ = v.shape
        return v.reshape(B_, H_ * W_, C_)
    def _from_tokens(t, like):
        return t.reshape(like.shape)

    x = x + _L0_conv_ref(_gn(x), L0_conv_qkv_w, L0_conv_dw_w, L0_conv_proj_w, L0_conv_temperature)
    x = x + _L1_conv_ref(_gn(x))
    return x


_drawn_inputs = setup_inputs


def setup_inputs(seed=0):
    import zlib

    import numpy as np

    out = dict(_drawn_inputs(seed))
    spreads = {'L0_conv_temperature': (1.0, 0.2)}
    factors = {}
    for name, (base, spread) in spreads.items():
        noise = np.random.default_rng([zlib.crc32(name.encode()), seed]).standard_normal(out[name].shape)
        drawn = base * np.exp(spread * noise) if base else spread * noise
        out[name] = jnp.asarray(drawn.astype(out[name].dtype))
    for name, factor in factors.items():
        out[name] = (out[name] * factor).astype(out[name].dtype)
    return out
```

```python
from contextlib import ExitStack

import numpy as np

import concourse.bass as bass
from concourse import mybir

F32 = mybir.dt.float32
BF16 = mybir.dt.bfloat16
U32 = mybir.dt.uint32
ALU = mybir.AluOpType
ACT = mybir.ActivationFunctionType
AX = mybir.AxisListType.X

H, W, C = 128, 128, 192
PLANE = W * C
IMG = H * PLANE
GROUPS, GC = 32, 6
HEADS, CH = 4, 48
THIRD = 64
SEG = 16384 // THIRD
MG, MC = 16, 8
HM, WM = W - 2, C - 2
NW = 9 * MC
PAD = 512
MAGIC = 12582912.0
WB = 5
FR = 8
NF = W // FR
HALO = FR + 2


def const_layout():
    widths = dict(ident=128, avg=128, left=6 * C, ones=128, sel=15 * NW, sele=6 * NW, icol=96, i72=NW,
                  bmask=NW, self8=8, w8=8, jrow=9, ktab=9, ctab=NF, rep=128, sela=9, selk=81, base=NF,
                  cnt=3 * C)
    at, out = 0, {}
    for k, w in widths.items():
        out[k] = (at, w)
        at += w
    return out, at


def const_table():
    lay, n = const_layout()
    t = np.zeros((128, n), np.float32)

    def put(name, a):
        o, w = lay[name]
        a = a.reshape(a.shape[0], -1)
        assert a.shape[1] == w
        t[:a.shape[0], o:o + w] = a

    put("ident", np.eye(128))
    put("avg", np.full((128, 128), 1.0 / 128))
    put("ones", np.ones((128, 128)))
    sel = np.zeros((128, 3, WB, NW))
    sele = np.zeros((128, 6, NW))
    for ki in range(3):
        for y in range(MC):
            for kj in range(3):
                m = y * 9 + ki * 3 + kj
                for wl in range(WB):
                    sel[wl * 24 + ki * MC + y, kj, wl, m] = 1
                for n_, (j, a, sign) in enumerate(EDGES):
                    if j == kj:
                        sele[a % 2 * 24 + ki * MC + y, n_, m] = sign
    put("sel", sel)
    put("sele", sele)
    icol = np.zeros((128, 96))
    for s in range(2):
        for c in range(CH):
            icol[64 * s + c, CH * s + c] = 1
    put("icol", icol)
    put("i72", np.eye(NW))
    m = np.arange(NW)
    put("bmask", (m[:, None] // 8 == m[None] // 8) * 1.0)
    put("self8", (m[:, None] % 8 == np.arange(8)[None]) * 1e30)
    put("w8", np.broadcast_to(8.0 - np.arange(8), (128, 8)))
    put("jrow", np.broadcast_to(np.arange(9.0), (128, 9)))
    put("ktab", np.broadcast_to(8.0 * np.arange(9), (128, 9)))
    g = np.arange(MG)
    chunk = (FR * np.arange(NF) - 2) * C + PAD
    put("ctab", g[:, None] * MC * PLANE + chunk[None])
    p = np.arange(128)
    put("rep", (g[:, None] == p[None] % MG) * 1.0)
    put("sela", (p[:, None] // MG == np.arange(9)[None]) * 1.0)
    i, k, j = p[:, None, None] // MG, np.arange(9)[None, :, None], np.arange(9)[None, None]
    put("selk", ((9 * i + k) // 8 == j) * 0.125)
    put("base", (p % MG)[:, None] * MC * PLANE + chunk[None])
    cols = np.full(C, 3.0)
    cols[[0, -1]], cols[[1, -2]] = 1, 2
    net = np.full(C, MAGIC)
    net[[1, -2]] = 0
    left = np.zeros((3, 2, C))
    left[0, 0] = left[1, 0] = left[1, 1] = left[2, 1] = net
    put("left", np.broadcast_to(left.reshape(1, -1), (128, 6 * C)))
    put("cnt", np.broadcast_to((np.arange(1, 4)[:, None] * cols[None]).ravel(), (128, 3 * C)))
    return t


EDGES = [(1, 2, 1), (1, 0, -1), (2, 2, 1), (2, 3, 1), (2, 0, -1), (2, 1, -1)]

STATS, QKV0, MIX0, QKV1, MIX1, NORM, GRAM, FOLD = range(8)
STEPS = 9


def motif_kernel(nc, x, qkv_w, dw_w, proj_w, temp, cst_d, out, B):
    x1d = nc.dram_tensor("x1_rows", [IMG], F32, kind="Internal").ap()
    xnd = nc.dram_tensor("x1_normed", [PAD + IMG + PAD], F32, kind="Internal").ap()
    vd = nc.dram_tensor("v_pieces", [128, CH * SEG], F32, kind="Internal").ap()
    xf = x.rearrange("b y w c -> b (y w c)")
    outf = out.rearrange("b y w c -> b (y w c)")
    lay, ncst = const_layout()

    ctx = ExitStack()
    with ctx:
        def sb(name, shape, dt=F32):
            return ctx.enter_context(nc.sbuf_tensor(name, shape, dt))

        def sem(name):
            return ctx.enter_context(nc.semaphore(name))

        cst = sb("cst", [128, ncst])

        def c_(name, rows=128):
            o, w = lay[name]
            return cst[0:rows, o:o + w]

        w_lo = sb("w_lo", [128, 3 * C])
        w_hi = sb("w_hi", [128, 2, 3 * C])
        pw = sb("pw", [128, 4, C])
        dwt = sb("dwt", [128, 9, 9])
        tcol = sb("tcol", [128, 2])
        ablk = sb("ablk", [128, 128])
        at = sb("at", [128, 96])
        small = sb("small", [128, 2048])
        cnt = sb("cnt", [128, 3, C])
        ident_b = sb("ident_b", [128, 128], BF16)
        left_b = sb("left_b", [128, 3, 2 * C], BF16)
        zrow = sb("zrow", [1, PAD])
        idxa = sb("idxa", [128, NF], U32)
        idxb = sb("idxb", [MG, 9, NF], U32)
        arena = sb("arena", [128, 37900])
        bank = [ctx.enter_context(nc.psum_tensor(f"bank{i}", [128, 512], F32)) for i in range(8)]

        xs = arena[:, 0:24576].rearrange("p (i r c) -> p i r c", i=4, c=C)
        xs3 = arena[:, 0:24576].rearrange("p (i f) -> p i f", i=4)
        bst = small[:, 0:768].rearrange("p (g n) -> p g n", g=GROUPS)
        mv = small[:, 768:832].rearrange("p (g n) -> p g n", g=GROUPS)
        dev = small[:, 832:864]
        var = small[:, 864:896]
        mean = small[:, 896:928]
        rstd = small[:, 928:960]
        nbias = small[:, 960:992]
        wide = small[:, 1024:1536].rearrange("p (n c) -> p n c", n=2)
        gnp = small[:, 992:996]
        mrow = small[:, 1024:1408].rearrange("p (a c) -> p a c", a=2)
        rrow = small[:, 1536:1920].rearrange("p (a c) -> p a c", a=2)

        NQ = CH * SEG
        qb = arena[:, 0:NQ]
        kb = arena[:, NQ:2 * NQ]
        o0 = 2 * NQ
        pre = arena[:, o0:o0 + 9 * 6 * 130].rearrange("p (t r c) -> p t r c", t=9, r=6)
        o0 += 9 * 6 * 130
        xa = [arena[:, o0 + 1536 * i:o0 + 1536 * (i + 1)].rearrange("p (s f) -> p s f", s=2) for i in range(1)]
        o0 += 1536
        xlo = [arena[:, o0:o0 + 1024].rearrange("p (s n) -> p s n", s=2)]
        o0 += 1024
        xhi = [arena[:, o0:o0 + 512]]
        o0 += 512
        vst = [arena[:, o0:o0 + 1536]]
        o0 += 1536
        acc = [arena[:, o0 + 512 * i:o0 + 512 * (i + 1)] for i in range(3)]
        o0 += 1536
        assert o0 <= 37900, o0
        junk = small[:, 1536:1792]
        sq = small[:, 0:96]
        nrm = small[:, 96:160]
        nsq = small[:, 160:224]
        rn = small[:, 224:288]
        lg = small[:, 288:336]
        mx = small[:, 336:337]
        nmx = small[:, 337:338]
        ex = small[:, 352:400]
        ssum = small[:, 338:339]
        rsum = small[:, 339:340]
        rq = small[:, 340:341]

        vb = arena[:, 0:16384].rearrange("p (e a w) -> p e a w", e=64, a=2)
        vbf = arena[:, 0:16384].rearrange("p (m w) -> p w m", w=128)
        ob = arena[:, 16384:16384 + 12288].rearrange("p (c w) -> p c w", w=128)
        obf = arena[:, 16384:16384 + 12288].rearrange("p (q w) -> p q w", w=384)
        xr = [arena[:, 28672 + 1536 * i:28672 + 1536 * (i + 1)].rearrange("p (r f) -> p r f", r=4) for i in range(2)]
        x1t = [arena[:, 31744 + 1536 * i:31744 + 1536 * (i + 1)].rearrange("p (r f) -> p r f", r=4) for i in range(2)]

        FW = C + 4
        fk = [arena[:, 4704 * i:4704 * (i + 1)].rearrange("p (q w) -> p q w", w=FW) for i in range(2)]
        o1 = 9408
        fs = [arena[:, o1 + 4608 * i:o1 + 4608 * (i + 1)].rearrange("p (w q) -> p w q", q=24) for i in range(2)]
        o1 += 9216
        rs = [arena[:, o1 + 216 * i:o1 + 216 * (i + 1)].rearrange("p (q v) -> p q v", v=9) for i in range(2)]
        o1 += 432
        res = [arena[:, o1 + 288 * i:o1 + 288 * (i + 1)].rearrange("p (s q v) -> p s q v", s=2, v=6) for i in range(2)]
        o1 += 576
        GN = MG * NW
        gs = arena[0:NW, o1:o1 + GN].rearrange("p (g m) -> p g m", g=MG)
        gi = arena[0:NW, o1 + GN:o1 + 2 * GN].rearrange("p (g m) -> p g m", g=MG)
        gt = arena[0:NW, o1 + 2 * GN:o1 + 3 * GN].rearrange("p (g m) -> p g m", g=MG)
        gif = arena[0:NW, o1 + GN:o1 + 2 * GN]
        sqm = small[0:NW, 0:16]
        d8 = small[0:NW, 128:256].rearrange("p (g c) -> p g c", g=MG)
        e8 = small[0:NW, 256:384].rearrange("p (g c) -> p g c", g=MG)
        dmin = small[0:NW, 16:32]
        best = small[0:NW, 32:48]
        bt = small[0:MG, 384:456].rearrange("p (j c) -> p j c", j=9)
        beq = small[0:MG, 456:528].rearrange("p (j c) -> p j c", j=9)
        tb = [small[0:MG, 528 + 9 * i:537 + 9 * i] for i in range(8)]
        offc = small[0:MG, 608:626]
        ib = small[0:MG, 640:640 + 9 * NF].rearrange("p (j n) -> p j n", j=9)
        rep = small[:, 800:818]
        ta = small[:, 818:827]
        ca = small[:, 827:828]
        ck = small[:, 828:837]
        tk = small[:, 840:921].rearrange("p (k j) -> p k j", k=9)
        ia = small[:, 924:924 + NF]

        CF = FR * C
        HF = HALO * C
        o2 = 0

        def ring(n, size):
            nonlocal o2
            got = [arena[:, o2 + size * i:o2 + size * (i + 1)] for i in range(n)]
            o2 += n * size
            return got

        ff = ring(4, CF)
        fx = ring(4, CF)
        hh = ring(4, HF)
        yy = ring(2, CF)
        zz = ring(2, CF)
        gg = [a.bitcast(BF16) for a in ring(2, CF // 2)]
        fm = ring(2, CF)
        assert o2 <= 37900, o2

        def rows(a):
            return a.rearrange("p (r w) -> p r w", w=C)

        names = ("setup_chain setup_dma setup_done phase_done turn_in turn_on turn_in2 turn_on2 "
                 "xs0 xs1 xs2 xs3 stored mv_ready mean_ready dev_ready var_ready veps_ready std_ready wide_ready col_ready gn_ready "
                 "xa_loaded transposed xt_ready qkv_done pre_ready halo_done conv_done squared v_stored "
                 "gram_done norm_done nrm_ready root_ready lg_ready exp_ready ablk_ready at_done "
                 "v_loaded v_copied xr_loaded0 xr_loaded1 mixed mix_out projected x1_ready x1_stored0 x1_stored1 "
                 "fk_loaded0 fk_loaded1 fk_padded fs_ready r_done r_out g_done g_out gi_ready sq_done best_ready bt_done idx_ready offc_ready rep_done "
                 "ff_loaded0 ff_loaded1 ff_loaded2 ff_loaded3 hh_loaded0 hh_loaded1 hh_loaded2 hh_loaded3 "
                 "y_ready z_ready g_ready summed base_ready out_ready out_stored0 out_stored1 "
                 "dve_chain pool_chain act_chain halo_chain").split()
        S = {n: sem(n) for n in names}
        keep = {"setup_chain", "setup_dma", "setup_done", "turn_in", "turn_on", "turn_in2", "turn_on2"} | {f"hh_loaded{i}" for i in range(4)}
        cleared = [S[n] for n in names if n not in keep]
        setup_chain = S["setup_chain"]
        setup_dma, setup_done, phase_done = S["setup_dma"], S["setup_done"], S["phase_done"]
        turn_in, turn_on, turn_in2, turn_on2 = S["turn_in"], S["turn_on"], S["turn_in2"], S["turn_on2"]

        def end_phase(eng, ph):
            eng.drain().then_inc(phase_done, 1)
            eng.wait_ge(phase_done, 5 * (ph + 1))

        def end_image(eng):
            eng.drain().then_inc(turn_in, 1)
            eng.wait_ge(turn_on, 1)
            eng.drain().then_inc(turn_in2, 1)
            eng.wait_ge(turn_on2, 1)
            eng.drain()

        def y_at(n, k):
            return 18 * (n // 2) + 2 * k + n % 2 + 1

        def fold_rows(n, ki):
            return max(0, ki - FR * n), min(FR, HM + ki - FR * n)

        SD = 16 * 15
        block = ctx.enter_context(nc.Block())

        @block.sync
        def _(sp):
            sp.dma_start(cst[:, :], cst_d).then_inc(setup_dma, 16)
            sp.dma_start(w_lo[:, :], qkv_w[0:128, :]).then_inc(setup_dma, 16)
            sp.dma_start(w_hi[0:64, 0, :], qkv_w[128:192, :]).then_inc(setup_dma, 16)
            sp.dma_start(w_hi[64:128, 1, :], qkv_w[128:192, :]).then_inc(setup_dma, 16)
            sp.dma_start(dwt[0:64, :, :], dw_w).then_inc(setup_dma, 16)
            sp.dma_start(dwt[64:128, :, :], dw_w).then_inc(setup_dma, 16)
            sp.dma_start(tcol[:, :], temp).then_inc(setup_dma, 16)
            sp.wait_ge(setup_done, 2)
            for n, a, z in ((0, 0, 0), (0, 1, 1), (1, 0, 1), (1, 1, 2), (2, 0, 2), (3, 1, 0)):
                sp.dma_start(pw[a:128:2, n, :], proj_w[64 * z:64 * z + 64, :]).then_inc(setup_dma, 16)
            sp.dma_start(xnd[0:PAD].rearrange("(a n) -> a n", a=1), zrow[:, :]).then_inc(setup_dma, 16)
            sp.dma_start(xnd[PAD + IMG:].rearrange("(a n) -> a n", a=1), zrow[:, :]).then_inc(setup_dma, 16)
            sp.wait_ge(setup_dma, SD)

            with sp.Fori(0, B) as b:
                def pairs(flat, first, n):
                    a = flat[first * 2 * PLANE:(first + n) * 2 * PLANE]
                    return a.rearrange("(r p f) -> p r f", p=128, f=2 * C)

                xb = xf[b, :]
                ob_ = outf[b, :]
                for i in range(4):
                    sp.dma_start(xs3[:, i, :].rearrange("p (r f) -> p r f", r=16),
                                 pairs(xb, 16 * i, 16)).then_inc(S[f"xs{i}"], 16)
                end_phase(sp, STATS)

                for hp in range(2):
                    for n in range(STEPS + 2):
                        if n < STEPS:
                            g = STEPS * hp + n
                            if g:
                                sp.wait_ge(S["transposed"], 3 * g)
                            for s in range(2):
                                row = 64 * hp + 32 * s + (4 * n - 3 if n else -1)
                                k = 4 if n else 2
                                lo, hi = 0, 128
                                per = k * C
                                if row < 0:
                                    sp.dma_start(xa[0][0:64, s, 0:per], xb[0:PLANE].rearrange("(p f) -> p f", p=64)).then_inc(S["xa_loaded"], 16)
                                    sp.dma_start(xa[0][64:128, s, 0:per], xb[0:PLANE].rearrange("(p f) -> p f", p=64)).then_inc(S["xa_loaded"], 16)
                                elif row + k > H:
                                    sp.dma_start(xa[0][0:96, s, 0:per], xb[row * PLANE:H * PLANE].rearrange("(p f) -> p f", p=96)).then_inc(S["xa_loaded"], 16)
                                    sp.dma_start(xa[0][96:128, s, 0:per], xb[(H - 1) * PLANE:H * PLANE].rearrange("(p f) -> p f", p=32)).then_inc(S["xa_loaded"], 16)
                                else:
                                    sp.dma_start(xa[0][:, s, 0:per], xb[row * PLANE:(row + k) * PLANE].rearrange("(p f) -> p f", p=128)).then_inc(S["xa_loaded"], 16)
                        if n >= 3:
                            m = n - 2
                            sp.wait_ge(S["v_copied"], 3 * (8 * hp + m))
                            sp.dma_start(vd[:, 1536 * (m - 1):1536 * m], vst[0]).then_inc(S["v_stored"], 16)
                    sp.wait_ge(S["v_stored"], 128 * (hp + 1))
                    end_phase(sp, QKV0 + 2 * hp)

                    for s in range(2):
                        for j in range(3):
                            for a in range(2):
                                src = vd[64 * s:64 * s + 64, :].rearrange("e (r a j w) -> j a r e w", a=2, j=3, w=128)
                                sp.dma_start(vb[64 * s + j:64 * s + CH:3, :, a, :], src[j, a]).then_inc(S["v_loaded"], 16)
                    for j in range(9):
                        if j < 8:
                            if j >= 2:
                                sp.wait_ge(S["x1_ready"], 32 * hp + 4 * (j - 1))
                            sp.dma_start(xr[j % 2], pairs(xb, 32 * hp + 4 * j, 4)).then_inc(S[f"xr_loaded{j % 2}"], 16)
                        if j:
                            m = j - 1
                            sp.wait_ge(S["x1_ready"], 32 * hp + 4 * (m + 1))
                            sp.dma_start(pairs(x1d, 32 * hp + 4 * m, 4), x1t[m % 2]).then_inc(S[f"x1_stored{m % 2}"], 16)
                    for i in range(2):
                        sp.wait_ge(S[f"x1_stored{i}"], 64 * (hp + 1))
                    end_phase(sp, MIX0 + 2 * hp)

                for i in range(4):
                    sp.dma_start(xs3[:, i, :].rearrange("p (r f) -> p r f", r=16),
                                 pairs(x1d, 16 * i, 16)).then_inc(S[f"xs{i}"], 16)
                for i in range(4):
                    sp.wait_ge(S["gn_ready"], 2 + i)
                    sp.dma_start(pairs(xnd[PAD:PAD + IMG], 16 * i, 16),
                                 xs3[:, i, :].rearrange("p (r f) -> p r f", r=16)).then_inc(S["stored"], 16)
                sp.wait_ge(S["stored"], 64)
                end_phase(sp, NORM)

                planes = xnd[PAD:PAD + IMG].rearrange("(y h w) -> h y w", y=H, w=C)
                sp.wait_ge(S["fk_padded"], 2)
                for g in range(MG):
                    if g >= 2:
                        sp.wait_ge(S["r_done"], g - 1)
                    for ki in range(3):
                        sp.dma_start(fk[g % 2][0:HM, 8 * ki:8 * ki + 8, 2:2 + C],
                                     planes[ki:ki + HM, 8 * g:8 * g + 8, :]).then_inc(S[f"fk_loaded{g % 2}"], 16)
                end_phase(sp, GRAM)

                fin = xnd[PAD:PAD + IMG].rearrange("(g i n f) -> n i g f", g=MG, i=MC, n=NF)
                x1in = x1d.rearrange("(g i n f) -> n i g f", g=MG, i=MC, n=NF)
                oo = ob_.rearrange("(g i n f) -> n i g f", g=MG, i=MC, n=NF)

                def store(n):
                    sp.wait_ge(S["out_ready"], n + 1)
                    sp.dma_start(oo[n], fm[n % 2]).then_inc(S[f"out_stored{n % 2}"], 16)

                for n in range(NF):
                    if n >= 4:
                        sp.wait_ge(S["out_ready"], n - 3)
                    sp.dma_start(ff[n % 4], fin[n]).then_inc(S[f"ff_loaded{n % 4}"], 16)
                    sp.dma_start(fx[n % 4], x1in[n]).then_inc(S[f"ff_loaded{n % 4}"], 16)
                    if n >= 3:
                        store(n - 3)
                for n in range(NF - 3, NF):
                    store(n)
                for i in range(2):
                    sp.wait_ge(S[f"out_stored{i}"], 16 * NF // 2)
                end_phase(sp, FOLD)

                sp.wait_ge(turn_in, 4)
                sp.sem_clear(turn_in)
                sp.sem_clear(turn_on2)
                for s_ in cleared:
                    sp.sem_clear(s_)
                sp.sem_inc(turn_on, 1)
                sp.wait_ge(turn_in2, 4)
                sp.sem_clear(turn_in2)
                sp.sem_clear(turn_on)
                sp.sem_inc(turn_on2, 1)

        @block.gpsimd
        def _(pool):
            pool.memset(zrow[:, :], 0.0).then_inc(setup_done, 1)
            pool.memset(w_hi[64:128, 0, :], 0.0).then_inc(setup_chain, 1)
            pool.wait_ge(setup_chain, 1)
            pool.memset(w_hi[0:64, 1, :], 0.0).then_inc(setup_chain, 1)
            pool.wait_ge(setup_chain, 2)
            pool.memset(pw[:, :, :], 0.0)
            pool.memset(ablk[:, :], 0.0)
            pool.memset(small[:, :], 0.0)
            pool.memset(arena[:, 0:16384], 0.0)
            pool.memset(cnt[:, :, :], 0.0).then_inc(setup_done, 1)
            pool.wait_ge(setup_dma, SD)
            pool.tensor_scalar(ident_b[:, :], c_("ident"), -1.0, None, ALU.mult)
            pool.tensor_copy(left_b[:, :, :].rearrange("p a c -> p (a c)"), c_("left")).then_inc(setup_done, 1)
            pool.wait_ge(setup_done, 3)
            with pool.Fori(0, B):
                end_phase(pool, STATS)
                for hp in range(2):
                    pool.memset(pre[:, :, :, 0:130:129], 0.0)
                    if hp == 0:
                        pool.drain()
                        pool.memset(pre[0:64, :, 4, 1:129], 0.0)
                    pool.drain().then_inc(S["halo_chain"], 1)
                    pool.wait_ge(S["halo_chain"], 1 + hp * 10)
                    for n in range(1, STEPS):
                        for t in range(9):
                            if n == 1:
                                pool.wait_ge(S["pre_ready"], 81 * hp + t + 1)
                            else:
                                pool.wait_ge(S["conv_done"], 72 * hp + 9 * (n - 2) + t + 1)
                            if hp == 1 and n == STEPS - 1:
                                pool.tensor_copy(pre[:, t, 0:2, 1:129], pre[:, t, 4:6, 1:129]).then_inc(S["halo_chain"], 1)
                                pool.wait_ge(S["halo_chain"], 12 + t)
                                pool.memset(pre[64:128, t, 5, 1:129], 0.0).then_inc(S["halo_done"], 1)
                                pool.wait_ge(S["halo_done"], 72 * hp + 9 * (n - 1) + t + 1)
                            else:
                                pool.tensor_copy(pre[:, t, 0:2, 1:129], pre[:, t, 4:6, 1:129]).then_inc(S["halo_done"], 1)
                    end_phase(pool, QKV0 + 2 * hp)
                    if hp == 0:
                        pool.sem_inc(S["halo_chain"], 9)
                    end_phase(pool, MIX0 + 2 * hp)
                end_phase(pool, NORM)
                for i in range(2):
                    pool.memset(fk[i][:, :, 0:2], 0.0)
                    pool.memset(fk[i][:, :, C + 2:C + 4], 0.0).then_inc(S["fk_padded"], 1)
                end_phase(pool, GRAM)

                def load_neighbours(n, k):
                    src = xnd.rearrange("(n a) -> n a", a=1)
                    if k == 0:
                        if n >= 4:
                            pool.wait_ge(S["y_ready"], y_at(n - 4, 8))
                        pool.indirect_dma_start(hh[n % 4], None, src,
                                                bass.IndirectOffsetOnAxis(ap=idxa[:, n:n + 1], axis=0)).then_inc(S[f"hh_loaded{n % 4}"], 16)
                    else:
                        pool.wait_ge(S["y_ready"], y_at(n, k - 1))
                        i = 8 - k
                        pool.indirect_dma_start(hh[n % 4][16 * i:16 * i + 16, :], None, src,
                                                bass.IndirectOffsetOnAxis(ap=idxb[:, i + 1, n:n + 1], axis=0)).then_inc(S[f"hh_loaded{n % 4}"], 16)

                def base(n):
                    pool.wait_ge(S[f"ff_loaded{n % 4}"], 32 * (n // 4 + 1))
                    if n >= 2:
                        pool.wait_ge(S[f"out_stored{n % 2}"], 16 * (n // 2))
                    f, m = rows(ff[n % 4]), rows(fm[n % 2])
                    parts = [(0, 1, 0), (1, 2, 1), (2, FR, 2)] if n == 0 else \
                        [(0, FR - 2, 2), (FR - 2, FR - 1, 1), (FR - 1, FR, 0)] if n == NF - 1 else [(0, FR, 2)]
                    for a, z, kind in parts:
                        last = pool.tensor_tensor(m[:, a:z, :], f[:, a:z, :],
                                                  cnt[:, kind:kind + 1, :].to_broadcast([128, z - a, C]), ALU.mult)
                    last.then_inc(S["pool_chain"], 1)
                    pool.wait_ge(S["pool_chain"], n + 1)
                    pool.tensor_tensor(fm[n % 2], fm[n % 2], fx[n % 4], ALU.add).then_inc(S["base_ready"], 1)

                load_neighbours(0, 0)
                load_neighbours(1, 0)
                for n in range(0, NF, 2):
                    if n + 2 < NF:
                        load_neighbours(n + 2, 0)
                        load_neighbours(n + 3, 0)
                    for k in range(1, 9):
                        load_neighbours(n, k)
                        load_neighbours(n + 1, k)
                        if k == 3:
                            base(n)
                        if k == 6:
                            base(n + 1)
                end_phase(pool, FOLD)
                pool.tensor_copy(cnt[:, :, :].rearrange("p a c -> p (a c)"), c_("cnt"))
                end_image(pool)

        @block.scalar
        def _(act):
            act.wait_ge(setup_done, 3)
            with act.Fori(0, B):
                def root(k):
                    act.wait_ge(S["veps_ready"], k + 1)
                    nc.scalar.activation(dev, var, ACT.Sqrt).then_inc(S["std_ready"], 1)

                root(0)
                end_phase(act, STATS)
                for hp in range(2):
                    def take_transposed(n):
                        g = STEPS * hp + n
                        k = 4 if n else 2
                        if g:
                            act.wait_ge(S["qkv_done"], 9 * g)
                        for j in range(3):
                            act.wait_ge(S["transposed"], 3 * g + j + 1)
                            dst = xlo[0][:, j, 0:k * 128] if j < 2 else xhi[0][:, 0:k * 128]
                            c = 1 if j == 2 else 0
                            nc.scalar.activation(dst.rearrange("p (q v) -> p q v", v=k),
                                                 bank[j][:, 0:k * 128].rearrange("p (v q) -> p q v", v=k),
                                                 ACT.Identity, scale=gnp[:, c:c + 1],
                                                 bias=gnp[:, 2 + c:3 + c]).then_inc(S["xt_ready"], 1)

                    def squares(n):
                        act.wait_ge(S["conv_done"], 72 * hp + 9 * (n - 1) + 6)
                        for c in range(6 * (n - 1), 6 * n):
                            for z, buf in enumerate((qb, kb)):
                                a_n[0] += 1
                                if a_n[0] > 1:
                                    act.wait_ge(S["act_chain"], a_n[0] - 1)
                                nc.scalar.activation(junk, buf[:, c * SEG:(c + 1) * SEG], ACT.Square,
                                                     accum_out=sq[:, CH * z + c:CH * z + c + 1]).then_inc(S["act_chain"], 1)

                    def sort_v(n):
                        if n > 1 or hp:
                            act.wait_ge(S["v_stored"], 16 * (8 * hp + n - 1))
                        for t in range(3):
                            act.wait_ge(S["conv_done"], 72 * hp + 9 * (n - 1) + 7 + t)
                            for z in range(2):
                                w0 = (3 * z + t) // 2
                                dst = vst[0].rearrange("p (r a q w) -> p r a q w", a=2, q=128, w=3)[:, :, (z + t) % 2, :, w0]
                                src = acc[t].rearrange("p (r q z) -> p r q z", z=2, q=128)[:, :, :, z]
                                last = nc.scalar.activation(dst, src, ACT.Copy)
                            last.then_inc(S["v_copied"], 1)

                    if hp == 0:
                        a_n = [0]
                    for n in range(STEPS):
                        take_transposed(n)
                        for t in range(9):
                            i = 81 * hp + 9 * n + t
                            act.wait_ge(S["qkv_done"], i + 1)
                            if n:
                                act.wait_ge(S["halo_done"], 72 * hp + 9 * (n - 1) + t + 1)
                            src = bank[3 + i % 4]
                            if n == 0:
                                parts = [(0, 64, 1, 2), (64, 128, 0, 2)] if hp == 0 else [(0, 128, 0, 2)]
                                first = 4
                            else:
                                parts = [(0, 64, 0, 4), (64, 128, 0, 3)] if hp and n == STEPS - 1 else [(0, 128, 0, 4)]
                                first = 2
                            for a, z, r0, r1 in parts:
                                last = nc.scalar.activation(
                                    pre[a:z, t, first + r0:first + r1, 1:129],
                                    src[a:z, 128 * r0:128 * r1].rearrange("p (r w) -> p r w", w=128), ACT.Copy)
                            last.then_inc(S["pre_ready"], 1)
                        if n >= 2:
                            sort_v(n - 1)
                            squares(n - 1)
                    sort_v(STEPS - 1)
                    squares(STEPS - 1)
                    act.wait_ge(S["act_chain"], 96 * (hp + 1))
                    act.drain().then_inc(S["squared"], 1)
                    for s in range(2):
                        r = slice(64 * s, 64 * s + CH)
                        act.wait_ge(S["nrm_ready"], 2 * hp + s + 1)
                        nc.scalar.activation(nsq[r, 0:49], nrm[r, 0:49], ACT.Sqrt).then_inc(S["root_ready"], 1)
                    for s in range(2):
                        r = slice(64 * s, 64 * s + CH)
                        act.wait_ge(S["lg_ready"], 2 * hp + s + 1)
                        nc.scalar.activation(ex[r, :], lg[r, :], ACT.Exp, bias=nmx[r, :],
                                             accum_out=ssum[r, :]).then_inc(S["exp_ready"], 1)
                    end_phase(act, QKV0 + 2 * hp)
                    for g in range(32):
                        act.wait_ge(S["mixed"], 32 * hp + g + 1)
                        nc.scalar.activation(ob[:, :, 4 * g:4 * g + 4],
                                             bank[g % 2][:, 0:384].rearrange("p (u c) -> p c u", u=4),
                                             ACT.Copy).then_inc(S["mix_out"], 1)
                    end_phase(act, MIX0 + 2 * hp)
                root(1)
                end_phase(act, NORM)

                def columns_first(g):
                    act.wait_ge(S[f"fk_loaded{g % 2}"], 48 * (g // 2 + 1))
                    if g >= 2:
                        act.wait_ge(S["r_done"], g - 1)
                    nc.scalar.activation(fs[g % 2][0:HM, :, :], fk[g % 2][0:HM, :, 2:2 + C].rearrange("p q w -> p w q"),
                                         ACT.Copy).then_inc(S["fs_ready"], 1)

                columns_first(0)
                for g in range(MG):
                    if g + 1 < MG:
                        columns_first(g + 1)
                    act.wait_ge(S["r_done"], g + 1)
                    if g >= 2:
                        act.wait_ge(S["g_done"], g - 1)
                    nc.scalar.activation(rs[g % 2][0:120, :, :], bank[g % 2][0:120, 0:216].rearrange("p (q v) -> p q v", v=9), ACT.Copy)
                    nc.scalar.activation(res[g % 2][0:48, :, :, :].rearrange("p s q v -> p (s q v)"),
                                         bank[2 + g % 2][0:48, 0:288], ACT.Copy).then_inc(S["r_out"], 1)
                end_phase(act, GRAM)

                for n in range(0, NF, 2):
                    for k in range(9):
                        for c in (n, n + 1):
                            r0, r1 = fold_rows(c, k // 3)
                            kj = k % 3
                            at_ = y_at(c, k)
                            act.wait_ge(S["y_ready"], at_)
                            if at_ > 2:
                                act.wait_ge(S["summed"], at_ - 2)
                            nc.scalar.activation(rows(zz[c % 2])[:, r0:r1, kj:kj + WM],
                                                 rows(yy[c % 2])[:, r0:r1, kj:kj + WM], ACT.Copy,
                                                 bias=MAGIC if k % 2 == 0 else -MAGIC).then_inc(S["z_ready"], 1)
                end_phase(act, FOLD)
                end_image(act)

        @block.vector
        def _(dve):
            dve.wait_ge(setup_done, 3)
            dve.wait_ge(setup_dma, SD)
            with dve.Fori(0, B) as b:
                chain = [0]

                def link(ins):
                    chain[0] += 1
                    ins.then_inc(S["dve_chain"], 1)
                    dve.wait_ge(S["dve_chain"], chain[0])

                def group_stats(k):
                    for i in range(4):
                        dve.wait_ge(S[f"xs{i}"], 16 * (k + 1))
                        for g in range(GROUPS):
                            last = nc.vector.bn_stats(bst[:, g, 6 * i:6 * i + 6], xs[:, i, :, GC * g:GC * g + GC])
                    link(last)
                    for g in range(GROUPS):
                        last = nc.vector.bn_aggr(mv[:, g, :], bst[:, g, :])
                    last.then_inc(S["mv_ready"], 1)
                    dve.wait_ge(S["mean_ready"], k + 1)
                    link(nc.vector.tensor_copy(mean, bank[0][:, 0:GROUPS]))
                    link(nc.vector.tensor_tensor(dev, mv[:, :, 0], mean, ALU.subtract))
                    link(nc.vector.tensor_tensor(dev, dev, dev, ALU.mult))
                    nc.vector.tensor_tensor(var, dev, mv[:, :, 1], ALU.add).then_inc(S["dev_ready"], 1)
                    dve.wait_ge(S["var_ready"], k + 1)
                    nc.vector.tensor_scalar(var, bank[1][:, 0:GROUPS], 1e-5, None, ALU.add).then_inc(S["veps_ready"], 1)
                    dve.wait_ge(S["std_ready"], k + 1)
                    link(nc.vector.reciprocal(rstd, dev))

                group_stats(0)
                link(nc.vector.scalar_tensor_tensor(nbias, mean, -1.0, rstd, ALU.mult, ALU.mult))
                for z, a in enumerate((rstd, nbias)):
                    w_ = wide[:, z, 0:C].rearrange("p (g c) -> p g c", c=GC)
                    link(nc.vector.tensor_copy(w_, a.rearrange("p (g a) -> p g a", a=1).to_broadcast([128, GROUPS, GC])))
                    last = nc.vector.tensor_copy(wide[:, z, C:256], wide[:, z, 128:192])
                    last.then_inc(S["wide_ready"], 1)
                dve.wait_ge(S["col_ready"], 1)
                nc.vector.tensor_copy(gnp, bank[2][:, 0:4]).then_inc(S["gn_ready"], 1)
                end_phase(dve, STATS)

                for hp in range(2):
                    for n in range(1, STEPS):
                        for t in range(9):
                            dve.wait_ge(S["pre_ready"], 81 * hp + 9 * n + t + 1)
                            a = acc[t % 3].rearrange("p (r w) -> p r w", w=128)
                            if t < 3 and (hp or n > 1):
                                dve.wait_ge(S["v_copied"], 3 * (8 * hp + n - 2) + t + 1)

                            def tap(j):
                                return pre[:, t, j // 3:j // 3 + 4, j % 3:j % 3 + 128]

                            link(nc.vector.tensor_scalar(a, tap(0), dwt[:, t, 0:1], None, ALU.mult))
                            for j in range(1, 8):
                                link(nc.vector.scalar_tensor_tensor(a, tap(j), dwt[:, t, j:j + 1], a, ALU.mult, ALU.add))
                            if t < 6:
                                dst = (qb, kb)[t // 3][:, 1536 * (n - 1):1536 * n]
                                dst = dst.rearrange("p (r w c) -> p r w c", w=128, c=3)[:, :, :, t % 3]
                            else:
                                dst = a
                            nc.vector.scalar_tensor_tensor(dst, tap(8), dwt[:, t, 8:9], a, ALU.mult, ALU.add).then_inc(S["conv_done"], 1)
                    for s in range(2):
                        r = slice(64 * s, 64 * s + CH)
                        dve.wait_ge(S["norm_done"], hp + 1)
                        nc.vector.tensor_scalar(nrm[r, 0:49], bank[3 + s][r, 0:49], 1e-12, None, ALU.max).then_inc(S["nrm_ready"], 1)
                    for s in range(2):
                        r = slice(64 * s, 64 * s + CH)
                        dve.wait_ge(S["root_ready"], 2 * hp + s + 1)
                        link(nc.vector.reciprocal(rn[r, 0:49], nsq[r, 0:49]))
                        link(nc.vector.tensor_tensor(rq[r, :], rn[r, 0:1], tcol[r, hp:hp + 1], ALU.mult))
                        link(nc.vector.scalar_tensor_tensor(lg[r, :], bank[s][r, 0:CH], rq[r, :], rn[r, 1:49], ALU.mult, ALU.mult))
                        link(nc.vector.tensor_reduce(mx[r, :], lg[r, :], AX, ALU.max))
                        nc.vector.tensor_scalar(nmx[r, :], mx[r, :], -1.0, None, ALU.mult).then_inc(S["lg_ready"], 1)
                    for s in range(2):
                        r = slice(64 * s, 64 * s + CH)
                        dve.wait_ge(S["exp_ready"], 2 * hp + s + 1)
                        link(nc.vector.reciprocal(rsum[r, :], ssum[r, :]))
                        nc.vector.tensor_scalar(ablk[r, 64 * s:64 * s + CH], ex[r, :], rsum[r, :], None, ALU.mult).then_inc(S["ablk_ready"], 1)
                    dve.wait_ge(S["at_done"], hp + 1)
                    nc.vector.tensor_copy(at[:, :], bank[5][:, 0:96])
                    end_phase(dve, QKV0 + 2 * hp)

                    for j in range(8):
                        dve.wait_ge(S[f"xr_loaded{j % 2}"], 64 * hp + 16 * (j // 2 + 1))
                        if j >= 2 or hp:
                            dve.wait_ge(S[f"x1_stored{j % 2}"], 64 * hp + 16 * (j // 2))
                        for r in range(4):
                            i = 4 * j + r
                            dve.wait_ge(S["projected"], 32 * hp + i + 1)
                            nc.vector.tensor_tensor(x1t[j % 2][:, r, :], xr[j % 2][:, r, :], bank[4 + i % 3][:, 0:384], ALU.add).then_inc(S["x1_ready"], 1)
                    end_phase(dve, MIX0 + 2 * hp)

                group_stats(1)
                for a, row in ((mean, mrow), (rstd, rrow)):
                    for z in range(2):
                        link(nc.vector.tensor_copy(row[:, z, :].rearrange("p (g c) -> p g c", c=GC),
                                                   a.rearrange("p (g a) -> p g a", a=1).to_broadcast([128, GROUPS, GC])))
                mr, rr = mrow[:, 0:1, :].to_broadcast([128, 32, C]), rrow[:, 0:1, :].to_broadcast([128, 32, C])
                for i in range(4):
                    link(nc.vector.tensor_tensor(xs[:, i, :, :], xs[:, i, :, :], mr, ALU.subtract))
                    nc.vector.tensor_tensor(xs[:, i, :, :], xs[:, i, :, :], rr, ALU.mult).then_inc(S["gn_ready"], 1)
                end_phase(dve, NORM)

                for g in range(MG):
                    dve.wait_ge(S["g_done"], g + 1)
                    for ki in range(3):
                        dst = gs[:, g, :].rearrange("p (y k) -> p y k", k=9)[:, :, 3 * ki:3 * ki + 3]
                        last = nc.vector.tensor_copy(dst, bank[4 + g % 2][0:NW, 24 * ki:24 * ki + 24].rearrange("p (y k) -> p y k", k=3))
                    last.then_inc(S["g_out"], 1)
                dve.wait_ge(S["g_out"], MG)
                i72 = c_("i72", NW).rearrange("p (a m) -> p a m", a=1).to_broadcast([NW, MG, NW])
                nc.vector.tensor_tensor(gi, gs, i72, ALU.mult).then_inc(S["gi_ready"], 1)
                dve.wait_ge(S["gi_ready"], 1)
                link(nc.vector.tensor_reduce(sqm, gi, AX, ALU.add))
                dve.wait_ge(S["sq_done"], 1)
                for q in range(3):
                    g0, g1 = (0, 6, 12)[q], (6, 12, 16)[q]
                    last = nc.vector.tensor_tensor(gt[:, g0:g1, :], bank[5 + q][0:NW, 0:(g1 - g0) * NW].rearrange("p (g m) -> p g m", m=NW),
                                                   sqm[:, g0:g1].rearrange("p (g a) -> p g a", a=1).to_broadcast([NW, g1 - g0, NW]), ALU.add)
                link(last)
                link(nc.vector.scalar_tensor_tensor(gt.rearrange("p g m -> p (g m)"), gs.rearrange("p g m -> p (g m)"), -2.0,
                                                    gt.rearrange("p g m -> p (g m)"), ALU.mult, ALU.add))
                bmask = c_("bmask", NW).rearrange("p (a m) -> p a m", a=1).to_broadcast([NW, MG, NW])
                link(nc.vector.tensor_tensor(gt, gt, bmask, ALU.mult))
                for g in range(MG):
                    last = nc.vector.tensor_reduce(d8[:, g, :], gt[:, g, :].rearrange("p (j c) -> p c j", j=9), AX, ALU.add)
                link(last)
                self8 = c_("self8", NW).rearrange("p (a m) -> p a m", a=1).to_broadcast([NW, MG, 8])
                link(nc.vector.tensor_tensor(d8, d8, self8, ALU.add))
                link(nc.vector.tensor_reduce(dmin, d8, AX, ALU.min))
                link(nc.vector.tensor_tensor(e8, d8, dmin.rearrange("p (g a) -> p g a", a=1).to_broadcast([NW, MG, 8]), ALU.is_le))
                w8 = c_("w8", NW).rearrange("p (a m) -> p a m", a=1).to_broadcast([NW, MG, 8])
                link(nc.vector.tensor_tensor(e8, e8, w8, ALU.mult))
                nc.vector.tensor_reduce(best, e8, AX, ALU.max).then_inc(S["best_ready"], 1)
                dve.wait_ge(S["bt_done"], 1)
                link(nc.vector.tensor_copy(bt.rearrange("p j c -> p (j c)"), bank[0][0:MG, 0:NW]))
                u, e, off = tb[0], tb[1], tb[2]
                link(nc.vector.tensor_reduce(u, bt, AX, ALU.min))
                link(nc.vector.tensor_tensor(beq, bt, u.rearrange("p (g a) -> p g a", a=1).to_broadcast([MG, 9, 8]), ALU.is_equal))
                link(nc.vector.tensor_reduce(offc[:, 9:18], beq, AX, ALU.add))
                link(nc.vector.tensor_scalar(u, u, -1.0, 8.0, ALU.mult, ALU.add))
                jr = c_("jrow", MG)
                link(nc.vector.tensor_tensor(e, u, jr, ALU.is_ge))
                link(nc.vector.tensor_tensor(e, e, jr, ALU.add))
                link(nc.vector.tensor_scalar(e, e, 1.0, None, ALU.subtract))
                link(nc.vector.tensor_tensor(u, u, c_("ktab", MG), ALU.add))
                link(nc.vector.scalar_tensor_tensor(u, e, -9.0, u, ALU.mult, ALU.add))
                link(nc.vector.tensor_scalar(tb[3], u, 3.0, None, ALU.is_ge))
                link(nc.vector.tensor_scalar(tb[4], u, 6.0, None, ALU.is_ge))
                link(nc.vector.tensor_tensor(tb[3], tb[3], tb[4], ALU.add))
                link(nc.vector.scalar_tensor_tensor(off, e, float(PLANE), u, ALU.mult, ALU.add))
                link(nc.vector.scalar_tensor_tensor(offc[:, 0:9], tb[3], float(C - 3), off, ALU.mult, ALU.add))
                nc.vector.tensor_copy(tb[5], offc[:, 0:9]).then_inc(S["offc_ready"], 1)
                dve.wait_ge(S["offc_ready"], 1)
                link(nc.vector.tensor_tensor(ib, tb[5].rearrange("p (j a) -> p j a", a=1).to_broadcast([MG, 9, NF]),
                                             c_("ctab", MG).rearrange("p (a n) -> p a n", a=1).to_broadcast([MG, 9, NF]), ALU.add))
                link(nc.vector.tensor_copy(idxb[:, :, :], ib))
                dve.wait_ge(S["rep_done"], 1)
                link(nc.vector.tensor_copy(rep, bank[1][:, 0:18]))
                link(nc.vector.tensor_tensor(ta, rep[:, 0:9], c_("sela"), ALU.mult))
                link(nc.vector.tensor_reduce(ca, ta, AX, ALU.add))
                link(nc.vector.tensor_scalar(ia, c_("base"), ca, None, ALU.add))
                link(nc.vector.tensor_copy(idxa[:, :], ia))
                link(nc.vector.tensor_tensor(tk, c_("selk").rearrange("p (k j) -> p k j", k=9),
                                             rep[:, 9:18].rearrange("p (a j) -> p a j", a=1).to_broadcast([128, 9, 9]), ALU.mult))
                link(nc.vector.tensor_reduce(ck, tk, AX, ALU.add))
                end_phase(dve, GRAM)

                def product(n, k):
                    at_ = y_at(n, k)
                    r0, r1 = fold_rows(n, k // 3)
                    ki, kj = k // 3, k % 3
                    if k == 0:
                        dve.wait_ge(S[f"ff_loaded{n % 4}"], 32 * (n // 4 + 1))
                    dve.wait_ge(S[f"hh_loaded{n % 4}"], b * (144 * NF // 4) + 144 * (n // 4) + 16 * (k + 1))
                    a = rows(ff[n % 4])[:, r0:r1, kj:kj + WM]
                    z = rows(hh[n % 4])[:, 2 - ki + r0:2 - ki + r1, 0:WM]
                    nc.vector.scalar_tensor_tensor(rows(yy[n % 2])[:, r0:r1, kj:kj + WM], a, ck[:, k:k + 1], z,
                                                   ALU.mult, ALU.mult).then_inc(S["y_ready"], 1)

                def above(n, k):
                    at_ = y_at(n, k)
                    r0, r1 = fold_rows(n, k // 3)
                    kj = k % 3
                    dve.wait_ge(S["z_ready"], at_)
                    if at_ > 2:
                        dve.wait_ge(S["summed"], at_ - 2)
                    nc.vector.scalar_tensor_tensor(rows(gg[n % 2])[:, r0:r1, kj:kj + WM],
                                                   rows(zz[n % 2])[:, r0:r1, kj:kj + WM],
                                                   -MAGIC if k % 2 == 0 else MAGIC,
                                                   rows(yy[n % 2])[:, r0:r1, kj:kj + WM],
                                                   ALU.add, ALU.is_gt).then_inc(S["g_ready"], 1)

                def finish(n):
                    dve.wait_ge(S["summed"], y_at(n, 8))
                    dve.wait_ge(S["base_ready"], n + 1)
                    b0 = 4 * (n % 2)
                    for q in range(4):
                        last = nc.vector.tensor_tensor(fm[n % 2][:, 384 * q:384 * q + 384], bank[b0 + q][:, 0:384],
                                                       fm[n % 2][:, 384 * q:384 * q + 384], ALU.add)
                    last.then_inc(S["out_ready"], 1)

                for n in range(0, NF, 2):
                    for k in range(9):
                        product(n, k)
                        if k == 0 and n:
                            finish(n - 2)
                        product(n + 1, k)
                        if k == 0 and n:
                            finish(n - 1)
                        above(n, k)
                        above(n + 1, k)
                        dve.wait_ge(S["g_ready"], y_at(n + 1, k))
                finish(NF - 2)
                finish(NF - 1)
                end_phase(dve, FOLD)
                end_image(dve)

        @block.tensor
        def _(pe):
            pe.wait_ge(setup_done, 3)
            pe.wait_ge(setup_dma, SD)
            mm = nc.tensor.matmul
            with pe.Fori(0, B):
                def average(k):
                    pe.wait_ge(S["mv_ready"], k + 1)
                    mm(bank[0][:, 0:GROUPS], c_("avg"), mv[:, :, 0], start=True, stop=True).then_inc(S["mean_ready"], 1)
                    pe.wait_ge(S["dev_ready"], k + 1)
                    mm(bank[1][:, 0:GROUPS], c_("avg"), var, start=True, stop=True).then_inc(S["var_ready"], 1)

                average(0)
                pe.wait_ge(S["wide_ready"], 2)
                one = c_("ones")[0:1, 0:1]
                for z in range(2):
                    for h in range(2):
                        last = mm(bank[2][:, 2 * z + h:2 * z + h + 1], wide[0:1, z, 128 * h:128 * h + 128], one, start=True, stop=True)
                last.then_inc(S["col_ready"], 1)
                end_phase(pe, STATS)

                for hp in range(2):
                    def transposes(n):
                        g = STEPS * hp + n
                        k = 4 if n else 2
                        dmas = 2 * (g + 1) + 1 + (1 if hp and n == STEPS - 1 else 0)
                        pe.wait_ge(S["xa_loaded"], 16 * dmas)
                        if g:
                            pe.wait_ge(S["xt_ready"], 3 * g)
                        xv = xa[0].rearrange("p s (v c) -> p s v c", c=C)
                        for j in range(2):
                            for v in range(k):
                                last = nc.tensor.transpose(bank[j][:, 128 * v:128 * v + 128], xv[:, j, v, 0:128], c_("ident"))
                            last.then_inc(S["transposed"], 1)
                        for v in range(k):
                            for s in range(2):
                                last = mm(bank[2][64 * s:64 * s + 64, 128 * v:128 * v + 128], xv[:, s, v, 128:C], c_("ident"), start=True, stop=True)
                        last.then_inc(S["transposed"], 1)

                    transposes(0)
                    for n in range(STEPS):
                        k = 4 if n else 2
                        g = STEPS * hp + n
                        pe.wait_ge(S["xt_ready"], 3 * (g + 1))
                        if n + 1 < STEPS:
                            transposes(n + 1)
                        for t in range(9):
                            i = 9 * g + t
                            if i >= 4:
                                pe.wait_ge(S["pre_ready"], i - 3)
                            for s in range(2):
                                dst = bank[3 + i % 4][64 * s:64 * s + 64, 0:128 * k]
                                mm(dst, w_lo[:, 64 * t:64 * t + 64], xlo[0][:, s, 0:128 * k], start=True, stop=False)
                                last = mm(dst, w_hi[:, s, 64 * t:64 * t + 64], xhi[0][:, 0:128 * k], start=False, stop=True)
                            last.then_inc(S["qkv_done"], 1)
                    pe.wait_ge(S["conv_done"], 72 * (hp + 1))
                    pe.wait_ge(S["squared"], hp + 1)
                    qv = qb.rearrange("p (c u) -> p u c", u=SEG)
                    kv = kb.rearrange("p (c u) -> p u c", u=SEG)
                    for u in range(SEG):
                        for s in range(2):
                            r = slice(64 * s, 64 * s + 64)
                            last = mm(bank[s][64 * s:64 * s + CH, 0:CH], qv[r, u, :], kv[r, u, :],
                                      start=(u == 0), stop=(u == SEG - 1))
                    for s in range(2):
                        r = slice(64 * s, 64 * s + 64)
                        mm(bank[3 + s][64 * s:64 * s + CH, 0:1], sq[r, 0:CH], c_("ones")[r, 0:1], start=True, stop=True)
                        last = mm(bank[3 + s][64 * s:64 * s + CH, 1:49], c_("ones")[r, 0:CH], sq[r, CH:2 * CH], start=True, stop=True)
                    last.then_inc(S["norm_done"], 1)
                    pe.wait_ge(S["ablk_ready"], 2 * (hp + 1))
                    mm(bank[5][:, 0:96], ablk[:, :], c_("icol"), start=True, stop=True).then_inc(S["at_done"], 1)
                    end_phase(pe, QKV0 + 2 * hp)

                    KR = 64 + CH
                    pe.wait_ge(S["v_loaded"], 192 * (hp + 1))
                    for g in range(32):
                        if g >= 2:
                            pe.wait_ge(S["mix_out"], 32 * hp + g - 1)
                        for i in range(4):
                            last = mm(bank[g % 2][:, 96 * i:96 * i + 96], vbf[0:KR, 4 * g + i, :], at[0:KR, :], start=True, stop=True)
                        last.then_inc(S["mixed"], 1)
                    pe.wait_ge(S["mix_out"], 32 * (hp + 1))
                    for i in range(32):
                        if i >= 3:
                            pe.wait_ge(S["x1_ready"], 32 * hp + i - 2)
                        bk = bank[4 + i % 3]
                        w3 = obf[:, i, :].rearrange("p (q w) -> p w q", w=3)
                        mm(bk[:, 0:C], w3[:, 0, :], pw[:, 0, :], start=True, stop=False)
                        mm(bk[:, 0:C], w3[:, 1, :], pw[:, 2, :], start=False, stop=True)
                        mm(bk[:, C:2 * C], w3[:, 1, :], pw[:, 3, :], start=True, stop=False)
                        mm(bk[:, C:2 * C], w3[:, 2, :], pw[:, 1, :], start=False, stop=True).then_inc(S["projected"], 1)
                    end_phase(pe, MIX0 + 2 * hp)
                average(1)
                end_phase(pe, NORM)

                selv = c_("sel").rearrange("p (k w m) -> p k w m", k=3, w=WB)
                selev = c_("sele").rearrange("p (n m) -> p n m", m=NW)

                def combine(g):
                    pe.wait_ge(S["r_out"], g + 1)
                    if g >= 2:
                        pe.wait_ge(S["g_out"], g - 1)
                    dst = bank[4 + g % 2][0:NW, 0:NW]
                    for kj in range(3):
                        for wl in range(WB):
                            v = wl + 2 - kj
                            mm(dst, selv[0:120, kj, wl, :], rs[g % 2][0:120, :, v:v + 3], start=(kj == 0 and wl == 0), stop=False)
                    for n, (kj, a, _) in enumerate(EDGES):
                        v = a % 2 + 2 - kj
                        last = mm(dst, selev[0:48, n, :], res[g % 2][0:48, a // 2, :, v:v + 3], start=False, stop=(n == 5))
                    last.then_inc(S["g_done"], 1)

                for g in range(MG):
                    pe.wait_ge(S[f"fk_loaded{g % 2}"], 48 * (g // 2 + 1))
                    pe.wait_ge(S["fs_ready"], g + 1)
                    if g >= 2:
                        pe.wait_ge(S["r_out"], g - 1)
                    f, st = fk[g % 2], fs[g % 2]
                    for w in range(0, WM, WB):
                        mm(bank[g % 2][0:120, 0:216], st[0:HM, w:w + WB, :], f[0:HM, :, w:w + WB + 4],
                           start=(w == 0), stop=(w == WM - WB))
                    for side in range(2):
                        w = side * WM
                        last = mm(bank[2 + g % 2][0:48, 144 * side:144 * side + 144], st[0:HM, w:w + 2, :],
                                  f[0:HM, :, w:w + 6], start=True, stop=True)
                    last.then_inc(S["r_done"], 1)
                    if g:
                        combine(g - 1)
                combine(MG - 1)
                pe.wait_ge(S["gi_ready"], 1)
                for q in range(3):
                    g0, g1 = (0, 6, 12)[q], (6, 12, 16)[q]
                    last = mm(bank[5 + q][0:NW, 0:(g1 - g0) * NW], c_("ones")[0:NW, 0:NW], gif[:, g0 * NW:g1 * NW], start=True, stop=True)
                last.then_inc(S["sq_done"], 1)
                pe.wait_ge(S["best_ready"], 1)
                nc.tensor.transpose(bank[0][0:MG, 0:NW], best, c_("ident")[0:NW, 0:NW]).then_inc(S["bt_done"], 1)
                pe.wait_ge(S["offc_ready"], 1)
                mm(bank[1][:, 0:18], c_("rep", MG), offc, start=True, stop=True).then_inc(S["rep_done"], 1)
                end_phase(pe, GRAM)

                def add_up(n, k):
                    at_ = y_at(n, k)
                    r0, r1 = fold_rows(n, k // 3)
                    kj = k % 3
                    b0 = 4 * (n % 2)
                    if k == 0:
                        if n >= 2:
                            pe.wait_ge(S["out_ready"], n - 1)
                        for q in range(4):
                            kind = 0 if n == q == 0 else 2 if (n, q) == (NF - 1, 3) else 1
                            mm(bank[b0 + q][:, 0:384], ident_b[:, :], left_b[:, kind, :], start=True, stop=False, skip_group_check=True)
                    pe.wait_ge(S["g_ready"], at_)
                    for wgt, src in ((c_("ident"), zz[n % 2]), (ident_b[:, :], gg[n % 2])):
                        for q in range(4):
                            a, z = max(2 * q, r0), min(2 * q + 2, r1)
                            if a < z:
                                dst = bank[b0 + q][:, 0:384].rearrange("p (r w) -> p r w", w=C)[:, a - 2 * q:z - 2 * q, kj:kj + WM]
                                last = mm(dst, wgt, rows(src)[:, a:z, kj:kj + WM], start=False, stop=(k == 8), skip_group_check=True)
                    last.then_inc(S["summed"], 1)

                for n in range(0, NF, 2):
                    for k in range(9):
                        add_up(n, k)
                        add_up(n + 1, k)
                end_phase(pe, FOLD)
                end_image(pe)


def kernel(x, L0_conv_qkv_w, L0_conv_dw_w, L0_conv_proj_w, L0_conv_temperature):
    import concourse.bacc as bacc
    from concourse.bass_utils import run_bass_kernel_spmd

    x = np.ascontiguousarray(x)
    B = x.shape[0]
    nc = bacc.Bacc("TRN2", target_bir_lowering=False, num_devices=1)
    dw = np.ascontiguousarray(np.asarray(L0_conv_dw_w).reshape(9, 9, THIRD).transpose(2, 1, 0))
    temp = np.ascontiguousarray(np.repeat(np.asarray(L0_conv_temperature).reshape(2, 2).T, 64, axis=0))
    arrays = {"x": x, "qkv_w": np.ascontiguousarray(L0_conv_qkv_w), "dw_w": dw,
              "proj_w": np.ascontiguousarray(L0_conv_proj_w), "temp": temp, "cst": const_table()}
    args = [nc.dram_tensor(f"in_{k}", a.shape, F32, kind="ExternalInput").ap() for k, a in arrays.items()]
    out = nc.dram_tensor("out", x.shape, F32, kind="ExternalOutput").ap()
    motif_kernel(nc, *args, out, B)
    r = run_bass_kernel_spmd(nc, [{f"in_{k}": a for k, a in arrays.items()}], core_ids=[0])
    return r.results[0]["out"]
```

```python
from contextlib import ExitStack

import numpy as np

import concourse.bass as bass
from concourse import mybir

F32 = mybir.dt.float32
BF16 = mybir.dt.bfloat16
U32 = mybir.dt.uint32
ALU = mybir.AluOpType
ACT = mybir.ActivationFunctionType
AX = mybir.AxisListType.X

H, W, C = 128, 128, 192
PLANE = W * C
IMG = H * PLANE
GROUPS, GC = 32, 6
HEADS, CH = 4, 48
THIRD = 64
SEG = 16384 // THIRD
MG, MC = 16, 8
HM, WM = W - 2, C - 2
NW = 9 * MC
PAD = 512
MAGIC = 12582912.0
WB = 5
FR = 8
NF = W // FR
HALO = FR + 2


def const_layout():
    widths = dict(ident=128, avg=128, ones=128, sel=15 * NW, sele=6 * NW, icol=96, i72=NW,
                  bmask=NW, self8=8, w8=8, jrow=9, ktab=9, ctab=NF, rep=128, sela=9, selk=81, base=NF,
                  cnt=3 * C, left=6 * C)
    at, out = 0, {}
    for k, w in widths.items():
        out[k] = (at, w)
        at += w
    return out, at


def const_table():
    lay, n = const_layout()
    t = np.zeros((128, n), np.float32)

    def put(name, a):
        o, w = lay[name]
        a = a.reshape(a.shape[0], -1)
        assert a.shape[1] == w
        t[:a.shape[0], o:o + w] = a

    put("ident", np.eye(128))
    put("avg", np.full((128, 128), 1.0 / 128))
    put("ones", np.ones((128, 128)))
    sel = np.zeros((128, 3, WB, NW))
    sele = np.zeros((128, 6, NW))
    for ki in range(3):
        for y in range(MC):
            for kj in range(3):
                m = y * 9 + ki * 3 + kj
                for wl in range(WB):
                    sel[wl * 24 + ki * MC + y, kj, wl, m] = 1
                for n_, (j, a, sign) in enumerate(EDGES):
                    if j == kj:
                        sele[a % 2 * 24 + ki * MC + y, n_, m] = sign
    put("sel", sel)
    put("sele", sele)
    icol = np.zeros((128, 96))
    for s in range(2):
        for c in range(CH):
            icol[64 * s + c, CH * s + c] = 1
    put("icol", icol)
    put("i72", np.eye(NW))
    m = np.arange(NW)
    put("bmask", (m[:, None] // 8 == m[None] // 8) * 1.0)
    put("self8", (m[:, None] % 8 == np.arange(8)[None]) * 1e30)
    put("w8", np.broadcast_to(8.0 - np.arange(8), (128, 8)))
    put("jrow", np.broadcast_to(np.arange(9.0), (128, 9)))
    put("ktab", np.broadcast_to(8.0 * np.arange(9), (128, 9)))
    g = np.arange(MG)
    chunk = (FR * np.arange(NF) - 2) * C + PAD
    put("ctab", g[:, None] * MC * PLANE + chunk[None])
    p = np.arange(128)
    put("rep", (g[:, None] == p[None] % MG) * 1.0)
    put("sela", (p[:, None] // MG == np.arange(9)[None]) * 1.0)
    i, k, j = p[:, None, None] // MG, np.arange(9)[None, :, None], np.arange(9)[None, None]
    put("selk", ((9 * i + k) // 8 == j) * 0.125)
    put("base", (p % MG)[:, None] * MC * PLANE + chunk[None])
    cols = np.full(C, 3.0)
    cols[[0, -1]], cols[[1, -2]] = 1, 2
    net = np.full(C, MAGIC)
    net[[1, -2]] = 0
    left = np.zeros((3, 2, C))
    left[0, 0] = left[1, 0] = left[1, 1] = left[2, 1] = net
    put("left", np.broadcast_to(left.reshape(1, -1), (128, 6 * C)))
    put("cnt", np.broadcast_to((np.arange(1, 4)[:, None] * cols[None]).ravel(), (128, 3 * C)))
    return t


EDGES = [(1, 2, 1), (1, 0, -1), (2, 2, 1), (2, 3, 1), (2, 0, -1), (2, 1, -1)]

DVE_T, PE_T, POOL_T = range(6), (6, 7), (8,)
STATS, QKV0, MIX0, QKV1, MIX1, NORM, GRAM, FOLD = range(8)
STEPS = 9


def motif_kernel(nc, x, qkv_w, dw_w, proj_w, temp, cst_d, out, B):
    x1d = nc.dram_tensor("x1_rows", [IMG], F32, kind="Internal").ap()
    xnd = nc.dram_tensor("x1_normed", [PAD + IMG + PAD], F32, kind="Internal").ap()
    vd = nc.dram_tensor("v_pieces", [128, CH * SEG], F32, kind="Internal").ap()
    xf = x.rearrange("b y w c -> b (y w c)")
    assert B & (B - 1) == 0
    outf = out.rearrange("b y w c -> b (y w c)")
    lay, ncst = const_layout()

    ctx = ExitStack()
    with ctx:
        def sb(name, shape, dt=F32):
            return ctx.enter_context(nc.sbuf_tensor(name, shape, dt))

        def sem(name):
            return ctx.enter_context(nc.semaphore(name))

        cnt_at, left_at = lay["cnt"][0], lay["left"][0]
        cst = sb("cst", [128, cnt_at])

        def c_(name, rows=128):
            o, w = lay[name]
            return cst[0:rows, o:o + w]

        w_lo = sb("w_lo", [128, 3 * C])
        w_hi = sb("w_hi", [128, 2, 3 * C])
        pw = sb("pw", [128, 4, C])
        dwt = sb("dwt", [128, 9, 9])
        tcol = sb("tcol", [128, 2])
        ablk = sb("ablk", [128, 128])
        at = sb("at", [128, 96])
        small = sb("small", [128, 1920])
        cnt = sb("cnt", [128, 3, C])
        ident_b = sb("ident_b", [128, 128], BF16)
        left_b = sb("left_b", [128, 3, 2 * C], BF16)
        diag = sb("diag", [128, len(PE_T), 9, 128])
        idxa = sb("idxa", [128, NF], U32)
        idxb = sb("idxb", [MG, 9, NF], U32)
        arena = sb("arena", [128, 42368])
        left_f = arena[:, 20000:20000 + 6 * C]
        bank = [ctx.enter_context(nc.psum_tensor(f"bank{i}", [128, 512], F32)) for i in range(8)]

        QUARTER = 16 * 2 * C
        xs = [arena[:, o:o + QUARTER].rearrange("p (r c) -> p r c", c=C) for o in (0, 6144, 12288, 21504)]
        bst = arena[:, 18432:18432 + GROUPS * 48].rearrange("p (g n) -> p g n", g=GROUPS)
        xg = [arena[:, o:o + QUARTER].rearrange("p (r c) -> p r c", c=C) for o in (23552, 29696)]
        bsx = arena[:, 35840:35840 + GROUPS * 24].rearrange("p (g n) -> p g n", g=GROUPS)
        mv = small[:, 768:832].rearrange("p (g n) -> p g n", g=GROUPS)
        mvh = small[:, 1792:1856].rearrange("p (g n) -> p g n", g=GROUPS)
        mvx = small[:, 1856:1920].rearrange("p (g n) -> p g n", g=GROUPS)
        dev = small[:, 832:864]
        var = small[:, 864:896]
        mean = small[:, 896:928]
        rstd = small[:, 928:960]
        nbias = small[:, 960:992]
        wide = small[:, 1024:1536].rearrange("p (n c) -> p n c", n=2)
        gnp = small[:, 992:996]
        zrow = small[0:1, 0:PAD]
        mrow = small[:, 1024:1408].rearrange("p (a c) -> p a c", a=2)
        rrow = small[:, 1536:1920].rearrange("p (a c) -> p a c", a=2)
        mr, rr = mrow[:, 0:1, :].to_broadcast([128, 32, C]), rrow[:, 0:1, :].to_broadcast([128, 32, C])

        NQ = CH * SEG
        qb = arena[:, 0:NQ]
        kb = arena[:, NQ:2 * NQ]
        o0 = 2 * NQ
        pre = arena[:, o0:o0 + 9 * 6 * 130].rearrange("p (t r c) -> p t r c", t=9, r=6)
        o0 += 9 * 6 * 130
        xa = [arena[:, o0 + 1536 * i:o0 + 1536 * (i + 1)].rearrange("p (s f) -> p s f", s=2) for i in range(1)]
        o0 += 1536
        xlo = [arena[:, o0 + 1024 * i:o0 + 1024 * (i + 1)].rearrange("p (s n) -> p s n", s=2) for i in range(2)]
        o0 += 2048
        xhi = [arena[:, o0 + 512 * i:o0 + 512 * (i + 1)] for i in range(2)]
        o0 += 1024
        vst = [arena[:, o0:o0 + 1536]]
        o0 += 1536
        acc = [arena[:, o0 + 512 * i:o0 + 512 * (i + 1)] for i in range(4)]
        o0 += 2048
        assert o0 <= 42368, o0
        o_qkv = o0
        junk = small[:, 1536:1792]
        sq = small[:, 0:96]
        nrm = small[:, 96:160]
        nsq = small[:, 160:224]
        rn = small[:, 224:288]
        lg = small[:, 288:336]
        mx = small[:, 336:337]
        nmx = small[:, 337:338]
        ex = small[:, 352:400]
        ssum = small[:, 338:339]
        rsum = small[:, 339:340]
        rq = small[:, 340:341]

        VB = 2 * NQ
        vb = arena[:, VB:VB + 16384].rearrange("p (e a w) -> p e a w", e=64, a=2)
        vbf = arena[:, VB:VB + 16384].rearrange("p (m w) -> p w m", w=128)
        ob = arena[:, 0:12288].rearrange("p (c w) -> p c w", w=128)
        obf = arena[:, 0:12288].rearrange("p (q w) -> p q w", w=384)
        xr = [arena[:, 12288 + 1536 * i:12288 + 1536 * (i + 1)].rearrange("p (r f) -> p r f", r=4) for i in range(2)]
        x1t = [arena[:, 15360 + 1536 * i:15360 + 1536 * (i + 1)].rearrange("p (r f) -> p r f", r=4) for i in range(2)]

        FW = C + 4
        fk = [arena[:, 4704 * i:4704 * (i + 1)].rearrange("p (q w) -> p q w", w=FW) for i in range(2)]
        o1 = 9408
        fs = [arena[:, o1 + 4608 * i:o1 + 4608 * (i + 1)].rearrange("p (w q) -> p w q", q=24) for i in range(2)]
        o1 += 9216
        rs = [arena[:, o1 + 216 * i:o1 + 216 * (i + 1)].rearrange("p (q v) -> p q v", v=9) for i in range(2)]
        o1 += 432
        res = [arena[:, o1 + 288 * i:o1 + 288 * (i + 1)].rearrange("p (s q v) -> p s q v", s=2, v=6) for i in range(2)]
        o1 += 576
        GN = MG * NW
        gs = arena[0:NW, o1:o1 + GN].rearrange("p (g m) -> p g m", g=MG)
        gi = arena[0:NW, o1 + GN:o1 + 2 * GN].rearrange("p (g m) -> p g m", g=MG)
        gt = arena[0:NW, o1 + 2 * GN:o1 + 3 * GN].rearrange("p (g m) -> p g m", g=MG)
        gif = arena[0:NW, o1 + GN:o1 + 2 * GN]
        sqm = small[0:NW, 0:16]
        d8 = small[0:NW, 128:256].rearrange("p (g c) -> p g c", g=MG)
        e8 = small[0:NW, 256:384].rearrange("p (g c) -> p g c", g=MG)
        dmin = small[0:NW, 16:32]
        best = small[0:NW, 32:48]
        bt = small[0:MG, 384:456].rearrange("p (j c) -> p j c", j=9)
        beq = small[0:MG, 456:528].rearrange("p (j c) -> p j c", j=9)
        tb = [small[0:MG, 528 + 9 * i:537 + 9 * i] for i in range(8)]
        offc = small[0:MG, 608:626]
        ib = small[0:MG, 640:640 + 9 * NF].rearrange("p (j n) -> p j n", j=9)
        rep = small[:, 800:818]
        ta = small[:, 818:827]
        ca = small[:, 827:828]
        ck = small[:, 828:837]
        tk = small[:, 840:921].rearrange("p (k j) -> p k j", k=9)
        ia = small[:, 924:924 + NF]

        CF = FR * C
        HF = HALO * C
        o2 = 0

        def ring(n, size):
            nonlocal o2
            got = [arena[:, o2 + size * i:o2 + size * (i + 1)] for i in range(n)]
            o2 += n * size
            return got

        ff = ring(4, CF)
        fx = ring(4, CF)
        hh = ring(4, HF)
        yy = ring(2, CF)
        zz = ring(4, CF)
        gg = [a.bitcast(BF16) for a in ring(4, CF // 2)]
        fm = ring(2, CF)
        assert o2 <= 42368, o2

        def rows(a):
            return a.rearrange("p (r w) -> p r w", w=C)

        names = ("first_loaded0 first_loaded1 first_read first_chain setup_chain setup_dma setup_done phase_done turn_in turn_on turn_in2 turn_on2 "
                 "xs0 xs1 xs2 xs3 stored next_loaded0 next_loaded1 next_read rows_ready quarter_chain quarter_ready mv_ready mean_ready dev_ready var_ready veps_ready std_ready wide_ready col_ready gn_ready "
                 "xa_loaded transposed xt_ready qkv_done pre_ready halo_done conv_done squared v_stored "
                 "gram_done norm_done nrm_ready root_ready lg_ready exp_ready ablk_ready at_done "
                 "v_loaded v_copied xr_loaded0 xr_loaded1 mixed mix_out projected x1_ready x1_stored0 x1_stored1 "
                 "fk_loaded0 fk_loaded1 fk_padded fs_ready r_done r_out g_done g_out gi_ready sq_done best_ready bt_done idx_ready offc_ready rep_done "
                 "ff_loaded0 ff_loaded1 ff_loaded2 ff_loaded3 hh_loaded0 hh_loaded1 hh_loaded2 hh_loaded3 "
                 "y_ready z_ready g_ready summed base_ready out_ready out_stored0 out_stored1 "
                 "cnt_loaded pe_conv pool_conv pool_tap dve_chain pool_chain act_chain border_done").split()
        S = {n: sem(n) for n in names}
        keep = {"first_loaded0", "first_loaded1", "first_read", "first_chain", "setup_chain", "setup_dma", "setup_done", "turn_in", "turn_on", "turn_in2", "turn_on2"} | {f"hh_loaded{i}" for i in range(4)}
        cleared = [S[n] for n in names if n not in keep]
        setup_chain = S["setup_chain"]
        first_loaded, first_read, first_chain = (S["first_loaded0"], S["first_loaded1"]), S["first_read"], S["first_chain"]
        next_loaded = (S["next_loaded0"], S["next_loaded1"])
        setup_dma, setup_done, phase_done = S["setup_dma"], S["setup_done"], S["phase_done"]
        turn_in, turn_on, turn_in2, turn_on2 = S["turn_in"], S["turn_on"], S["turn_in2"], S["turn_on2"]

        def end_phase(eng, ph):
            eng.drain().then_inc(phase_done, 1)
            eng.wait_ge(phase_done, 5 * (ph + 1))

        def end_image(eng):
            eng.drain().then_inc(turn_in, 1)
            eng.wait_ge(turn_on, 1)
            eng.drain().then_inc(turn_in2, 1)
            eng.wait_ge(turn_on2, 1)
            eng.drain()

        def y_at(n, k):
            return 18 * (n // 2) + 2 * k + n % 2 + 1

        def fold_rows(n, ki):
            return max(0, ki - FR * n), min(FR, HM + ki - FR * n)

        SD = 16 * 16
        block = ctx.enter_context(nc.Block())

        @block.sync
        def _(sp):
            sp.dma_start(cst[:, :], cst_d[:, 0:cnt_at]).then_inc(setup_dma, 16)
            sp.dma_start(left_f, cst_d[:, left_at:left_at + 6 * C]).then_inc(setup_dma, 16)
            sp.dma_start(w_lo[:, :], qkv_w[0:128, :]).then_inc(setup_dma, 16)
            sp.dma_start(w_hi[0:64, 0, :], qkv_w[128:192, :]).then_inc(setup_dma, 16)
            sp.dma_start(w_hi[64:128, 1, :], qkv_w[128:192, :]).then_inc(setup_dma, 16)
            sp.dma_start(dwt[0:64, :, :], dw_w).then_inc(setup_dma, 16)
            sp.dma_start(dwt[64:128, :, :], dw_w).then_inc(setup_dma, 16)
            sp.dma_start(tcol[:, :], temp).then_inc(setup_dma, 16)
            sp.wait_ge(setup_done, 2)
            for n, a, z in ((0, 0, 0), (0, 1, 1), (1, 0, 1), (1, 1, 2), (2, 0, 2), (3, 1, 0)):
                sp.dma_start(pw[a:128:2, n, :], proj_w[64 * z:64 * z + 64, :]).then_inc(setup_dma, 16)
            sp.dma_start(xnd[0:PAD].rearrange("(a n) -> a n", a=1), zrow[:, :]).then_inc(setup_dma, 16)
            sp.dma_start(xnd[PAD + IMG:].rearrange("(a n) -> a n", a=1), zrow[:, :]).then_inc(setup_dma, 16)
            sp.wait_ge(setup_dma, SD)
            sp.wait_ge(setup_done, 3)

            def pairs(flat, first, n):
                a = flat[first * 2 * PLANE:(first + n) * 2 * PLANE]
                return a.rearrange("(r p f) -> p r f", p=128, f=2 * C)

            def load_quarter(flat, i, loaded):
                sp.dma_start(xg[i % 2].rearrange("p (r a) c -> p r (a c)", a=2), pairs(flat, 16 * i, 16)).then_inc(loaded[i % 2], 16)

            for i in range(4):
                if i >= 2:
                    sp.wait_ge(first_read, i - 1)
                load_quarter(xf[0, :], i, first_loaded)

            with sp.Fori(0, B) as b:
                xb = xf[b, :]
                xnext = xf[(b + 1) & (B - 1), :]
                ob_ = outf[b, :]
                end_phase(sp, STATS)

                for hp in range(2):
                    for n in range(STEPS + 3):
                        if n < STEPS:
                            g = STEPS * hp + n
                            if g:
                                sp.wait_ge(S["transposed"], 3 * g)
                            for s in range(2):
                                row = 64 * hp + 32 * s + (4 * n - 3 if n else -1)
                                k = 4 if n else 2
                                lo, hi = 0, 128
                                per = k * C
                                if row < 0:
                                    sp.dma_start(xa[0][0:64, s, 0:per], xb[0:PLANE].rearrange("(p f) -> p f", p=64)).then_inc(S["xa_loaded"], 16)
                                    sp.dma_start(xa[0][64:128, s, 0:per], xb[0:PLANE].rearrange("(p f) -> p f", p=64)).then_inc(S["xa_loaded"], 16)
                                elif row + k > H:
                                    sp.dma_start(xa[0][0:96, s, 0:per], xb[row * PLANE:H * PLANE].rearrange("(p f) -> p f", p=96)).then_inc(S["xa_loaded"], 16)
                                    sp.dma_start(xa[0][96:128, s, 0:per], xb[(H - 1) * PLANE:H * PLANE].rearrange("(p f) -> p f", p=32)).then_inc(S["xa_loaded"], 16)
                                else:
                                    sp.dma_start(xa[0][:, s, 0:per], xb[row * PLANE:(row + k) * PLANE].rearrange("(p f) -> p f", p=128)).then_inc(S["xa_loaded"], 16)
                        if n >= 4:
                            m = n - 3
                            sp.wait_ge(S["v_copied"], 3 * (8 * hp + m))
                            sp.dma_start(vd[:, 1536 * (m - 1):1536 * m], vst[0]).then_inc(S["v_stored"], 16)
                    sp.wait_ge(S["v_stored"], 128 * (hp + 1))

                    def load_v():
                        for s in range(2):
                            for j in range(3):
                                for a in range(2):
                                    src = vd[64 * s:64 * s + 64, :].rearrange("e (r a j w) -> j a r e w", a=2, j=3, w=128)
                                    sp.dma_start(vb[64 * s + j:64 * s + CH:3, :, a, :], src[j, a]).then_inc(S["v_loaded"], 16)

                    sp.wait_ge(S["conv_done"], 48 * (hp + 1))
                    load_v()
                    end_phase(sp, QKV0 + 2 * hp)
                    for j in range(9):
                        if j < 8:
                            if j >= 2:
                                sp.wait_ge(S["x1_ready"], 32 * hp + 4 * (j - 1))
                            sp.dma_start(xr[j % 2], pairs(xb, 32 * hp + 4 * j, 4)).then_inc(S[f"xr_loaded{j % 2}"], 16)
                        if j:
                            m = j - 1
                            sp.wait_ge(S["x1_ready"], 32 * hp + 4 * (m + 1))
                            sp.dma_start(pairs(x1d, 32 * hp + 4 * m, 4), x1t[m % 2]).then_inc(S[f"x1_stored{m % 2}"], 16)
                    for i in range(2):
                        sp.wait_ge(S[f"x1_stored{i}"], 64 * (hp + 1))
                    end_phase(sp, MIX0 + 2 * hp)

                for i in range(4):
                    sp.dma_start(xs[i].rearrange("p (r a) c -> p r (a c)", a=2),
                                 pairs(x1d, 16 * i, 16)).then_inc(S[f"xs{i}"], 16)
                for i in range(4):
                    if i < 3:
                        sp.wait_ge(S["gn_ready"], 2 + i)
                    else:
                        sp.wait_ge(S["quarter_ready"], 1)
                    sp.dma_start(pairs(xnd[PAD:PAD + IMG], 16 * i, 16),
                                 xs[i].rearrange("p (r a) c -> p r (a c)", a=2)).then_inc(S["stored"], 16)
                sp.wait_ge(S["stored"], 64)
                end_phase(sp, NORM)

                planes = xnd[PAD:PAD + IMG].rearrange("(y h w) -> h y w", y=H, w=C)
                sp.wait_ge(S["fk_padded"], 2)
                for g in range(MG):
                    if g >= 2:
                        sp.wait_ge(S["r_done"], g - 1)
                    for ki in range(3):
                        sp.dma_start(fk[g % 2][0:HM, 8 * ki:8 * ki + 8, 2:2 + C],
                                     planes[ki:ki + HM, 8 * g:8 * g + 8, :]).then_inc(S[f"fk_loaded{g % 2}"], 16)
                    if g in (1, 2, 5, 8):
                        i = (1, 2, 5, 8).index(g)
                        if i >= 2:
                            sp.wait_ge(S["next_read"], i - 1)
                        load_quarter(xnext, i, next_loaded)
                end_phase(sp, GRAM)

                fin = xnd[PAD:PAD + IMG].rearrange("(g i n f) -> n i g f", g=MG, i=MC, n=NF)
                x1in = x1d.rearrange("(g i n f) -> n i g f", g=MG, i=MC, n=NF)
                oo = ob_.rearrange("(g i n f) -> n i g f", g=MG, i=MC, n=NF)

                def store(n):
                    sp.wait_ge(S["out_ready"], n + 1)
                    sp.dma_start(oo[n], fm[n % 2]).then_inc(S[f"out_stored{n % 2}"], 16)

                for n in range(NF):
                    if n >= 4:
                        sp.wait_ge(S["out_ready"], n - 3)
                    sp.dma_start(ff[n % 4], fin[n]).then_inc(S[f"ff_loaded{n % 4}"], 16)
                    sp.dma_start(fx[n % 4], x1in[n]).then_inc(S[f"ff_loaded{n % 4}"], 16)
                    if n >= 3:
                        store(n - 3)
                for n in range(NF - 3, NF):
                    store(n)
                sp.wait_ge(S["base_ready"], NF)
                sp.dma_start(cnt[:, :, :].rearrange("p a c -> p (a c)"), cst_d[:, cnt_at:cnt_at + 3 * C]).then_inc(S["cnt_loaded"], 16)
                sp.wait_ge(S["cnt_loaded"], 16)
                for i in range(2):
                    sp.wait_ge(S[f"out_stored{i}"], 16 * NF // 2)
                end_phase(sp, FOLD)

                sp.wait_ge(turn_in, 4)
                sp.sem_clear(turn_in)
                sp.sem_clear(turn_on2)
                for s_ in cleared:
                    sp.sem_clear(s_)
                sp.sem_inc(turn_on, 1)
                sp.wait_ge(turn_in2, 4)
                sp.sem_clear(turn_in2)
                sp.sem_clear(turn_on)
                sp.sem_inc(turn_on2, 1)

        @block.gpsimd
        def _(pool):
            pool.memset(w_hi[64:128, 0, :], 0.0).then_inc(setup_chain, 1)
            pool.wait_ge(setup_chain, 1)
            pool.memset(w_hi[0:64, 1, :], 0.0).then_inc(setup_chain, 1)
            pool.wait_ge(setup_chain, 2)
            pool.memset(pw[:, :, :], 0.0)
            pool.memset(ablk[:, :], 0.0)
            pool.memset(arena[:, o_qkv:VB + 16384], 0.0)
            pool.memset(small[:, :], 0.0).then_inc(setup_done, 1)
            pool.memset(cnt[:, :, :], 0.0).then_inc(setup_done, 1)
            pool.wait_ge(setup_dma, SD)
            pool.tensor_scalar(ident_b[:, :], c_("ident"), -1.0, None, ALU.mult)
            pool.tensor_copy(left_b[:, :, :].rearrange("p a c -> p (a c)"), left_f).then_inc(setup_done, 1)
            pool.wait_ge(setup_done, 3)
            with pool.Fori(0, B):
                end_phase(pool, STATS)
                for hp in range(2):
                    pool.memset(pre[:, :, :, 0:130:129], 0.0)
                    if hp == 0:
                        pool.drain()
                        pool.memset(pre[0:64, :, 4, 1:129], 0.0)
                    pool.drain().then_inc(S["border_done"], 1)

                    def convolve(n, t):
                        pool.wait_ge(S["pre_ready"], 81 * hp + 9 * n + t + 1)
                        if hp or n > 1:
                            pool.wait_ge(S["v_copied"], 3 * (8 * hp + n - 1))
                        a, b_ = (acc[i].rearrange("p (r w) -> p r w", w=128) for i in (2, 3))
                        for j in range(9):
                            dst = b_ if j else a
                            pool.tensor_scalar(dst, pre[:, t, j // 3:j // 3 + 4, j % 3:j % 3 + 128], dwt[:, t, j:j + 1], None, ALU.mult).then_inc(S["pool_tap"], 1)
                            pool_n[0] += 1
                            pool.wait_ge(S["pool_tap"], pool_n[0])
                            if j:
                                ins = pool.tensor_tensor(a, a, b_, ALU.add)
                                if j < 8:
                                    ins.then_inc(S["pool_tap"], 1)
                                    pool_n[0] += 1
                                    pool.wait_ge(S["pool_tap"], pool_n[0])
                        ins.then_inc(S["pool_conv"], 1)

                    if hp == 0:
                        pool_n = [0]
                    for n in range(1, STEPS):
                        for t in POOL_T:
                            convolve(n, t)
                    end_phase(pool, QKV0 + 2 * hp)
                    end_phase(pool, MIX0 + 2 * hp)
                pool.wait_ge(S["rows_ready"], 2)
                pool.wait_ge(S["xs3"], 16)
                pool.tensor_tensor(xs[3], xs[3], mr, ALU.subtract).then_inc(S["quarter_chain"], 1)
                pool.wait_ge(S["quarter_chain"], 1)
                pool.tensor_tensor(xs[3], xs[3], rr, ALU.mult).then_inc(S["quarter_ready"], 1)
                end_phase(pool, NORM)
                for i in range(2):
                    pool.memset(fk[i][:, :, 0:2], 0.0)
                    pool.memset(fk[i][:, :, C + 2:C + 4], 0.0).then_inc(S["fk_padded"], 1)
                end_phase(pool, GRAM)

                def load_neighbours(n, k):
                    src = xnd.rearrange("(n a) -> n a", a=1)
                    if k == 0:
                        if n >= 4:
                            pool.wait_ge(S["y_ready"], y_at(n - 4, 8))
                        pool.indirect_dma_start(hh[n % 4], None, src,
                                                bass.IndirectOffsetOnAxis(ap=idxa[:, n:n + 1], axis=0)).then_inc(S[f"hh_loaded{n % 4}"], 16)
                    else:
                        pool.wait_ge(S["y_ready"], y_at(n, k - 1))
                        i = 8 - k
                        pool.indirect_dma_start(hh[n % 4][16 * i:16 * i + 16, :], None, src,
                                                bass.IndirectOffsetOnAxis(ap=idxb[:, i + 1, n:n + 1], axis=0)).then_inc(S[f"hh_loaded{n % 4}"], 16)

                def base(n):
                    pool.wait_ge(S[f"ff_loaded{n % 4}"], 32 * (n // 4 + 1))
                    if n >= 2:
                        pool.wait_ge(S[f"out_stored{n % 2}"], 16 * (n // 2))
                    f, m = rows(ff[n % 4]), rows(fm[n % 2])
                    parts = [(0, 1, 0), (1, 2, 1), (2, FR, 2)] if n == 0 else \
                        [(0, FR - 2, 2), (FR - 2, FR - 1, 1), (FR - 1, FR, 0)] if n == NF - 1 else [(0, FR, 2)]
                    for a, z, kind in parts:
                        last = pool.tensor_tensor(m[:, a:z, :], f[:, a:z, :],
                                                  cnt[:, kind:kind + 1, :].to_broadcast([128, z - a, C]), ALU.mult)
                    last.then_inc(S["pool_chain"], 1)
                    pool.wait_ge(S["pool_chain"], n + 1)
                    pool.tensor_tensor(fm[n % 2], fm[n % 2], fx[n % 4], ALU.add).then_inc(S["base_ready"], 1)

                load_neighbours(0, 0)
                load_neighbours(1, 0)
                for n in range(0, NF, 2):
                    if n + 2 < NF:
                        load_neighbours(n + 2, 0)
                        load_neighbours(n + 3, 0)
                    for k in range(1, 9):
                        load_neighbours(n, k)
                        load_neighbours(n + 1, k)
                        if k == 3:
                            base(n)
                        if k == 6:
                            base(n + 1)
                end_phase(pool, FOLD)
                end_image(pool)

        @block.scalar
        def _(act):
            act.wait_ge(setup_done, 3)
            with act.Fori(0, B):
                def root(k):
                    act.wait_ge(S["veps_ready"], k + 1)
                    nc.scalar.activation(dev, var, ACT.Sqrt).then_inc(S["std_ready"], 1)

                root(0)
                end_phase(act, STATS)
                for hp in range(2):
                    def take_transposed(n):
                        g = STEPS * hp + n
                        k = 4 if n else 2
                        if g > 1:
                            act.wait_ge(S["qkv_done"], 9 * (g - 1))
                        for j in range(3):
                            act.wait_ge(S["transposed"], 3 * g + j + 1)
                            dst = xlo[g % 2][:, j, 0:k * 128] if j < 2 else xhi[g % 2][:, 0:k * 128]
                            c = 1 if j == 2 else 0
                            nc.scalar.activation(dst.rearrange("p (q v) -> p q v", v=k),
                                                 bank[j][:, 0:k * 128].rearrange("p (v q) -> p q v", v=k),
                                                 ACT.Identity, scale=gnp[:, c:c + 1],
                                                 bias=gnp[:, 2 + c:3 + c]).then_inc(S["xt_ready"], 1)

                    def squares(n):
                        act.wait_ge(S["conv_done"], 48 * hp + 6 * n)
                        for c in range(6 * (n - 1), 6 * n):
                            for z, buf in enumerate((qb, kb)):
                                a_n[0] += 1
                                if a_n[0] > 1:
                                    act.wait_ge(S["act_chain"], a_n[0] - 1)
                                nc.scalar.activation(junk, buf[:, c * SEG:(c + 1) * SEG], ACT.Square,
                                                     accum_out=sq[:, CH * z + c:CH * z + c + 1]).then_inc(S["act_chain"], 1)

                    def move_up(n, t):
                        if n > 1 and t in DVE_T:
                            act.wait_ge(S["conv_done"], 48 * hp + 6 * (n - 2) + t + 1)
                        elif n > 1 and t in PE_T:
                            act.wait_ge(S["pe_conv"], 16 * hp + 2 * (n - 2) + t - 5)
                        elif n > 1:
                            act.wait_ge(S["pool_conv"], 8 * hp + n - 1)
                        else:
                            act.wait_ge(S["pre_ready"], 81 * hp + t + 1)
                        nc.scalar.activation(pre[:, t, 0:2, 1:129], pre[:, t, 4:6, 1:129], ACT.Copy).then_inc(S["halo_done"], 1)

                    def sort_v(n):
                        if n > 1 or hp:
                            act.wait_ge(S["v_stored"], 16 * (8 * hp + n - 1))
                        for t in range(3):
                            if t < 2:
                                act.wait_ge(S["pe_conv"], 16 * hp + 2 * (n - 1) + t + 1)
                                made = bank[6 + t][:, :]
                            else:
                                act.wait_ge(S["pool_conv"], 8 * hp + n)
                                made = acc[2]
                            for z in range(2):
                                w0 = (3 * z + t) // 2
                                dst = vst[0].rearrange("p (r a q w) -> p r a q w", a=2, q=128, w=3)[:, :, (z + t) % 2, :, w0]
                                src = made.rearrange("p (r q z) -> p r q z", z=2, q=128)[:, :, :, z]
                                last = nc.scalar.activation(dst, src, ACT.Copy)
                            last.then_inc(S["v_copied"], 1)

                    if hp == 0:
                        a_n = [0]
                    take_transposed(0)
                    for n in range(STEPS):
                        if n:
                            move_up(n, 0)
                        else:
                            act.wait_ge(S["border_done"], hp + 1)
                        for t in range(9):
                            i = 81 * hp + 9 * n + t
                            if n and t < 8:
                                move_up(n, t + 1)
                            if t == 7 and n < STEPS - 1:
                                take_transposed(n + 1)
                            act.wait_ge(S["qkv_done"], i + 1)
                            if n:
                                act.wait_ge(S["halo_done"], 72 * hp + 9 * (n - 1) + t + 1)
                            src = bank[3 + i % 3]
                            if n == 0:
                                parts = [(0, 64, 1, 2), (64, 128, 0, 2)] if hp == 0 else [(0, 128, 0, 2)]
                                first = 4
                            else:
                                parts = [(0, 64, 0, 4), (64, 128, 0, 3)] if hp and n == STEPS - 1 else [(0, 128, 0, 4)]
                                first = 2
                            for a, z, r0, r1 in parts:
                                last = nc.scalar.activation(
                                    pre[a:z, t, first + r0:first + r1, 1:129],
                                    src[a:z, 128 * r0:128 * r1].rearrange("p (r w) -> p r w", w=128), ACT.Copy)
                            if hp and n == STEPS - 1:
                                last = nc.scalar.activation(pre[64:128, t, 5, 1:129], w_hi[64:128, 0, 0:128], ACT.Copy)
                            last.then_inc(S["pre_ready"], 1)
                        if n >= 2:
                            sort_v(n - 1)
                            squares(n - 1)
                    squares(STEPS - 1)
                    act.wait_ge(S["act_chain"], 96 * (hp + 1))
                    act.drain().then_inc(S["squared"], 1)
                    sort_v(STEPS - 1)
                    for s in range(2):
                        r = slice(64 * s, 64 * s + CH)
                        act.wait_ge(S["nrm_ready"], 2 * hp + s + 1)
                        nc.scalar.activation(nsq[r, 0:49], nrm[r, 0:49], ACT.Sqrt).then_inc(S["root_ready"], 1)
                    for s in range(2):
                        r = slice(64 * s, 64 * s + CH)
                        act.wait_ge(S["lg_ready"], 2 * hp + s + 1)
                        nc.scalar.activation(ex[r, :], lg[r, :], ACT.Exp, bias=nmx[r, :],
                                             accum_out=ssum[r, :]).then_inc(S["exp_ready"], 1)
                    end_phase(act, QKV0 + 2 * hp)
                    for g in range(32):
                        act.wait_ge(S["mixed"], 32 * hp + g + 1)
                        nc.scalar.activation(ob[:, :, 4 * g:4 * g + 4],
                                             bank[g % 2][:, 0:384].rearrange("p (u c) -> p c u", u=4),
                                             ACT.Copy).then_inc(S["mix_out"], 1)
                    end_phase(act, MIX0 + 2 * hp)
                root(1)
                end_phase(act, NORM)

                def columns_first(g):
                    act.wait_ge(S[f"fk_loaded{g % 2}"], 48 * (g // 2 + 1))
                    if g >= 2:
                        act.wait_ge(S["r_done"], g - 1)
                    nc.scalar.activation(fs[g % 2][0:HM, :, :], fk[g % 2][0:HM, :, 2:2 + C].rearrange("p q w -> p w q"),
                                         ACT.Copy).then_inc(S["fs_ready"], 1)

                columns_first(0)
                for g in range(MG):
                    if g + 1 < MG:
                        columns_first(g + 1)
                    act.wait_ge(S["r_done"], g + 1)
                    if g >= 2:
                        act.wait_ge(S["g_done"], g - 1)
                    nc.scalar.activation(rs[g % 2][0:120, :, :], bank[g % 2][0:120, 0:216].rearrange("p (q v) -> p q v", v=9), ACT.Copy)
                    nc.scalar.activation(res[g % 2][0:48, :, :, :].rearrange("p s q v -> p (s q v)"),
                                         bank[2 + g % 2][0:48, 0:288], ACT.Copy).then_inc(S["r_out"], 1)
                end_phase(act, GRAM)

                for n in range(0, NF, 2):
                    for k in range(9):
                        for c in (n, n + 1):
                            r0, r1 = fold_rows(c, k // 3)
                            kj = k % 3
                            at_ = y_at(c, k)
                            act.wait_ge(S["y_ready"], at_)
                            if at_ > 4:
                                act.wait_ge(S["summed"], at_ - 4)
                            nc.scalar.activation(rows(zz[at_ % 4])[:, r0:r1, kj:kj + WM],
                                                 rows(yy[c % 2])[:, r0:r1, kj:kj + WM], ACT.Copy,
                                                 bias=MAGIC if k % 2 == 0 else -MAGIC).then_inc(S["z_ready"], 1)
                end_phase(act, FOLD)
                end_image(act)

        @block.vector
        def _(dve):
            dve.wait_ge(setup_done, 3)
            dve.wait_ge(setup_dma, SD)
            for i, t in enumerate(PE_T):
                for j in range(9):
                    last = nc.vector.tensor_scalar(diag[:, i, j, :], c_("ident"), dwt[:, t, j:j + 1], None, ALU.mult)
            last.then_inc(setup_done, 1)
            def quarter_stats(i, loaded, count, read):
                dve.wait_ge(loaded[i % 2], count)
                for g in range(GROUPS):
                    last = nc.vector.bn_stats(bsx[:, g, 6 * i:6 * i + 6], xg[i % 2][:, :, GC * g:GC * g + GC])
                last.then_inc(read, 1)

            for i in range(4):
                quarter_stats(i, first_loaded, 16 * (i // 2 + 1), first_read)
            dve.wait_ge(first_read, 4)
            for g in range(GROUPS):
                last = nc.vector.bn_aggr(mvx[:, g, :], bsx[:, g, :])
            last.then_inc(first_read, 1)
            dve.wait_ge(first_read, 5)

            with dve.Fori(0, B) as b:
                chain = [0]

                def link(ins):
                    chain[0] += 1
                    ins.then_inc(S["dve_chain"], 1)
                    dve.wait_ge(S["dve_chain"], chain[0])

                def group_stats(k):
                    m_ = (mvx, mv)[k]
                    if k:
                        link(nc.vector.tensor_tensor(dev, mvh[:, :, 0], mv[:, :, 0], ALU.subtract))
                        link(nc.vector.tensor_tensor(mv, mvh, mv, ALU.add))
                        link(nc.vector.tensor_scalar(mv, mv, 0.5, None, ALU.mult))
                        link(nc.vector.scalar_tensor_tensor(dev, dev, 0.25, dev, ALU.mult, ALU.mult))
                        nc.vector.tensor_tensor(mv[:, :, 1], mv[:, :, 1], dev, ALU.add).then_inc(S["mv_ready"], 1)
                        dve.wait_ge(S["mv_ready"], 1)
                    dve.wait_ge(S["mean_ready"], k + 1)
                    link(nc.vector.tensor_copy(mean, bank[0][:, 0:GROUPS]))
                    link(nc.vector.tensor_tensor(dev, m_[:, :, 0], mean, ALU.subtract))
                    link(nc.vector.tensor_tensor(dev, dev, dev, ALU.mult))
                    nc.vector.tensor_tensor(var, dev, m_[:, :, 1], ALU.add).then_inc(S["dev_ready"], 1)
                    dve.wait_ge(S["var_ready"], k + 1)
                    nc.vector.tensor_scalar(var, bank[1][:, 0:GROUPS], 1e-5, None, ALU.add).then_inc(S["veps_ready"], 1)
                    dve.wait_ge(S["std_ready"], k + 1)
                    link(nc.vector.reciprocal(rstd, dev))

                group_stats(0)
                link(nc.vector.scalar_tensor_tensor(nbias, mean, -1.0, rstd, ALU.mult, ALU.mult))
                for z, a in enumerate((rstd, nbias)):
                    w_ = wide[:, z, 0:C].rearrange("p (g c) -> p g c", c=GC)
                    link(nc.vector.tensor_copy(w_, a.rearrange("p (g a) -> p g a", a=1).to_broadcast([128, GROUPS, GC])))
                    last = nc.vector.tensor_copy(wide[:, z, C:256], wide[:, z, 128:192])
                    last.then_inc(S["wide_ready"], 1)
                dve.wait_ge(S["col_ready"], 1)
                nc.vector.tensor_copy(gnp, bank[2][:, 0:4]).then_inc(S["gn_ready"], 1)
                end_phase(dve, STATS)

                for hp in range(2):
                    for n in range(1, STEPS):
                        for t0 in DVE_T[::2]:
                            ts, summed = (t0, t0 + 1), [0, 0]

                            def tap(t, j):
                                return pre[:, t, j // 3:j // 3 + 4, j % 3:j % 3 + 128]

                            for j in range(9):
                                for t in ts:
                                    a = acc[t % 2].rearrange("p (r w) -> p r w", w=128)
                                    if j:
                                        dve.wait_ge(S["dve_chain"], summed[t % 2])
                                    else:
                                        dve.wait_ge(S["pre_ready"], 81 * hp + 9 * n + t + 1)
                                        done = 48 * hp + 6 * (n - 1) + t - 1
                                        if done > 0:
                                            dve.wait_ge(S["conv_done"], done)
                                    if j == 0:
                                        ins = nc.vector.tensor_scalar(a, tap(t, 0), dwt[:, t, 0:1], None, ALU.mult)
                                    elif j < 8:
                                        ins = nc.vector.scalar_tensor_tensor(a, tap(t, j), dwt[:, t, j:j + 1], a, ALU.mult, ALU.add)
                                    else:
                                        dst = (qb, kb)[t // 3][:, 1536 * (n - 1):1536 * n]
                                        dst = dst.rearrange("p (r w c) -> p r w c", w=128, c=3)[:, :, :, t % 3]
                                        nc.vector.scalar_tensor_tensor(dst, tap(t, 8), dwt[:, t, 8:9], a, ALU.mult, ALU.add).then_inc(S["conv_done"], 1)
                                        continue
                                    ins.then_inc(S["dve_chain"], 1)
                                    chain[0] += 1
                                    summed[t % 2] = chain[0]
                    for s in range(2):
                        r = slice(64 * s, 64 * s + CH)
                        dve.wait_ge(S["norm_done"], hp + 1)
                        nc.vector.tensor_scalar(nrm[r, 0:49], bank[3 + s][r, 0:49], 1e-12, None, ALU.max).then_inc(S["nrm_ready"], 1)
                    for s in range(2):
                        r = slice(64 * s, 64 * s + CH)
                        dve.wait_ge(S["root_ready"], 2 * hp + s + 1)
                        link(nc.vector.reciprocal(rn[r, 0:49], nsq[r, 0:49]))
                        link(nc.vector.tensor_tensor(rq[r, :], rn[r, 0:1], tcol[r, hp:hp + 1], ALU.mult))
                        link(nc.vector.scalar_tensor_tensor(lg[r, :], bank[s][r, 0:CH], rq[r, :], rn[r, 1:49], ALU.mult, ALU.mult))
                        link(nc.vector.tensor_reduce(mx[r, :], lg[r, :], AX, ALU.max))
                        nc.vector.tensor_scalar(nmx[r, :], mx[r, :], -1.0, None, ALU.mult).then_inc(S["lg_ready"], 1)
                    for s in range(2):
                        r = slice(64 * s, 64 * s + CH)
                        dve.wait_ge(S["exp_ready"], 2 * hp + s + 1)
                        link(nc.vector.reciprocal(rsum[r, :], ssum[r, :]))
                        nc.vector.tensor_scalar(ablk[r, 64 * s:64 * s + CH], ex[r, :], rsum[r, :], None, ALU.mult).then_inc(S["ablk_ready"], 1)
                    dve.wait_ge(S["at_done"], hp + 1)
                    nc.vector.tensor_copy(at[:, :], bank[5][:, 0:96])
                    end_phase(dve, QKV0 + 2 * hp)

                    for j in range(8):
                        dve.wait_ge(S[f"xr_loaded{j % 2}"], 64 * hp + 16 * (j // 2 + 1))
                        if j >= 2 or hp:
                            dve.wait_ge(S[f"x1_stored{j % 2}"], 64 * hp + 16 * (j // 2))
                        for r in range(4):
                            i = 4 * j + r
                            dve.wait_ge(S["projected"], 32 * hp + i + 1)
                            nc.vector.tensor_tensor(x1t[j % 2][:, r, :], xr[j % 2][:, r, :], bank[4 + i % 3][:, 0:384], ALU.add).then_inc(S["x1_ready"], 1)
                        dve.wait_ge(S["x1_ready"], 32 * hp + 4 * (j + 1))
                        rc = x1t[j % 2].rearrange("p r (a c) -> p (r a) c", c=C)
                        at_ = 6 * j
                        for g in range(GROUPS):
                            last = nc.vector.bn_stats(bst[:, g, at_:at_ + 6], rc[:, :, GC * g:GC * g + GC])
                        link(last)
                    for g in range(GROUPS):
                        last = nc.vector.bn_aggr((mvh, mv)[hp][:, g, :], bst[:, g, :])
                    link(last)
                    end_phase(dve, MIX0 + 2 * hp)

                group_stats(1)
                for a, row in ((mean, mrow), (rstd, rrow)):
                    nc.vector.tensor_copy(row[:, 0, :].rearrange("p (g c) -> p g c", c=GC),
                                          a.rearrange("p (g a) -> p g a", a=1).to_broadcast([128, GROUPS, GC])).then_inc(S["rows_ready"], 1)
                dve.wait_ge(S["rows_ready"], 2)
                for i in range(3):
                    dve.wait_ge(S[f"xs{i}"], 16)
                    link(nc.vector.tensor_tensor(xs[i], xs[i], mr, ALU.subtract))
                    nc.vector.tensor_tensor(xs[i], xs[i], rr, ALU.mult).then_inc(S["gn_ready"], 1)
                end_phase(dve, NORM)

                for g in range(MG):
                    dve.wait_ge(S["g_done"], g + 1)
                    for ki in range(3):
                        dst = gs[:, g, :].rearrange("p (y k) -> p y k", k=9)[:, :, 3 * ki:3 * ki + 3]
                        last = nc.vector.tensor_copy(dst, bank[4 + g % 2][0:NW, 24 * ki:24 * ki + 24].rearrange("p (y k) -> p y k", k=3))
                    last.then_inc(S["g_out"], 1)
                    if g in (1, 4, 7, 10):
                        i = (1, 4, 7, 10).index(g)
                        quarter_stats(i, next_loaded, 16 * (i // 2 + 1), S["next_read"])
                    if g == 12:
                        dve.wait_ge(S["next_read"], 4)
                        for gg_ in range(GROUPS):
                            last = nc.vector.bn_aggr(mvx[:, gg_, :], bsx[:, gg_, :])
                        link(last)
                dve.wait_ge(S["g_out"], MG)
                i72 = c_("i72", NW).rearrange("p (a m) -> p a m", a=1).to_broadcast([NW, MG, NW])
                nc.vector.tensor_tensor(gi, gs, i72, ALU.mult).then_inc(S["gi_ready"], 1)
                dve.wait_ge(S["gi_ready"], 1)
                link(nc.vector.tensor_reduce(sqm, gi, AX, ALU.add))
                dve.wait_ge(S["sq_done"], 1)
                for q in range(3):
                    g0, g1 = (0, 6, 12)[q], (6, 12, 16)[q]
                    last = nc.vector.tensor_tensor(gt[:, g0:g1, :], bank[5 + q][0:NW, 0:(g1 - g0) * NW].rearrange("p (g m) -> p g m", m=NW),
                                                   sqm[:, g0:g1].rearrange("p (g a) -> p g a", a=1).to_broadcast([NW, g1 - g0, NW]), ALU.add)
                link(last)
                link(nc.vector.scalar_tensor_tensor(gt.rearrange("p g m -> p (g m)"), gs.rearrange("p g m -> p (g m)"), -2.0,
                                                    gt.rearrange("p g m -> p (g m)"), ALU.mult, ALU.add))
                bmask = c_("bmask", NW).rearrange("p (a m) -> p a m", a=1).to_broadcast([NW, MG, NW])
                link(nc.vector.tensor_tensor(gt, gt, bmask, ALU.mult))
                for g in range(MG):
                    last = nc.vector.tensor_reduce(d8[:, g, :], gt[:, g, :].rearrange("p (j c) -> p c j", j=9), AX, ALU.add)
                link(last)
                self8 = c_("self8", NW).rearrange("p (a m) -> p a m", a=1).to_broadcast([NW, MG, 8])
                link(nc.vector.tensor_tensor(d8, d8, self8, ALU.add))
                link(nc.vector.tensor_reduce(dmin, d8, AX, ALU.min))
                link(nc.vector.tensor_tensor(e8, d8, dmin.rearrange("p (g a) -> p g a", a=1).to_broadcast([NW, MG, 8]), ALU.is_le))
                w8 = c_("w8", NW).rearrange("p (a m) -> p a m", a=1).to_broadcast([NW, MG, 8])
                link(nc.vector.tensor_tensor(e8, e8, w8, ALU.mult))
                nc.vector.tensor_reduce(best, e8, AX, ALU.max).then_inc(S["best_ready"], 1)
                dve.wait_ge(S["bt_done"], 1)
                link(nc.vector.tensor_copy(bt.rearrange("p j c -> p (j c)"), bank[0][0:MG, 0:NW]))
                u, e, off = tb[0], tb[1], tb[2]
                link(nc.vector.tensor_reduce(u, bt, AX, ALU.min))
                link(nc.vector.tensor_tensor(beq, bt, u.rearrange("p (g a) -> p g a", a=1).to_broadcast([MG, 9, 8]), ALU.is_equal))
                link(nc.vector.tensor_reduce(offc[:, 9:18], beq, AX, ALU.add))
                link(nc.vector.tensor_scalar(u, u, -1.0, 8.0, ALU.mult, ALU.add))
                jr = c_("jrow", MG)
                link(nc.vector.tensor_tensor(e, u, jr, ALU.is_ge))
                link(nc.vector.tensor_tensor(e, e, jr, ALU.add))
                link(nc.vector.tensor_scalar(e, e, 1.0, None, ALU.subtract))
                link(nc.vector.tensor_tensor(u, u, c_("ktab", MG), ALU.add))
                link(nc.vector.scalar_tensor_tensor(u, e, -9.0, u, ALU.mult, ALU.add))
                link(nc.vector.tensor_scalar(tb[3], u, 3.0, None, ALU.is_ge))
                link(nc.vector.tensor_scalar(tb[4], u, 6.0, None, ALU.is_ge))
                link(nc.vector.tensor_tensor(tb[3], tb[3], tb[4], ALU.add))
                link(nc.vector.scalar_tensor_tensor(off, e, float(PLANE), u, ALU.mult, ALU.add))
                link(nc.vector.scalar_tensor_tensor(offc[:, 0:9], tb[3], float(C - 3), off, ALU.mult, ALU.add))
                nc.vector.tensor_copy(tb[5], offc[:, 0:9]).then_inc(S["offc_ready"], 1)
                dve.wait_ge(S["offc_ready"], 1)
                link(nc.vector.tensor_tensor(ib, tb[5].rearrange("p (j a) -> p j a", a=1).to_broadcast([MG, 9, NF]),
                                             c_("ctab", MG).rearrange("p (a n) -> p a n", a=1).to_broadcast([MG, 9, NF]), ALU.add))
                link(nc.vector.tensor_copy(idxb[:, :, :], ib))
                dve.wait_ge(S["rep_done"], 1)
                link(nc.vector.tensor_copy(rep, bank[1][:, 0:18]))
                link(nc.vector.tensor_tensor(ta, rep[:, 0:9], c_("sela"), ALU.mult))
                link(nc.vector.tensor_reduce(ca, ta, AX, ALU.add))
                link(nc.vector.tensor_scalar(ia, c_("base"), ca, None, ALU.add))
                link(nc.vector.tensor_copy(idxa[:, :], ia))
                link(nc.vector.tensor_tensor(tk, c_("selk").rearrange("p (k j) -> p k j", k=9),
                                             rep[:, 9:18].rearrange("p (a j) -> p a j", a=1).to_broadcast([128, 9, 9]), ALU.mult))
                link(nc.vector.tensor_reduce(ck, tk, AX, ALU.add))
                end_phase(dve, GRAM)

                def product(n, k):
                    at_ = y_at(n, k)
                    r0, r1 = fold_rows(n, k // 3)
                    ki, kj = k // 3, k % 3
                    if k == 0:
                        dve.wait_ge(S[f"ff_loaded{n % 4}"], 32 * (n // 4 + 1))
                    dve.wait_ge(S[f"hh_loaded{n % 4}"], b * (144 * NF // 4) + 144 * (n // 4) + 16 * (k + 1))
                    a = rows(ff[n % 4])[:, r0:r1, kj:kj + WM]
                    z = rows(hh[n % 4])[:, 2 - ki + r0:2 - ki + r1, 0:WM]
                    nc.vector.scalar_tensor_tensor(rows(yy[n % 2])[:, r0:r1, kj:kj + WM], a, ck[:, k:k + 1], z,
                                                   ALU.mult, ALU.mult).then_inc(S["y_ready"], 1)

                def above(n, k):
                    at_ = y_at(n, k)
                    r0, r1 = fold_rows(n, k // 3)
                    kj = k % 3
                    dve.wait_ge(S["z_ready"], at_)
                    if at_ > 4:
                        dve.wait_ge(S["summed"], at_ - 4)
                    nc.vector.scalar_tensor_tensor(rows(gg[at_ % 4])[:, r0:r1, kj:kj + WM],
                                                   rows(zz[at_ % 4])[:, r0:r1, kj:kj + WM],
                                                   -MAGIC if k % 2 == 0 else MAGIC,
                                                   rows(yy[n % 2])[:, r0:r1, kj:kj + WM],
                                                   ALU.add, ALU.is_gt).then_inc(S["g_ready"], 1)

                def finish(n):
                    dve.wait_ge(S["summed"], y_at(n, 8))
                    dve.wait_ge(S["base_ready"], n + 1)
                    b0 = 4 * (n % 2)
                    for q in range(4):
                        last = nc.vector.tensor_tensor(fm[n % 2][:, 384 * q:384 * q + 384], bank[b0 + q][:, 0:384],
                                                       fm[n % 2][:, 384 * q:384 * q + 384], ALU.add)
                    last.then_inc(S["out_ready"], 1)

                for n in range(0, NF, 2):
                    for k in range(9):
                        product(n, k)
                        if k == 0 and n:
                            finish(n - 2)
                        product(n + 1, k)
                        if k == 0 and n:
                            finish(n - 1)
                        above(n, k)
                        above(n + 1, k)
                        dve.wait_ge(S["g_ready"], y_at(n + 1, k))
                finish(NF - 2)
                finish(NF - 1)
                end_phase(dve, FOLD)
                end_image(dve)

        @block.tensor
        def _(pe):
            pe.wait_ge(setup_done, 4)
            pe.wait_ge(setup_dma, SD)
            pe.wait_ge(first_read, 5)
            mm = nc.tensor.matmul
            with pe.Fori(0, B):
                def average(k):
                    if k:
                        pe.wait_ge(S["mv_ready"], 1)
                    mm(bank[0][:, 0:GROUPS], c_("avg"), (mvx, mv)[k][:, :, 0], start=True, stop=True).then_inc(S["mean_ready"], 1)
                    pe.wait_ge(S["dev_ready"], k + 1)
                    mm(bank[1][:, 0:GROUPS], c_("avg"), var, start=True, stop=True).then_inc(S["var_ready"], 1)

                average(0)
                pe.wait_ge(S["wide_ready"], 2)
                one = c_("ones")[0:1, 0:1]
                for z in range(2):
                    for h in range(2):
                        last = mm(bank[2][:, 2 * z + h:2 * z + h + 1], wide[0:1, z, 128 * h:128 * h + 128], one, start=True, stop=True)
                last.then_inc(S["col_ready"], 1)
                end_phase(pe, STATS)

                for hp in range(2):
                    def transposes(n):
                        g = STEPS * hp + n
                        k = 4 if n else 2
                        dmas = 2 * (g + 1) + 1 + (1 if hp and n == STEPS - 1 else 0)
                        pe.wait_ge(S["xa_loaded"], 16 * dmas)
                        if g:
                            pe.wait_ge(S["xt_ready"], 3 * g)
                        xv = xa[0].rearrange("p s (v c) -> p s v c", c=C)
                        for j in range(2):
                            for v in range(k):
                                last = nc.tensor.transpose(bank[j][:, 128 * v:128 * v + 128], xv[:, j, v, 0:128], c_("ident"))
                            last.then_inc(S["transposed"], 1)
                        for v in range(k):
                            for s in range(2):
                                last = mm(bank[2][64 * s:64 * s + 64, 128 * v:128 * v + 128], xv[:, s, v, 128:C], c_("ident"), start=True, stop=True)
                        last.then_inc(S["transposed"], 1)

                    def convolve(n, t):
                        pe.wait_ge(S["pre_ready"], 81 * hp + 9 * n + t + 1)
                        if hp or n > 1:
                            pe.wait_ge(S["v_copied"], 3 * (8 * hp + n - 2) + t - 5)
                        for j in range(9):
                            last = mm(bank[t][:, :], diag[:, t - 6, j, :], pre[:, t, j // 3:j // 3 + 4, j % 3:j % 3 + 128],
                                      start=(j == 0), stop=(j == 8))
                        last.then_inc(S["pe_conv"], 1)

                    transposes(0)
                    for n in range(STEPS):
                        k = 4 if n else 2
                        g = STEPS * hp + n
                        pe.wait_ge(S["xt_ready"], 3 * (g + 1))
                        if n + 1 < STEPS:
                            transposes(n + 1)
                        for t in range(9):
                            if n > 1 and t in (2, 4):
                                convolve(n - 1, PE_T[t // 2 - 1])
                            i = 9 * g + t
                            if i >= 3:
                                pe.wait_ge(S["pre_ready"], i - 2)
                            for s in range(2):
                                dst = bank[3 + i % 3][64 * s:64 * s + 64, 0:128 * k]
                                mm(dst, w_lo[:, 64 * t:64 * t + 64], xlo[g % 2][:, s, 0:128 * k], start=True, stop=False)
                                last = mm(dst, w_hi[:, s, 64 * t:64 * t + 64], xhi[g % 2][:, 0:128 * k], start=False, stop=True)
                            last.then_inc(S["qkv_done"], 1)
                    for t in PE_T:
                        convolve(STEPS - 1, t)
                    pe.wait_ge(S["xt_ready"], 3 * STEPS * (hp + 1))
                    pe.wait_ge(S["conv_done"], 48 * (hp + 1))
                    qv = qb.rearrange("p (c u) -> p u c", u=SEG)
                    kv = kb.rearrange("p (c u) -> p u c", u=SEG)
                    for u in range(SEG):
                        for s in range(2):
                            r = slice(64 * s, 64 * s + 64)
                            last = mm(bank[s][64 * s:64 * s + CH, 0:CH], qv[r, u, :], kv[r, u, :],
                                      start=(u == 0), stop=(u == SEG - 1))
                    pe.wait_ge(S["squared"], hp + 1)
                    for s in range(2):
                        r = slice(64 * s, 64 * s + 64)
                        mm(bank[3 + s][64 * s:64 * s + CH, 0:1], sq[r, 0:CH], c_("ones")[r, 0:1], start=True, stop=True)
                        last = mm(bank[3 + s][64 * s:64 * s + CH, 1:49], c_("ones")[r, 0:CH], sq[r, CH:2 * CH], start=True, stop=True)
                    last.then_inc(S["norm_done"], 1)
                    pe.wait_ge(S["ablk_ready"], 2 * (hp + 1))
                    mm(bank[5][:, 0:96], ablk[:, :], c_("icol"), start=True, stop=True).then_inc(S["at_done"], 1)
                    end_phase(pe, QKV0 + 2 * hp)

                    KR = 64 + CH
                    pe.wait_ge(S["v_loaded"], 192 * (hp + 1))
                    for g in range(32):
                        if g >= 2:
                            pe.wait_ge(S["mix_out"], 32 * hp + g - 1)
                        for i in range(4):
                            last = mm(bank[g % 2][:, 96 * i:96 * i + 96], vbf[0:KR, 4 * g + i, :], at[0:KR, :], start=True, stop=True)
                        last.then_inc(S["mixed"], 1)
                    pe.wait_ge(S["mix_out"], 32 * (hp + 1))
                    for i in range(32):
                        if i >= 3:
                            pe.wait_ge(S["x1_ready"], 32 * hp + i - 2)
                        bk = bank[4 + i % 3]
                        w3 = obf[:, i, :].rearrange("p (q w) -> p w q", w=3)
                        mm(bk[:, 0:C], w3[:, 0, :], pw[:, 0, :], start=True, stop=False)
                        mm(bk[:, 0:C], w3[:, 1, :], pw[:, 2, :], start=False, stop=True)
                        mm(bk[:, C:2 * C], w3[:, 1, :], pw[:, 3, :], start=True, stop=False)
                        mm(bk[:, C:2 * C], w3[:, 2, :], pw[:, 1, :], start=False, stop=True).then_inc(S["projected"], 1)
                    end_phase(pe, MIX0 + 2 * hp)
                average(1)
                end_phase(pe, NORM)

                selv = c_("sel").rearrange("p (k w m) -> p k w m", k=3, w=WB)
                selev = c_("sele").rearrange("p (n m) -> p n m", m=NW)

                def combine(g):
                    pe.wait_ge(S["r_out"], g + 1)
                    if g >= 2:
                        pe.wait_ge(S["g_out"], g - 1)
                    dst = bank[4 + g % 2][0:NW, 0:NW]
                    for kj in range(3):
                        for wl in range(WB):
                            v = wl + 2 - kj
                            mm(dst, selv[0:120, kj, wl, :], rs[g % 2][0:120, :, v:v + 3], start=(kj == 0 and wl == 0), stop=False)
                    for n, (kj, a, _) in enumerate(EDGES):
                        v = a % 2 + 2 - kj
                        last = mm(dst, selev[0:48, n, :], res[g % 2][0:48, a // 2, :, v:v + 3], start=False, stop=(n == 5))
                    last.then_inc(S["g_done"], 1)

                for g in range(MG):
                    pe.wait_ge(S[f"fk_loaded{g % 2}"], 48 * (g // 2 + 1))
                    pe.wait_ge(S["fs_ready"], g + 1)
                    if g >= 2:
                        pe.wait_ge(S["r_out"], g - 1)
                    f, st = fk[g % 2], fs[g % 2]
                    for w in range(0, WM, WB):
                        mm(bank[g % 2][0:120, 0:216], st[0:HM, w:w + WB, :], f[0:HM, :, w:w + WB + 4],
                           start=(w == 0), stop=(w == WM - WB))
                    for side in range(2):
                        w = side * WM
                        last = mm(bank[2 + g % 2][0:48, 144 * side:144 * side + 144], st[0:HM, w:w + 2, :],
                                  f[0:HM, :, w:w + 6], start=True, stop=True)
                    last.then_inc(S["r_done"], 1)
                    if g:
                        combine(g - 1)
                combine(MG - 1)
                pe.wait_ge(S["gi_ready"], 1)
                for q in range(3):
                    g0, g1 = (0, 6, 12)[q], (6, 12, 16)[q]
                    last = mm(bank[5 + q][0:NW, 0:(g1 - g0) * NW], c_("ones")[0:NW, 0:NW], gif[:, g0 * NW:g1 * NW], start=True, stop=True)
                last.then_inc(S["sq_done"], 1)
                pe.wait_ge(S["best_ready"], 1)
                nc.tensor.transpose(bank[0][0:MG, 0:NW], best, c_("ident")[0:NW, 0:NW]).then_inc(S["bt_done"], 1)
                pe.wait_ge(S["offc_ready"], 1)
                mm(bank[1][:, 0:18], c_("rep", MG), offc, start=True, stop=True).then_inc(S["rep_done"], 1)
                end_phase(pe, GRAM)

                def add_up(n, k):
                    at_ = y_at(n, k)
                    r0, r1 = fold_rows(n, k // 3)
                    kj = k % 3
                    b0 = 4 * (n % 2)
                    if k == 0:
                        if n >= 2:
                            pe.wait_ge(S["out_ready"], n - 1)
                        for q in range(4):
                            kind = 0 if n == q == 0 else 2 if (n, q) == (NF - 1, 3) else 1
                            mm(bank[b0 + q][:, 0:384], ident_b[:, :], left_b[:, kind, :], start=True, stop=False, skip_group_check=True)
                    pe.wait_ge(S["g_ready"], at_)
                    for wgt, src in ((c_("ident"), zz[at_ % 4]), (ident_b[:, :], gg[at_ % 4])):
                        for q in range(4):
                            a, z = max(2 * q, r0), min(2 * q + 2, r1)
                            if a < z:
                                dst = bank[b0 + q][:, 0:384].rearrange("p (r w) -> p r w", w=C)[:, a - 2 * q:z - 2 * q, kj:kj + WM]
                                last = mm(dst, wgt, rows(src)[:, a:z, kj:kj + WM], start=False, stop=(k == 8), skip_group_check=True)
                    last.then_inc(S["summed"], 1)

                for n in range(0, NF, 2):
                    for k in range(9):
                        add_up(n, k)
                        add_up(n + 1, k)
                end_phase(pe, FOLD)
                end_image(pe)


def kernel(x, L0_conv_qkv_w, L0_conv_dw_w, L0_conv_proj_w, L0_conv_temperature):
    import concourse.bacc as bacc
    from concourse.bass_utils import run_bass_kernel_spmd

    x = np.ascontiguousarray(x)
    B = x.shape[0]
    nc = bacc.Bacc("TRN2", target_bir_lowering=False, num_devices=1)
    dw = np.ascontiguousarray(np.asarray(L0_conv_dw_w).reshape(9, 9, THIRD).transpose(2, 1, 0))
    temp = np.ascontiguousarray(np.repeat(np.asarray(L0_conv_temperature).reshape(2, 2).T, 64, axis=0))
    arrays = {"x": x, "qkv_w": np.ascontiguousarray(L0_conv_qkv_w), "dw_w": dw,
              "proj_w": np.ascontiguousarray(L0_conv_proj_w), "temp": temp, "cst": const_table()}
    args = [nc.dram_tensor(f"in_{k}", a.shape, F32, kind="ExternalInput").ap() for k, a in arrays.items()]
    out = nc.dram_tensor("out", x.shape, F32, kind="ExternalOutput").ap()
    motif_kernel(nc, *args, out, B)
    r = run_bass_kernel_spmd(nc, [{f"in_{k}": a for k, a in arrays.items()}], core_ids=[0])
    return r.results[0]["out"]
```

```python
from contextlib import ExitStack

import numpy as np

import concourse.bass as bass
from concourse import mybir

F32 = mybir.dt.float32
BF16 = mybir.dt.bfloat16
U32 = mybir.dt.uint32
ALU = mybir.AluOpType
ACT = mybir.ActivationFunctionType
AX = mybir.AxisListType.X

H, W, C = 128, 128, 192
PLANE = W * C
IMG = H * PLANE
GROUPS, GC = 32, 6
HEADS, CH = 4, 48
THIRD = 64
SEG = 16384 // THIRD
MG, MC = 16, 8
HM, WM = W - 2, C - 2
NW = 9 * MC
PAD = 512
MAGIC = 12582912.0
WB = 5
FR = 8
NF = W // FR
HALO = FR + 2


def const_layout():
    widths = dict(ident=128, avg=128, ones=128, icol=96, i72=NW,
                  bmask=NW, self8=8, w8=8, jrow=9, ktab=9, ctab=NF, rep=128, sela=9, selk=81, base=NF,
                  cnt=3 * C, left=6 * C, sel=15 * NW, sele=6 * NW)
    at, out = 0, {}
    for k, w in widths.items():
        out[k] = (at, w)
        at += w
    return out, at


def const_table():
    lay, n = const_layout()
    t = np.zeros((128, n), np.float32)

    def put(name, a):
        o, w = lay[name]
        a = a.reshape(a.shape[0], -1)
        assert a.shape[1] == w
        t[:a.shape[0], o:o + w] = a

    put("ident", np.eye(128))
    put("avg", np.full((128, 128), 1.0 / 128))
    put("ones", np.ones((128, 128)))
    sel = np.zeros((128, 3, WB, NW))
    sele = np.zeros((128, 6, NW))
    for ki in range(3):
        for y in range(MC):
            for kj in range(3):
                m = y * 9 + ki * 3 + kj
                for wl in range(WB):
                    sel[wl * 24 + ki * MC + y, kj, wl, m] = 1
                for n_, (j, a, sign) in enumerate(EDGES):
                    if j == kj:
                        sele[a % 2 * 24 + ki * MC + y, n_, m] = sign
    put("sel", sel)
    put("sele", sele)
    icol = np.zeros((128, 96))
    for s in range(2):
        for c in range(CH):
            icol[64 * s + c, CH * s + c] = 1
    put("icol", icol)
    put("i72", np.eye(NW))
    m = np.arange(NW)
    put("bmask", (m[:, None] // 8 == m[None] // 8) * 1.0)
    put("self8", (m[:, None] % 8 == np.arange(8)[None]) * 1e30)
    put("w8", np.broadcast_to(8.0 - np.arange(8), (128, 8)))
    put("jrow", np.broadcast_to(np.arange(9.0), (128, 9)))
    put("ktab", np.broadcast_to(8.0 * np.arange(9), (128, 9)))
    g = np.arange(MG)
    chunk = (FR * np.arange(NF) - 2) * C + PAD
    put("ctab", g[:, None] * MC * PLANE + chunk[None])
    p = np.arange(128)
    put("rep", (g[:, None] == p[None] % MG) * 1.0)
    put("sela", (p[:, None] // MG == np.arange(9)[None]) * 1.0)
    i, k, j = p[:, None, None] // MG, np.arange(9)[None, :, None], np.arange(9)[None, None]
    put("selk", ((9 * i + k) // 8 == j) * 0.125)
    put("base", (p % MG)[:, None] * MC * PLANE + chunk[None])
    cols = np.full(C, 3.0)
    cols[[0, -1]], cols[[1, -2]] = 1, 2
    net = np.full(C, MAGIC)
    net[[1, -2]] = 0
    left = np.zeros((3, 2, C))
    left[0, 0] = left[1, 0] = left[1, 1] = left[2, 1] = net
    put("left", np.broadcast_to(left.reshape(1, -1), (128, 6 * C)))
    put("cnt", np.broadcast_to((np.arange(1, 4)[:, None] * cols[None]).ravel(), (128, 3 * C)))
    return t


EDGES = [(1, 2, 1), (1, 0, -1), (2, 2, 1), (2, 3, 1), (2, 0, -1), (2, 1, -1)]

DVE_T, PE_T, POOL_T = range(5), (6,), (5, 7, 8)
STATS, QKV0, MIX0, QKV1, MIX1, GRAM, FOLD = range(7)
TAPS = 5
TAPS_AT = (9, 12, 15, 17, 19, 21, 23, 25, 27)
STEPS = 9


def motif_kernel(nc, x, qkv_w, dw_w, proj_w, temp, cst_d, out, B):
    x1d = nc.dram_tensor("x1_rows", [IMG], F32, kind="Internal").ap()
    xnd = nc.dram_tensor("x1_normed", [PAD + IMG + PAD], F32, kind="Internal").ap()
    vd = nc.dram_tensor("v_pieces", [128, CH * SEG], F32, kind="Internal").ap()
    xf = x.rearrange("b y w c -> b (y w c)")
    assert B & (B - 1) == 0
    outf = out.rearrange("b y w c -> b (y w c)")
    lay, ncst = const_layout()

    ARENA = 44400
    ctx = ExitStack()
    with ctx:
        def sb(name, shape, dt=F32):
            return ctx.enter_context(nc.sbuf_tensor(name, shape, dt))

        def sem(name):
            return ctx.enter_context(nc.semaphore(name))

        cnt_at, left_at = lay["cnt"][0], lay["left"][0]
        cst = sb("cst", [128, cnt_at])

        def c_(name, rows=128):
            o, w = lay[name]
            return cst[0:rows, o:o + w]

        w_lo = sb("w_lo", [128, 3 * C])
        w_hi = sb("w_hi", [128, 2, 3 * C])
        pw = sb("pw", [128, 4, C])
        dwt = sb("dwt", [128, 9, 9])
        tcol = sb("tcol", [128, 2])
        ablk = sb("ablk", [128, 128])
        at = sb("at", [128, 96])
        small = sb("small", [128, 1920])
        cnt = sb("cnt", [128, 3, C])
        ident_b = sb("ident_b", [128, 128], BF16)
        left_b = sb("left_b", [128, 3, 2 * C], BF16)
        diag = sb("diag", [128, len(PE_T), 9, 128])
        idxa = sb("idxa", [128, NF], U32)
        idxb = sb("idxb", [MG, 9, NF], U32)
        arena = sb("arena", [128, ARENA])
        left_f = arena[:, 20000:20000 + 6 * C]
        bank = [ctx.enter_context(nc.psum_tensor(f"bank{i}", [128, 512], F32)) for i in range(8)]

        QUARTER = 16 * 2 * C
        xs = [arena[:, o:o + QUARTER].rearrange("p (r c) -> p r c", c=C) for o in (14016, 23552, 29696, 35840)]
        bst = arena[:, 18432:18432 + GROUPS * 48].rearrange("p (g n) -> p g n", g=GROUPS)
        xg = [arena[:, o:o + QUARTER].rearrange("p (r c) -> p r c", c=C) for o in (23552, 29696)]
        bsx = arena[:, 35840:35840 + GROUPS * 24].rearrange("p (g n) -> p g n", g=GROUPS)
        mv = small[:, 768:832].rearrange("p (g n) -> p g n", g=GROUPS)
        mvh = small[:, 1792:1856].rearrange("p (g n) -> p g n", g=GROUPS)
        mvx = small[:, 1856:1920].rearrange("p (g n) -> p g n", g=GROUPS)
        dev = small[:, 832:864]
        var = small[:, 864:896]
        mean = small[:, 896:928]
        rstd = small[:, 928:960]
        nbias = small[:, 960:992]
        wide = small[:, 1024:1536].rearrange("p (n c) -> p n c", n=2)
        gnp = small[:, 992:996]
        zrow = small[0:1, 0:PAD]
        mrow = small[:, 1024:1408].rearrange("p (a c) -> p a c", a=2)
        rrow = small[:, 1536:1920].rearrange("p (a c) -> p a c", a=2)
        mr, rr = mrow[:, 0:1, :].to_broadcast([128, 32, C]), rrow[:, 0:1, :].to_broadcast([128, 32, C])

        NQ = CH * SEG
        qb = arena[:, 0:NQ]
        kb = arena[:, NQ:2 * NQ]
        o0 = 2 * NQ
        pre = arena[:, o0:o0 + 9 * 6 * 130].rearrange("p (t r c) -> p t r c", t=9, r=6)
        o0 += 9 * 6 * 130
        xa = arena[:, o0:o0 + 1536].rearrange("p (s f) -> p s f", s=2)
        o0 += 1536
        xlo = [arena[:, o0 + 1024 * i:o0 + 1024 * (i + 1)].rearrange("p (s n) -> p s n", s=2) for i in range(2)]
        o0 += 2048
        xhi = [arena[:, o0 + 512 * i:o0 + 512 * (i + 1)] for i in range(2)]
        o0 += 1024
        vst = [arena[:, o0:o0 + 1536]]
        o0 += 1536
        acc = [arena[:, o0 + 512 * i:o0 + 512 * (i + 1)] for i in range(3)]
        o0 += 3 * 512
        pool_acc = {t: arena[:, o0 + 512 * i:o0 + 512 * (i + 1)] for i, t in enumerate(POOL_T)}
        o0 += len(POOL_T) * 512
        pool_half = arena[:, o0:o0 + 512]
        o0 += 512
        taps = [arena[:, o0 + 512 * i:o0 + 512 * (i + 1)] for i in range(TAPS)]
        o0 += TAPS * 512
        assert o0 <= ARENA, o0
        junk = small[:, 1536:1792]
        sq = small[:, 0:96]
        nrm = small[:, 96:160]
        nsq = small[:, 160:224]
        rn = small[:, 224:288]
        lg = small[:, 288:336]
        mx = small[:, 336:337]
        nmx = small[:, 337:338]
        ex = small[:, 352:400]
        ssum = small[:, 338:339]
        rsum = small[:, 339:340]
        rq = small[:, 340:341]

        VB = 2 * NQ
        vb = arena[:, VB:VB + 16384].rearrange("p (e a w) -> p e a w", e=64, a=2)
        vbf = arena[:, VB:VB + 16384].rearrange("p (m w) -> p w m", w=128)
        ob = arena[:, 0:12288].rearrange("p (c w) -> p c w", w=128)
        obf = arena[:, 0:12288].rearrange("p (q w) -> p q w", w=384)
        xr = [arena[:, 12288 + 1536 * i:12288 + 1536 * (i + 1)].rearrange("p (r f) -> p r f", r=4) for i in range(2)]
        x1t = [arena[:, 15360 + 1536 * i:15360 + 1536 * (i + 1)].rearrange("p (r f) -> p r f", r=4) for i in range(2)]

        FW = C + 4
        fk = [arena[:, 4704 * i:4704 * (i + 1)].rearrange("p (q w) -> p q w", w=FW) for i in range(2)]
        o1 = 9408
        fs = [arena[:, o1 + 4608 * i:o1 + 4608 * (i + 1)].rearrange("p (w q) -> p w q", q=24) for i in range(2)]
        o1 += 9216
        rs = [arena[:, o1 + 216 * i:o1 + 216 * (i + 1)].rearrange("p (q v) -> p q v", v=9) for i in range(2)]
        o1 += 432
        res = [arena[:, o1 + 288 * i:o1 + 288 * (i + 1)].rearrange("p (s q v) -> p s q v", s=2, v=6) for i in range(2)]
        o1 += 576
        GN = MG * NW
        gs = arena[0:NW, o1:o1 + GN].rearrange("p (g m) -> p g m", g=MG)
        sels = arena[:, 42000:42000 + 21 * NW]
        gi = arena[0:NW, o1 + GN:o1 + 2 * GN].rearrange("p (g m) -> p g m", g=MG)
        gt = arena[0:NW, o1 + 2 * GN:o1 + 3 * GN].rearrange("p (g m) -> p g m", g=MG)
        gif = arena[0:NW, o1 + GN:o1 + 2 * GN]
        sqm = small[0:NW, 0:16]
        d8 = small[0:NW, 128:256].rearrange("p (g c) -> p g c", g=MG)
        e8 = small[0:NW, 256:384].rearrange("p (g c) -> p g c", g=MG)
        dmin = small[0:NW, 16:32]
        best = small[0:NW, 32:48]
        bt = small[0:MG, 384:456].rearrange("p (j c) -> p j c", j=9)
        beq = small[0:MG, 456:528].rearrange("p (j c) -> p j c", j=9)
        tb = [small[0:MG, 528 + 9 * i:537 + 9 * i] for i in range(8)]
        offc = small[0:MG, 608:626]
        ib = small[0:MG, 640:640 + 9 * NF].rearrange("p (j n) -> p j n", j=9)
        rep = small[:, 800:818]
        ta = small[:, 818:827]
        ca = small[:, 827:828]
        ck = small[:, 828:837]
        tk = small[:, 840:921].rearrange("p (k j) -> p k j", k=9)
        ia = small[:, 924:924 + NF]

        CF = FR * C
        HF = HALO * C
        o2 = 0

        def ring(n, size):
            nonlocal o2
            got = [arena[:, o2 + size * i:o2 + size * (i + 1)] for i in range(n)]
            o2 += n * size
            return got

        ff = ring(4, CF)
        fx = ring(4, CF)
        hh = ring(4, HF)
        yy = ring(2, CF)
        zz = ring(4, CF)
        gg = [a.bitcast(BF16) for a in ring(4, CF // 2)]
        fm = ring(2, CF)
        ou = ring(2, CF)
        assert o2 <= ARENA, o2

        def rows(a):
            return a.rearrange("p (r w) -> p r w", w=C)

        names = ("first_loaded0 first_loaded1 first_read lifted x1_measured setup_chain setup_dma setup_done phase_done "
                 "turn_in turn_on turn_in2 turn_on2 xs0 xs1 xs2 xs3 stored next_loaded0 next_loaded1 next_read "
                 "rows_ready quarter_chain quarter_ready mv_ready mean_ready dev_ready var_ready veps_ready "
                 "std_ready wide_ready col_ready gn_ready xa_loaded transposed xt_ready qkv_done pre_ready "
                 "halo_done own_halo conv_done squared v_stored norm_done nrm_ready root_ready lg_ready "
                 "exp_ready ablk_ready at_done v_loaded v_copied xr_loaded0 xr_loaded1 mixed mix_out projected "
                 "x1_ready x1_stored0 x1_stored1 fk_loaded0 fk_loaded1 fk_padded fs_ready r_done r_out g_done "
                 "g_out gi_ready sq_done best_ready bt_done offc_ready rep_done ff_loaded0 ff_loaded1 ff_loaded2 "
                 "ff_loaded3 hh_loaded0 hh_loaded1 hh_loaded2 hh_loaded3 y_ready z_ready g_ready summed "
                 "base_ready taken out_ready out_stored0 out_stored1 cnt_loaded pe_conv tap_ready tap_used "
                 "sels_loaded dve_chain pool_chain act_chain border_done").split()
        S = {n: sem(n) for n in names}
        keep = {"first_loaded0", "first_loaded1", "first_read", "setup_chain", "setup_dma", "setup_done", "turn_in", "turn_on", "turn_in2", "turn_on2"} | {f"hh_loaded{i}" for i in range(4)}
        cleared = [S[n] for n in names if n not in keep]
        setup_chain = S["setup_chain"]
        first_loaded, first_read = (S["first_loaded0"], S["first_loaded1"]), S["first_read"]
        next_loaded = (S["next_loaded0"], S["next_loaded1"])
        setup_dma, setup_done, phase_done = S["setup_dma"], S["setup_done"], S["phase_done"]
        turn_in, turn_on, turn_in2, turn_on2 = S["turn_in"], S["turn_on"], S["turn_in2"], S["turn_on2"]

        def end_phase(eng, ph):
            eng.drain().then_inc(phase_done, 1)
            eng.wait_ge(phase_done, 5 * (ph + 1))

        def end_image(eng):
            eng.drain().then_inc(turn_in, 1)
            eng.wait_ge(turn_on, 1)
            eng.drain().then_inc(turn_in2, 1)
            eng.wait_ge(turn_on2, 1)
            eng.drain()

        def y_at(n, k):
            return 18 * (n // 2) + 2 * k + n % 2 + 1

        def fold_rows(n, ki):
            return max(0, ki - FR * n), min(FR, HM + ki - FR * n)

        def adds_before(p):
            return 8 * (p // 9) + (1, 1, 2, 2, 3, 4, 5, 6, 7)[p % 9]

        SD = 16 * 16
        block = ctx.enter_context(nc.Block())

        @block.sync
        def _(sp):
            sp.dma_start(cst[:, :], cst_d[:, 0:cnt_at]).then_inc(setup_dma, 16)
            sp.dma_start(left_f, cst_d[:, left_at:left_at + 6 * C]).then_inc(setup_dma, 16)
            sp.dma_start(w_lo[:, :], qkv_w[0:128, :]).then_inc(setup_dma, 16)
            sp.dma_start(w_hi[0:64, 0, :], qkv_w[128:192, :]).then_inc(setup_dma, 16)
            sp.dma_start(w_hi[64:128, 1, :], qkv_w[128:192, :]).then_inc(setup_dma, 16)
            sp.dma_start(dwt[0:64, :, :], dw_w).then_inc(setup_dma, 16)
            sp.dma_start(dwt[64:128, :, :], dw_w).then_inc(setup_dma, 16)
            sp.dma_start(tcol[:, :], temp).then_inc(setup_dma, 16)
            sp.wait_ge(setup_done, 2)
            for n, a, z in ((0, 0, 0), (0, 1, 1), (1, 0, 1), (1, 1, 2), (2, 0, 2), (3, 1, 0)):
                sp.dma_start(pw[a:128:2, n, :], proj_w[64 * z:64 * z + 64, :]).then_inc(setup_dma, 16)
            sp.dma_start(xnd[0:PAD].rearrange("(a n) -> a n", a=1), zrow[:, :]).then_inc(setup_dma, 16)
            sp.dma_start(xnd[PAD + IMG:].rearrange("(a n) -> a n", a=1), zrow[:, :]).then_inc(setup_dma, 16)
            sp.wait_ge(setup_dma, SD)
            sp.wait_ge(setup_done, 3)

            def pairs(flat, first, n):
                a = flat[first * 2 * PLANE:(first + n) * 2 * PLANE]
                return a.rearrange("(r p f) -> p r f", p=128, f=2 * C)

            def load_quarter(flat, i, loaded):
                sp.dma_start(xg[i % 2].rearrange("p (r a) c -> p r (a c)", a=2), pairs(flat, 16 * i, 16)).then_inc(loaded[i % 2], 16)

            for i in range(4):
                if i >= 2:
                    sp.wait_ge(first_read, i - 1)
                load_quarter(xf[0, :], i, first_loaded)

            with sp.Fori(0, B) as b:
                xb = xf[b, :]
                xnext = xf[(b + 1) & (B - 1), :]
                ob_ = outf[b, :]
                end_phase(sp, STATS)

                for hp in range(2):
                    for n in range(STEPS + 3):
                        if n < STEPS:
                            g = STEPS * hp + n
                            if g:
                                sp.wait_ge(S["transposed"], 3 * g)
                            for s in range(2):
                                row = 64 * hp + 32 * s + (4 * n - 3 if n else -1)
                                k = 4 if n else 2

                                def pixels(lo, hi, src):
                                    sp.dma_start(xa[lo:hi, s, 0:k * C], src.rearrange("(p f) -> p f", p=hi - lo)).then_inc(S["xa_loaded"], 16)

                                if row < 0:
                                    pixels(0, 64, xb[0:PLANE])
                                    pixels(64, 128, xb[0:PLANE])
                                elif row + k > H:
                                    pixels(0, 96, xb[row * PLANE:H * PLANE])
                                    pixels(96, 128, xb[(H - 1) * PLANE:H * PLANE])
                                else:
                                    pixels(0, 128, xb[row * PLANE:(row + k) * PLANE])
                        if n >= 4:
                            m = n - 3
                            sp.wait_ge(S["v_copied"], 3 * (8 * hp + m))
                            sp.dma_start(vd[:, 1536 * (m - 1):1536 * m], vst[0]).then_inc(S["v_stored"], 16)
                    sp.wait_ge(S["v_stored"], 128 * (hp + 1))

                    def load_v():
                        for s in range(2):
                            for j in range(3):
                                for a in range(2):
                                    src = vd[64 * s:64 * s + 64, :].rearrange("e (r a j w) -> j a r e w", a=2, j=3, w=128)
                                    sp.dma_start(vb[64 * s + j:64 * s + CH:3, :, a, :], src[j, a]).then_inc(S["v_loaded"], 16)

                    sp.wait_ge(S["conv_done"], 40 * (hp + 1))
                    sp.wait_ge(S["tap_used"], 192 * (hp + 1))
                    load_v()
                    end_phase(sp, QKV0 + 2 * hp)
                    for j in range(9):
                        if j < 8:
                            if j >= 2:
                                sp.wait_ge(S["x1_ready"], 32 * hp + 4 * (j - 1))
                            sp.dma_start(xr[j % 2], pairs(xb, 32 * hp + 4 * j, 4)).then_inc(S[f"xr_loaded{j % 2}"], 16)
                        if j:
                            m = j - 1
                            sp.wait_ge(S["x1_ready"], 32 * hp + 4 * (m + 1))
                            sp.dma_start(pairs(x1d, 32 * hp + 4 * m, 4), x1t[m % 2]).then_inc(S[f"x1_stored{m % 2}"], 16)
                    for i in range(2):
                        sp.wait_ge(S[f"x1_stored{i}"], 64 * (hp + 1))
                    end_phase(sp, MIX0 + 2 * hp)

                def load_x1_quarter(i):
                    sp.dma_start(xs[i].rearrange("p (r a) c -> p r (a c)", a=2),
                                 pairs(x1d, 16 * i, 16)).then_inc(S[f"xs{i}"], 16)

                load_x1_quarter(0)
                load_x1_quarter(3)
                sp.dma_start(sels, cst_d[:, lay["sel"][0]:lay["sel"][0] + 21 * NW]).then_inc(S["sels_loaded"], 16)

                def store_quarter(i):
                    if i < 3:
                        sp.wait_ge(S["gn_ready"], 2 + i)
                    else:
                        sp.wait_ge(S["quarter_ready"], 1)
                    sp.dma_start(pairs(xnd[PAD:PAD + IMG], 16 * i, 16),
                                 xs[i].rearrange("p (r a) c -> p r (a c)", a=2)).then_inc(S["stored"], 16)

                planes = xnd[PAD:PAD + IMG].rearrange("(y h w) -> h y w", y=H, w=C)
                store_quarter(0)
                sp.wait_ge(S["stored"], 16)
                sp.wait_ge(S["fk_padded"], 2)
                for g in range(MG):
                    if g == 2:
                        load_x1_quarter(1)
                        load_x1_quarter(2)
                    if g == 3:
                        store_quarter(1)
                    if g in (4, 8, 12):
                        sp.wait_ge(S["stored"], 4 * g + 16)
                    if g >= 2:
                        sp.wait_ge(S["r_done"], g - 1)
                    for ki in range(3):
                        sp.dma_start(fk[g % 2][0:HM, 8 * ki:8 * ki + 8, 2:2 + C],
                                     planes[ki:ki + HM, 8 * g:8 * g + 8, :]).then_inc(S[f"fk_loaded{g % 2}"], 16)
                    if g in (4, 5):
                        store_quarter(g - 2)
                    if g == 7:
                        sp.wait_ge(S["stored"], 64)
                    if g in (7, 8, 10, 12):
                        i = (7, 8, 10, 12).index(g)
                        if i >= 2:
                            sp.wait_ge(S["next_read"], i - 1)
                        load_quarter(xnext, i, next_loaded)
                fin = xnd[PAD:PAD + IMG].rearrange("(g i n f) -> n i g f", g=MG, i=MC, n=NF)
                x1in = x1d.rearrange("(g i n f) -> n i g f", g=MG, i=MC, n=NF)

                def load_image(n):
                    sp.dma_start(ff[n % 4], fin[n]).then_inc(S[f"ff_loaded{n % 4}"], 16)

                def load_x1(n):
                    sp.dma_start(fx[n % 4], x1in[n]).then_inc(S[f"ff_loaded{n % 4}"], 16)

                sp.wait_ge(S["r_done"], MG)
                for n in range(2):
                    load_image(n)
                    load_x1(n)
                end_phase(sp, GRAM)

                oo = ob_.rearrange("(g i n f) -> n i g f", g=MG, i=MC, n=NF)

                def store(n):
                    sp.wait_ge(S["out_ready"], n + 1)
                    sp.dma_start(oo[n], fm[n % 2]).then_inc(S[f"out_stored{n % 2}"], 16)

                for n in range(0, NF, 2):
                    more = n + 2 < NF
                    if more:
                        sp.wait_ge(S["y_ready"], y_at(n, 0))
                        if n:
                            sp.wait_ge(S["base_ready"], n)
                        load_image(n + 2)
                        sp.wait_ge(S["y_ready"], y_at(n, 1))
                        load_x1(n + 2)
                    if n:
                        store(n - 2)
                        store(n - 1)
                    if more:
                        sp.wait_ge(S["y_ready"], y_at(n, 4))
                        load_image(n + 3)
                        sp.wait_ge(S["y_ready"], y_at(n, 6))
                        load_x1(n + 3)
                store(NF - 2)
                store(NF - 1)
                sp.wait_ge(S["base_ready"], NF)
                sp.dma_start(cnt[:, :, :].rearrange("p a c -> p (a c)"), cst_d[:, cnt_at:cnt_at + 3 * C]).then_inc(S["cnt_loaded"], 16)
                sp.wait_ge(S["cnt_loaded"], 16)
                for i in range(2):
                    sp.wait_ge(S[f"out_stored{i}"], 16 * NF // 2)
                end_phase(sp, FOLD)

                sp.wait_ge(turn_in, 4)
                sp.sem_clear(turn_in)
                sp.sem_clear(turn_on2)
                for s_ in cleared:
                    sp.sem_clear(s_)
                sp.sem_inc(turn_on, 1)
                sp.wait_ge(turn_in2, 4)
                sp.sem_clear(turn_in2)
                sp.sem_clear(turn_on)
                sp.sem_inc(turn_on2, 1)

        @block.gpsimd
        def _(pool):
            pool.memset(w_hi[64:128, 0, :], 0.0).then_inc(setup_chain, 1)
            pool.wait_ge(setup_chain, 1)
            pool.memset(w_hi[0:64, 1, :], 0.0).then_inc(setup_chain, 1)
            pool.wait_ge(setup_chain, 2)
            pool.memset(pw[:, :, :], 0.0)
            pool.memset(ablk[:, :], 0.0)
            pool.memset(small[:, :], 0.0).then_inc(setup_done, 1)
            pool.memset(cnt[:, :, :], 0.0).then_inc(setup_done, 1)
            pool.wait_ge(setup_dma, SD)
            pool.tensor_scalar(ident_b[:, :], c_("ident"), -1.0, None, ALU.mult)
            pool.tensor_copy(left_b[:, :, :].rearrange("p a c -> p (a c)"), left_f).then_inc(setup_done, 1)
            pool.wait_ge(setup_done, 3)
            with pool.Fori(0, B):
                end_phase(pool, STATS)
                for hp in range(2):
                    pool.memset(pre[:, :, :, 0:130:129], 0.0)
                    if hp == 0:
                        pool.drain()
                        pool.memset(pre[0:64, :, 4, 1:129], 0.0)
                    pool.drain().then_inc(S["border_done"], 1)

                    for n in range(1, STEPS):
                        for q, t in enumerate(POOL_T):
                            q += 3 * (8 * hp + n - 1)
                            a = pool_acc[t]
                            if t > 5 and q > 2:
                                pool.wait_ge(S["v_copied"], 3 * (8 * hp + n - 1))
                            for m in range(1, 9):
                                new = (1, 3, 4, 5, 6, 7, 8, None)[m - 1]
                                if new:
                                    pool.wait_ge(S["tap_ready"], 9 * q + new + 1)
                                done = 8 * q + m - (1 if m == 8 else 2)
                                if done > 0:
                                    pool.wait_ge(S["tap_used"], done)
                                dst = first = (a, pool_half)[(m - 1) % 2]
                                if m < 3:
                                    first = taps[(9 * q + new - 1) % TAPS]
                                second = taps[(9 * q + new) % TAPS] if new else pool_half
                                if m == 8:
                                    dst = first = a
                                    if t == 5:
                                        dst = kb[:, 1536 * (n - 1):1536 * n].rearrange("p (w c) -> p w c", c=3)[:, :, 2]
                                pool.tensor_tensor(dst, first, second, ALU.add).then_inc(S["tap_used"], 1)
                    end_phase(pool, QKV0 + 2 * hp)
                    for i in range(32):
                        j, r = i // 4, i % 4
                        if r == 0:
                            pool.wait_ge(S[f"xr_loaded{j % 2}"], 64 * hp + 16 * (j // 2 + 1))
                        pool.wait_ge(S["lifted"], 32 * hp + i + 1)
                        pool.tensor_tensor(x1t[j % 2][:, r, :], x1t[j % 2][:, r, :], xr[j % 2][:, r, :], ALU.add).then_inc(S["x1_ready"], 1)
                    end_phase(pool, MIX0 + 2 * hp)
                for i in range(2):
                    pool.memset(fk[i][:, :, 0:2], 0.0)
                    pool.memset(fk[i][:, :, C + 2:C + 4], 0.0).then_inc(S["fk_padded"], 1)
                pool.wait_ge(S["rows_ready"], 2)
                pool.wait_ge(S["xs3"], 16)
                pool.tensor_tensor(xs[3], xs[3], mr, ALU.subtract).then_inc(S["quarter_chain"], 1)
                pool.wait_ge(S["quarter_chain"], 1)
                pool.tensor_tensor(xs[3], xs[3], rr, ALU.mult).then_inc(S["quarter_ready"], 1)
                end_phase(pool, GRAM)

                def load_neighbours(n, k):
                    src = xnd.rearrange("(n a) -> n a", a=1)
                    if k == 0:
                        if n >= 4:
                            pool.wait_ge(S["y_ready"], y_at(n - 4, 8))
                        pool.indirect_dma_start(hh[n % 4], None, src,
                                                bass.IndirectOffsetOnAxis(ap=idxa[:, n:n + 1], axis=0)).then_inc(S[f"hh_loaded{n % 4}"], 16)
                    else:
                        pool.wait_ge(S["y_ready"], y_at(n, k - 1))
                        i = 8 - k
                        pool.indirect_dma_start(hh[n % 4][16 * i:16 * i + 16, :], None, src,
                                                bass.IndirectOffsetOnAxis(ap=idxb[:, i + 1, n:n + 1], axis=0)).then_inc(S[f"hh_loaded{n % 4}"], 16)

                def base(n):
                    pool.wait_ge(S[f"ff_loaded{n % 4}"], 32 * (n // 4 + 1))
                    if n >= 2:
                        pool.wait_ge(S[f"out_stored{n % 2}"], 16 * (n // 2))
                    f, m = rows(ff[n % 4]), rows(fm[n % 2])
                    parts = [(0, 1, 0), (1, 2, 1), (2, FR, 2)] if n == 0 else \
                        [(0, FR - 2, 2), (FR - 2, FR - 1, 1), (FR - 1, FR, 0)] if n == NF - 1 else [(0, FR, 2)]
                    for a, z, kind in parts:
                        last = pool.tensor_tensor(m[:, a:z, :], f[:, a:z, :],
                                                  cnt[:, kind:kind + 1, :].to_broadcast([128, z - a, C]), ALU.mult)
                    last.then_inc(S["pool_chain"], 1)

                def base_end(n):
                    pool.wait_ge(S["pool_chain"], n + 1)
                    pool.tensor_tensor(fm[n % 2], fm[n % 2], fx[n % 4], ALU.add).then_inc(S["base_ready"], 1)

                def total(n):
                    pool.wait_ge(S["base_ready"], n + 1)
                    pool.wait_ge(S["taken"], n + 1)
                    pool.tensor_tensor(fm[n % 2], fm[n % 2], ou[n % 2], ALU.add).then_inc(S["out_ready"], 1)

                load_neighbours(0, 0)
                load_neighbours(1, 0)
                for n in range(0, NF, 2):
                    for k in range(1, 9):
                        load_neighbours(n, k)
                        load_neighbours(n + 1, k)
                        if k in (1, 2) and n:
                            total(n - 3 + k)
                        if k in (5, 7) and n + 2 < NF:
                            load_neighbours(n + 2 + (k - 5) // 2, 0)
                        if k in (3, 5):
                            base(n + (k - 3) // 2)
                        if k in (4, 6):
                            base_end(n + (k - 4) // 2)
                end_phase(pool, FOLD)
                end_image(pool)

        @block.scalar
        def _(act):
            act.wait_ge(setup_done, 3)
            with act.Fori(0, B):
                def root(k):
                    act.wait_ge(S["veps_ready"], k + 1)
                    nc.scalar.activation(dev, var, ACT.Sqrt).then_inc(S["std_ready"], 1)

                root(0)
                end_phase(act, STATS)
                for hp in range(2):
                    def take_transposed(n):
                        g = STEPS * hp + n
                        k = 4 if n else 2
                        if g > 1:
                            act.wait_ge(S["qkv_done"], 9 * (g - 1))
                        for j in range(3):
                            act.wait_ge(S["transposed"], 3 * g + j + 1)
                            dst = xlo[g % 2][:, j, 0:k * 128] if j < 2 else xhi[g % 2][:, 0:k * 128]
                            c = 1 if j == 2 else 0
                            nc.scalar.activation(dst.rearrange("p (q v) -> p q v", v=k),
                                                 bank[j][:, 0:k * 128].rearrange("p (v q) -> p q v", v=k),
                                                 ACT.Identity, scale=gnp[:, c:c + 1],
                                                 bias=gnp[:, 2 + c:3 + c]).then_inc(S["xt_ready"], 1)

                    def squares(n, half):
                        act.wait_ge(S["conv_done"], 40 * hp + 5 * n)
                        act.wait_ge(S["tap_used"], 8 * (3 * (8 * hp + n) - 2))
                        for c in range(6 * (n - 1) + 3 * half, 6 * (n - 1) + 3 * half + 3):
                            for z, buf in enumerate((qb, kb)):
                                a_n[0] += 1
                                if a_n[0] > 1:
                                    act.wait_ge(S["act_chain"], a_n[0] - 1)
                                nc.scalar.activation(junk, buf[:, c * SEG:(c + 1) * SEG], ACT.Square,
                                                     accum_out=sq[:, CH * z + c:CH * z + c + 1]).then_inc(S["act_chain"], 1)

                    def move_up(n, t):
                        if n > 1 and t in PE_T:
                            act.wait_ge(S["pe_conv"], 8 * hp + n - 1)
                        elif n > 1:
                            act.wait_ge(S["tap_ready"], 9 * (3 * (8 * hp + n - 2) + POOL_T.index(t) + 1))
                        else:
                            act.wait_ge(S["pre_ready"], 81 * hp + t + 1)
                        nc.scalar.activation(pre[:, t, 0:2, 1:129], pre[:, t, 4:6, 1:129], ACT.Copy).then_inc(S["halo_done"], 1)

                    def sort_v(n):
                        if n > 1 or hp:
                            act.wait_ge(S["v_stored"], 16 * (8 * hp + n - 1))
                        for t in range(3):
                            if t == 0:
                                act.wait_ge(S["pe_conv"], 8 * hp + n)
                                made = bank[6][:, :]
                            else:
                                act.wait_ge(S["tap_used"], 24 * (8 * hp + n - 1) + 8 * (t + 1))
                                made = pool_acc[6 + t]
                            for z in range(2):
                                w0 = (3 * z + t) // 2
                                dst = vst[0].rearrange("p (r a q w) -> p r a q w", a=2, q=128, w=3)[:, :, (z + t) % 2, :, w0]
                                src = made.rearrange("p (r q z) -> p r q z", z=2, q=128)[:, :, :, z]
                                last = nc.scalar.activation(dst, src, ACT.Copy)
                            last.then_inc(S["v_copied"], 1)

                    def tap_products(n, first, last_):
                        for m in range(first, last_):
                            t, j = POOL_T[m // 9], m % 9
                            p = 27 * (8 * hp + n - 1) + m
                            act.wait_ge(S["pre_ready"], 81 * hp + 9 * n + t + 1)
                            if p >= TAPS:
                                act.wait_ge(S["tap_used"], adds_before(p - TAPS))
                            nc.scalar.activation(taps[p % TAPS].rearrange("p (r w) -> p r w", w=128),
                                                 pre[:, t, j // 3:j // 3 + 4, j % 3:j % 3 + 128], ACT.Copy,
                                                 scale=dwt[:, t, j:j + 1]).then_inc(S["tap_ready"], 1)

                    if hp == 0:
                        a_n = [0]
                    take_transposed(0)
                    for n in range(STEPS):
                        if not n:
                            act.wait_ge(S["border_done"], hp + 1)
                        for t in range(9):
                            i = 81 * hp + 9 * n + t
                            if n > 1 and t < 8:
                                tap_products(n - 1, TAPS_AT[t], TAPS_AT[t + 1])
                            if n and 4 <= t < 8:
                                move_up(n, t + 1)
                            if t == 7 and n < STEPS - 1:
                                take_transposed(n + 1)
                            act.wait_ge(S["qkv_done"], i + 1)
                            if n:
                                if t in DVE_T:
                                    act.wait_ge(S["own_halo"], 40 * hp + 5 * (n - 1) + t + 1)
                                else:
                                    act.wait_ge(S["halo_done"], 32 * hp + 4 * (n - 1) + t - 4)
                            src = bank[3 + i % 3]
                            if n == 0:
                                parts = [(0, 64, 1, 2), (64, 128, 0, 2)] if hp == 0 else [(0, 128, 0, 2)]
                                first = 4
                            else:
                                parts = [(0, 64, 0, 4), (64, 128, 0, 3)] if hp and n == STEPS - 1 else [(0, 128, 0, 4)]
                                first = 2
                            for a, z, r0, r1 in parts:
                                last = nc.scalar.activation(
                                    pre[a:z, t, first + r0:first + r1, 1:129],
                                    src[a:z, 128 * r0:128 * r1].rearrange("p (r w) -> p r w", w=128), ACT.Copy)
                            if hp and n == STEPS - 1:
                                last = nc.scalar.activation(pre[64:128, t, 5, 1:129], w_hi[64:128, 0, 0:128], ACT.Copy)
                            last.then_inc(S["pre_ready"], 1)
                        if n:
                            tap_products(n, 0, 3)
                        if n >= 2:
                            sort_v(n - 1)
                        if n:
                            tap_products(n, 3, 6)
                        if n >= 2:
                            squares(n - 1, 0)
                        if n:
                            tap_products(n, 6, 9)
                        if n >= 2:
                            squares(n - 1, 1)
                    tap_products(STEPS - 1, 9, 27)
                    squares(STEPS - 1, 0)
                    squares(STEPS - 1, 1)
                    act.wait_ge(S["act_chain"], 96 * (hp + 1))
                    act.drain().then_inc(S["squared"], 1)
                    sort_v(STEPS - 1)
                    for s in range(2):
                        r = slice(64 * s, 64 * s + CH)
                        act.wait_ge(S["nrm_ready"], 2 * hp + s + 1)
                        nc.scalar.activation(nsq[r, 0:49], nrm[r, 0:49], ACT.Sqrt).then_inc(S["root_ready"], 1)
                    for s in range(2):
                        r = slice(64 * s, 64 * s + CH)
                        act.wait_ge(S["lg_ready"], 2 * hp + s + 1)
                        nc.scalar.activation(ex[r, :], lg[r, :], ACT.Exp, bias=nmx[r, :],
                                             accum_out=ssum[r, :]).then_inc(S["exp_ready"], 1)
                    end_phase(act, QKV0 + 2 * hp)
                    for g in range(32):
                        act.wait_ge(S["mixed"], 32 * hp + g + 1)
                        nc.scalar.activation(ob[:, :, 4 * g:4 * g + 4],
                                             bank[g % 2][:, 0:384].rearrange("p (u c) -> p c u", u=4),
                                             ACT.Copy).then_inc(S["mix_out"], 1)
                    for i in range(32):
                        j, r = i // 4, i % 4
                        if r == 0 and (j >= 2 or hp):
                            act.wait_ge(S[f"x1_stored{j % 2}"], 64 * hp + 16 * (j // 2))
                        if r == 0 and j >= 2:
                            act.wait_ge(S["x1_measured"], 8 * hp + j - 1)
                        act.wait_ge(S["projected"], 32 * hp + i + 1)
                        nc.scalar.activation(x1t[j % 2][:, r, :], bank[4 + i % 3][:, 0:384], ACT.Copy).then_inc(S["lifted"], 1)
                    end_phase(act, MIX0 + 2 * hp)
                root(1)

                def columns_first(g):
                    act.wait_ge(S[f"fk_loaded{g % 2}"], 48 * (g // 2 + 1))
                    if g >= 2:
                        act.wait_ge(S["r_done"], g - 1)
                    nc.scalar.activation(fs[g % 2][0:HM, :, :], fk[g % 2][0:HM, :, 2:2 + C].rearrange("p q w -> p w q"),
                                         ACT.Copy).then_inc(S["fs_ready"], 1)

                columns_first(0)
                for g in range(MG):
                    if g + 1 < MG:
                        columns_first(g + 1)
                    act.wait_ge(S["r_done"], g + 1)
                    if g >= 2:
                        act.wait_ge(S["g_done"], g - 1)
                    nc.scalar.activation(rs[g % 2][0:120, :, :], bank[g % 2][0:120, 0:216].rearrange("p (q v) -> p q v", v=9), ACT.Copy)
                    nc.scalar.activation(res[g % 2][0:48, :, :, :].rearrange("p s q v -> p (s q v)"),
                                         bank[2 + g % 2][0:48, 0:288], ACT.Copy).then_inc(S["r_out"], 1)
                end_phase(act, GRAM)

                def take(n):
                    act.wait_ge(S["summed"], y_at(n, 8))
                    if n >= 2:
                        act.wait_ge(S["out_ready"], n - 1)
                    for q in range(4):
                        last = nc.scalar.activation(ou[n % 2][:, 384 * q:384 * q + 384], bank[4 * (n % 2) + q][:, 0:384], ACT.Copy)
                    last.then_inc(S["taken"], 1)

                for n in range(0, NF, 2):
                    for k in range(9):
                        for c in (n, n + 1):
                            r0, r1 = fold_rows(c, k // 3)
                            kj = k % 3
                            at_ = y_at(c, k)
                            act.wait_ge(S["y_ready"], at_)
                            if at_ > 4:
                                act.wait_ge(S["summed"], at_ - 4)
                            nc.scalar.activation(rows(zz[at_ % 4])[:, r0:r1, kj:kj + WM],
                                                 rows(yy[c % 2])[:, r0:r1, kj:kj + WM], ACT.Copy,
                                                 bias=MAGIC if k % 2 == 0 else -MAGIC).then_inc(S["z_ready"], 1)
                            if k == 0 and n:
                                take(c - 2)
                end_phase(act, FOLD)
                end_image(act)

        @block.vector
        def _(dve):
            dve.wait_ge(setup_done, 3)
            dve.wait_ge(setup_dma, SD)
            for i, t in enumerate(PE_T):
                for j in range(9):
                    last = nc.vector.tensor_scalar(diag[:, i, j, :], c_("ident"), dwt[:, t, j:j + 1], None, ALU.mult)
            last.then_inc(setup_done, 1)

            def quarter_stats(i, loaded, count, read):
                dve.wait_ge(loaded[i % 2], count)
                for g in range(GROUPS):
                    last = nc.vector.bn_stats(bsx[:, g, 6 * i:6 * i + 6], xg[i % 2][:, :, GC * g:GC * g + GC])
                last.then_inc(read, 1)

            for i in range(4):
                quarter_stats(i, first_loaded, 16 * (i // 2 + 1), first_read)
            dve.wait_ge(first_read, 4)
            for g in range(GROUPS):
                last = nc.vector.bn_aggr(mvx[:, g, :], bsx[:, g, :])
            last.then_inc(first_read, 1)
            dve.wait_ge(first_read, 5)

            with dve.Fori(0, B) as b:
                chain = [0]

                def link(ins):
                    chain[0] += 1
                    ins.then_inc(S["dve_chain"], 1)
                    dve.wait_ge(S["dve_chain"], chain[0])

                def group_stats(k):
                    m_ = (mvx, mv)[k]
                    if k:
                        link(nc.vector.tensor_tensor(dev, mvh[:, :, 0], mv[:, :, 0], ALU.subtract))
                        link(nc.vector.tensor_tensor(mv, mvh, mv, ALU.add))
                        link(nc.vector.tensor_scalar(mv, mv, 0.5, None, ALU.mult))
                        link(nc.vector.scalar_tensor_tensor(dev, dev, 0.25, dev, ALU.mult, ALU.mult))
                        nc.vector.tensor_tensor(mv[:, :, 1], mv[:, :, 1], dev, ALU.add).then_inc(S["mv_ready"], 1)
                        dve.wait_ge(S["mv_ready"], 1)
                    dve.wait_ge(S["mean_ready"], k + 1)
                    link(nc.vector.tensor_copy(mean, bank[0][:, 0:GROUPS]))
                    link(nc.vector.tensor_tensor(dev, m_[:, :, 0], mean, ALU.subtract))
                    link(nc.vector.tensor_tensor(dev, dev, dev, ALU.mult))
                    nc.vector.tensor_tensor(var, dev, m_[:, :, 1], ALU.add).then_inc(S["dev_ready"], 1)
                    dve.wait_ge(S["var_ready"], k + 1)
                    nc.vector.tensor_scalar(var, bank[1][:, 0:GROUPS], 1e-5, None, ALU.add).then_inc(S["veps_ready"], 1)
                    dve.wait_ge(S["std_ready"], k + 1)
                    link(nc.vector.reciprocal(rstd, dev))

                group_stats(0)
                link(nc.vector.scalar_tensor_tensor(nbias, mean, -1.0, rstd, ALU.mult, ALU.mult))
                for z, a in enumerate((rstd, nbias)):
                    w_ = wide[:, z, 0:C].rearrange("p (g c) -> p g c", c=GC)
                    link(nc.vector.tensor_copy(w_, a.rearrange("p (g a) -> p g a", a=1).to_broadcast([128, GROUPS, GC])))
                    nc.vector.tensor_copy(wide[:, z, C:256], wide[:, z, 128:192]).then_inc(S["wide_ready"], 1)
                dve.wait_ge(S["col_ready"], 1)
                nc.vector.tensor_copy(gnp, bank[2][:, 0:4]).then_inc(S["gn_ready"], 1)
                end_phase(dve, STATS)

                for hp in range(2):
                    def move_own(t):
                        nc.vector.tensor_copy(pre[:, t, 0:2, 1:129], pre[:, t, 4:6, 1:129]).then_inc(S["own_halo"], 1)

                    for t in DVE_T:
                        dve.wait_ge(S["pre_ready"], 81 * hp + t + 1)
                        move_own(t)
                    for n in range(1, STEPS):
                        for ts in ((0, 1), (2, 3, 4)):
                            summed = [0, 0, 0]

                            def tap(t, j):
                                return pre[:, t, j // 3:j // 3 + 4, j % 3:j % 3 + 128]

                            for j in range(9):
                                for t in ts:
                                    a = acc[t % 3].rearrange("p (r w) -> p r w", w=128)
                                    if j:
                                        dve.wait_ge(S["dve_chain"], summed[t % 3])
                                    else:
                                        dve.wait_ge(S["pre_ready"], 81 * hp + 9 * n + t + 1)
                                        dve.wait_ge(S["own_halo"], 40 * hp + 5 * (n - 1) + t + 1)
                                        done = 40 * hp + 5 * (n - 1) + max(t - 2, 0)
                                        if done > 0:
                                            dve.wait_ge(S["conv_done"], done)
                                    if j == 0:
                                        ins = nc.vector.tensor_scalar(a, tap(t, 0), dwt[:, t, 0:1], None, ALU.mult)
                                    elif j < 8:
                                        ins = nc.vector.scalar_tensor_tensor(a, tap(t, j), dwt[:, t, j:j + 1], a, ALU.mult, ALU.add)
                                    else:
                                        dst = (qb, kb)[t // 3][:, 1536 * (n - 1):1536 * n]
                                        dst = dst.rearrange("p (r w c) -> p r w c", w=128, c=3)[:, :, :, t % 3]
                                        nc.vector.scalar_tensor_tensor(dst, tap(t, 8), dwt[:, t, 8:9], a, ALU.mult, ALU.add).then_inc(S["conv_done"], 1)
                                        if n < STEPS - 1:
                                            dve.wait_ge(S["conv_done"], 40 * hp + 5 * (n - 1) + t + 1)
                                            move_own(t)
                                        continue
                                    ins.then_inc(S["dve_chain"], 1)
                                    chain[0] += 1
                                    summed[t % 3] = chain[0]
                    for s in range(2):
                        r = slice(64 * s, 64 * s + CH)
                        dve.wait_ge(S["norm_done"], hp + 1)
                        nc.vector.tensor_scalar(nrm[r, 0:49], bank[3 + s][r, 0:49], 1e-12, None, ALU.max).then_inc(S["nrm_ready"], 1)
                    for s in range(2):
                        r = slice(64 * s, 64 * s + CH)
                        dve.wait_ge(S["root_ready"], 2 * hp + s + 1)
                        link(nc.vector.reciprocal(rn[r, 0:49], nsq[r, 0:49]))
                        link(nc.vector.tensor_tensor(rq[r, :], rn[r, 0:1], tcol[r, hp:hp + 1], ALU.mult))
                        link(nc.vector.scalar_tensor_tensor(lg[r, :], bank[s][r, 0:CH], rq[r, :], rn[r, 1:49], ALU.mult, ALU.mult))
                        link(nc.vector.tensor_reduce(mx[r, :], lg[r, :], AX, ALU.max))
                        nc.vector.tensor_scalar(nmx[r, :], mx[r, :], -1.0, None, ALU.mult).then_inc(S["lg_ready"], 1)
                    for s in range(2):
                        r = slice(64 * s, 64 * s + CH)
                        dve.wait_ge(S["exp_ready"], 2 * hp + s + 1)
                        link(nc.vector.reciprocal(rsum[r, :], ssum[r, :]))
                        nc.vector.tensor_scalar(ablk[r, 64 * s:64 * s + CH], ex[r, :], rsum[r, :], None, ALU.mult).then_inc(S["ablk_ready"], 1)
                    dve.wait_ge(S["at_done"], hp + 1)
                    nc.vector.tensor_copy(at[:, :], bank[5][:, 0:96])
                    end_phase(dve, QKV0 + 2 * hp)

                    for j in range(8):
                        dve.wait_ge(S["x1_ready"], 32 * hp + 4 * (j + 1))
                        rc = x1t[j % 2].rearrange("p r (a c) -> p (r a) c", c=C)
                        at_ = 6 * j
                        for g in range(GROUPS):
                            last = nc.vector.bn_stats(bst[:, g, at_:at_ + 6], rc[:, :, GC * g:GC * g + GC])
                        last.then_inc(S["x1_measured"], 1)
                    dve.wait_ge(S["x1_measured"], 8 * (hp + 1))
                    for g in range(GROUPS):
                        last = nc.vector.bn_aggr((mvh, mv)[hp][:, g, :], bst[:, g, :])
                    link(last)
                    end_phase(dve, MIX0 + 2 * hp)

                group_stats(1)
                for a, row in ((mean, mrow), (rstd, rrow)):
                    nc.vector.tensor_copy(row[:, 0, :].rearrange("p (g c) -> p g c", c=GC),
                                          a.rearrange("p (g a) -> p g a", a=1).to_broadcast([128, GROUPS, GC])).then_inc(S["rows_ready"], 1)
                dve.wait_ge(S["rows_ready"], 2)
                for i in range(3):
                    dve.wait_ge(S[f"xs{i}"], 16)
                    link(nc.vector.tensor_tensor(xs[i], xs[i], mr, ALU.subtract))
                    nc.vector.tensor_tensor(xs[i], xs[i], rr, ALU.mult).then_inc(S["gn_ready"], 1)

                for g in range(MG):
                    dve.wait_ge(S["g_done"], g + 1)
                    for ki in range(3):
                        dst = gs[:, g, :].rearrange("p (y k) -> p y k", k=9)[:, :, 3 * ki:3 * ki + 3]
                        last = nc.vector.tensor_copy(dst, bank[4 + g % 2][0:NW, 24 * ki:24 * ki + 24].rearrange("p (y k) -> p y k", k=3))
                    last.then_inc(S["g_out"], 1)
                    if g in (8, 9, 11, 13):
                        i = (8, 9, 11, 13).index(g)
                        quarter_stats(i, next_loaded, 16 * (i // 2 + 1), S["next_read"])
                    if g == 14:
                        dve.wait_ge(S["next_read"], 4)
                        for gg_ in range(GROUPS):
                            last = nc.vector.bn_aggr(mvx[:, gg_, :], bsx[:, gg_, :])
                        link(last)
                dve.wait_ge(S["g_out"], MG)
                i72 = c_("i72", NW).rearrange("p (a m) -> p a m", a=1).to_broadcast([NW, MG, NW])
                nc.vector.tensor_tensor(gi, gs, i72, ALU.mult).then_inc(S["gi_ready"], 1)
                dve.wait_ge(S["gi_ready"], 1)
                link(nc.vector.tensor_reduce(sqm, gi, AX, ALU.add))
                dve.wait_ge(S["sq_done"], 1)
                for q in range(3):
                    g0, g1 = (0, 6, 12)[q], (6, 12, 16)[q]
                    last = nc.vector.tensor_tensor(gt[:, g0:g1, :], bank[5 + q][0:NW, 0:(g1 - g0) * NW].rearrange("p (g m) -> p g m", m=NW),
                                                   sqm[:, g0:g1].rearrange("p (g a) -> p g a", a=1).to_broadcast([NW, g1 - g0, NW]), ALU.add)
                link(last)
                link(nc.vector.scalar_tensor_tensor(gt.rearrange("p g m -> p (g m)"), gs.rearrange("p g m -> p (g m)"), -2.0,
                                                    gt.rearrange("p g m -> p (g m)"), ALU.mult, ALU.add))
                bmask = c_("bmask", NW).rearrange("p (a m) -> p a m", a=1).to_broadcast([NW, MG, NW])
                link(nc.vector.tensor_tensor(gt, gt, bmask, ALU.mult))
                for g in range(MG):
                    last = nc.vector.tensor_reduce(d8[:, g, :], gt[:, g, :].rearrange("p (j c) -> p c j", j=9), AX, ALU.add)
                link(last)
                self8 = c_("self8", NW).rearrange("p (a m) -> p a m", a=1).to_broadcast([NW, MG, 8])
                link(nc.vector.tensor_tensor(d8, d8, self8, ALU.add))
                link(nc.vector.tensor_reduce(dmin, d8, AX, ALU.min))
                link(nc.vector.tensor_tensor(e8, d8, dmin.rearrange("p (g a) -> p g a", a=1).to_broadcast([NW, MG, 8]), ALU.is_le))
                w8 = c_("w8", NW).rearrange("p (a m) -> p a m", a=1).to_broadcast([NW, MG, 8])
                link(nc.vector.tensor_tensor(e8, e8, w8, ALU.mult))
                nc.vector.tensor_reduce(best, e8, AX, ALU.max).then_inc(S["best_ready"], 1)
                dve.wait_ge(S["bt_done"], 1)
                link(nc.vector.tensor_copy(bt.rearrange("p j c -> p (j c)"), bank[0][0:MG, 0:NW]))
                u, e, off = tb[0], tb[1], tb[2]
                link(nc.vector.tensor_reduce(u, bt, AX, ALU.min))
                link(nc.vector.tensor_tensor(beq, bt, u.rearrange("p (g a) -> p g a", a=1).to_broadcast([MG, 9, 8]), ALU.is_equal))
                link(nc.vector.tensor_reduce(offc[:, 9:18], beq, AX, ALU.add))
                link(nc.vector.tensor_scalar(u, u, -1.0, 8.0, ALU.mult, ALU.add))
                jr = c_("jrow", MG)
                link(nc.vector.tensor_tensor(e, u, jr, ALU.is_ge))
                link(nc.vector.tensor_tensor(e, e, jr, ALU.add))
                link(nc.vector.tensor_scalar(e, e, 1.0, None, ALU.subtract))
                link(nc.vector.tensor_tensor(u, u, c_("ktab", MG), ALU.add))
                link(nc.vector.scalar_tensor_tensor(u, e, -9.0, u, ALU.mult, ALU.add))
                link(nc.vector.tensor_scalar(tb[3], u, 3.0, None, ALU.is_ge))
                link(nc.vector.tensor_scalar(tb[4], u, 6.0, None, ALU.is_ge))
                link(nc.vector.tensor_tensor(tb[3], tb[3], tb[4], ALU.add))
                link(nc.vector.scalar_tensor_tensor(off, e, float(PLANE), u, ALU.mult, ALU.add))
                link(nc.vector.scalar_tensor_tensor(offc[:, 0:9], tb[3], float(C - 3), off, ALU.mult, ALU.add))
                nc.vector.tensor_copy(tb[5], offc[:, 0:9]).then_inc(S["offc_ready"], 1)
                dve.wait_ge(S["offc_ready"], 1)
                link(nc.vector.tensor_tensor(ib, tb[5].rearrange("p (j a) -> p j a", a=1).to_broadcast([MG, 9, NF]),
                                             c_("ctab", MG).rearrange("p (a n) -> p a n", a=1).to_broadcast([MG, 9, NF]), ALU.add))
                link(nc.vector.tensor_copy(idxb[:, :, :], ib))
                dve.wait_ge(S["rep_done"], 1)
                link(nc.vector.tensor_copy(rep, bank[1][:, 0:18]))
                link(nc.vector.tensor_tensor(ta, rep[:, 0:9], c_("sela"), ALU.mult))
                link(nc.vector.tensor_reduce(ca, ta, AX, ALU.add))
                link(nc.vector.tensor_scalar(ia, c_("base"), ca, None, ALU.add))
                link(nc.vector.tensor_copy(idxa[:, :], ia))
                link(nc.vector.tensor_tensor(tk, c_("selk").rearrange("p (k j) -> p k j", k=9),
                                             rep[:, 9:18].rearrange("p (a j) -> p a j", a=1).to_broadcast([128, 9, 9]), ALU.mult))
                link(nc.vector.tensor_reduce(ck, tk, AX, ALU.add))
                end_phase(dve, GRAM)

                def product(n, k):
                    at_ = y_at(n, k)
                    r0, r1 = fold_rows(n, k // 3)
                    ki, kj = k // 3, k % 3
                    if k == 0:
                        dve.wait_ge(S[f"ff_loaded{n % 4}"], 32 * (n // 4 + 1))
                    dve.wait_ge(S[f"hh_loaded{n % 4}"], b * (144 * NF // 4) + 144 * (n // 4) + 16 * (k + 1))
                    a = rows(ff[n % 4])[:, r0:r1, kj:kj + WM]
                    z = rows(hh[n % 4])[:, 2 - ki + r0:2 - ki + r1, 0:WM]
                    nc.vector.scalar_tensor_tensor(rows(yy[n % 2])[:, r0:r1, kj:kj + WM], a, ck[:, k:k + 1], z,
                                                   ALU.mult, ALU.mult).then_inc(S["y_ready"], 1)

                def above(n, k):
                    at_ = y_at(n, k)
                    r0, r1 = fold_rows(n, k // 3)
                    kj = k % 3
                    dve.wait_ge(S["z_ready"], at_)
                    if at_ > 4:
                        dve.wait_ge(S["summed"], at_ - 4)
                    nc.vector.scalar_tensor_tensor(rows(gg[at_ % 4])[:, r0:r1, kj:kj + WM],
                                                   rows(zz[at_ % 4])[:, r0:r1, kj:kj + WM],
                                                   -MAGIC if k % 2 == 0 else MAGIC,
                                                   rows(yy[n % 2])[:, r0:r1, kj:kj + WM],
                                                   ALU.add, ALU.is_gt).then_inc(S["g_ready"], 1)

                def finish(n):
                    dve.wait_ge(S["out_ready"], n)
                    dve.wait_ge(S["summed"], y_at(n, 8))
                    dve.wait_ge(S["base_ready"], n + 1)
                    b0 = 4 * (n % 2)
                    for q in range(4):
                        last = nc.vector.tensor_tensor(fm[n % 2][:, 384 * q:384 * q + 384], bank[b0 + q][:, 0:384],
                                                       fm[n % 2][:, 384 * q:384 * q + 384], ALU.add)
                    last.then_inc(S["out_ready"], 1)

                for n in range(0, NF, 2):
                    for k in range(9):
                        product(n, k)
                        product(n + 1, k)
                        above(n, k)
                        above(n + 1, k)
                        dve.wait_ge(S["g_ready"], y_at(n + 1, k))
                finish(NF - 2)
                finish(NF - 1)
                end_phase(dve, FOLD)
                end_image(dve)

        @block.tensor
        def _(pe):
            pe.wait_ge(setup_done, 4)
            pe.wait_ge(setup_dma, SD)
            pe.wait_ge(first_read, 5)
            mm = nc.tensor.matmul
            with pe.Fori(0, B):
                def average(k):
                    if k:
                        pe.wait_ge(S["mv_ready"], 1)
                    mm(bank[0][:, 0:GROUPS], c_("avg"), (mvx, mv)[k][:, :, 0], start=True, stop=True).then_inc(S["mean_ready"], 1)
                    pe.wait_ge(S["dev_ready"], k + 1)
                    mm(bank[1][:, 0:GROUPS], c_("avg"), var, start=True, stop=True).then_inc(S["var_ready"], 1)

                average(0)
                pe.wait_ge(S["wide_ready"], 2)
                one = c_("ones")[0:1, 0:1]
                for z in range(2):
                    for h in range(2):
                        last = mm(bank[2][:, 2 * z + h:2 * z + h + 1], wide[0:1, z, 128 * h:128 * h + 128], one, start=True, stop=True)
                last.then_inc(S["col_ready"], 1)
                end_phase(pe, STATS)

                for hp in range(2):
                    def transposes(n):
                        g = STEPS * hp + n
                        k = 4 if n else 2
                        dmas = 2 * (g + 1) + 1 + (1 if hp and n == STEPS - 1 else 0)
                        pe.wait_ge(S["xa_loaded"], 16 * dmas)
                        if g:
                            pe.wait_ge(S["xt_ready"], 3 * g)
                        xv = xa.rearrange("p s (v c) -> p s v c", c=C)
                        for j in range(2):
                            for v in range(k):
                                last = nc.tensor.transpose(bank[j][:, 128 * v:128 * v + 128], xv[:, j, v, 0:128], c_("ident"))
                            last.then_inc(S["transposed"], 1)
                        for v in range(k):
                            for s in range(2):
                                last = mm(bank[2][64 * s:64 * s + 64, 128 * v:128 * v + 128], xv[:, s, v, 128:C], c_("ident"), start=True, stop=True)
                        last.then_inc(S["transposed"], 1)

                    def convolve(n, t):
                        pe.wait_ge(S["pre_ready"], 81 * hp + 9 * n + t + 1)
                        if hp or n > 1:
                            pe.wait_ge(S["v_copied"], 3 * (8 * hp + n - 2) + t - 5)
                        for j in range(9):
                            last = mm(bank[t][:, :], diag[:, t - 6, j, :], pre[:, t, j // 3:j // 3 + 4, j % 3:j % 3 + 128],
                                      start=(j == 0), stop=(j == 8))
                        last.then_inc(S["pe_conv"], 1)

                    transposes(0)
                    for n in range(STEPS):
                        k = 4 if n else 2
                        g = STEPS * hp + n
                        pe.wait_ge(S["xt_ready"], 3 * (g + 1))
                        if n + 1 < STEPS:
                            transposes(n + 1)
                        for t in range(9):
                            if n > 1 and t == 2:
                                convolve(n - 1, PE_T[0])
                            i = 9 * g + t
                            if i >= 3:
                                pe.wait_ge(S["pre_ready"], i - 2)
                            for s in range(2):
                                dst = bank[3 + i % 3][64 * s:64 * s + 64, 0:128 * k]
                                mm(dst, w_lo[:, 64 * t:64 * t + 64], xlo[g % 2][:, s, 0:128 * k], start=True, stop=False)
                                last = mm(dst, w_hi[:, s, 64 * t:64 * t + 64], xhi[g % 2][:, 0:128 * k], start=False, stop=True)
                            last.then_inc(S["qkv_done"], 1)
                    for t in PE_T:
                        convolve(STEPS - 1, t)
                    pe.wait_ge(S["xt_ready"], 3 * STEPS * (hp + 1))
                    pe.wait_ge(S["conv_done"], 40 * (hp + 1))
                    pe.wait_ge(S["tap_used"], 24 * (8 * hp + 8) - 16)
                    qv = qb.rearrange("p (c u) -> p u c", u=SEG)
                    kv = kb.rearrange("p (c u) -> p u c", u=SEG)
                    for u in range(SEG):
                        for s in range(2):
                            r = slice(64 * s, 64 * s + 64)
                            last = mm(bank[s][64 * s:64 * s + CH, 0:CH], qv[r, u, :], kv[r, u, :],
                                      start=(u == 0), stop=(u == SEG - 1))
                    pe.wait_ge(S["squared"], hp + 1)
                    for s in range(2):
                        r = slice(64 * s, 64 * s + 64)
                        mm(bank[3 + s][64 * s:64 * s + CH, 0:1], sq[r, 0:CH], c_("ones")[r, 0:1], start=True, stop=True)
                        last = mm(bank[3 + s][64 * s:64 * s + CH, 1:49], c_("ones")[r, 0:CH], sq[r, CH:2 * CH], start=True, stop=True)
                    last.then_inc(S["norm_done"], 1)
                    pe.wait_ge(S["ablk_ready"], 2 * (hp + 1))
                    mm(bank[5][:, 0:96], ablk[:, :], c_("icol"), start=True, stop=True).then_inc(S["at_done"], 1)
                    end_phase(pe, QKV0 + 2 * hp)

                    KR = 64 + CH
                    pe.wait_ge(S["v_loaded"], 192 * (hp + 1))
                    for g in range(32):
                        if g >= 2:
                            pe.wait_ge(S["mix_out"], 32 * hp + g - 1)
                        for i in range(4):
                            last = mm(bank[g % 2][:, 96 * i:96 * i + 96], vbf[0:KR, 4 * g + i, :], at[0:KR, :], start=True, stop=True)
                        last.then_inc(S["mixed"], 1)
                    pe.wait_ge(S["mix_out"], 32 * (hp + 1))
                    for i in range(32):
                        if i >= 3:
                            pe.wait_ge(S["lifted"], 32 * hp + i - 2)
                        bk = bank[4 + i % 3]
                        w3 = obf[:, i, :].rearrange("p (q w) -> p w q", w=3)
                        mm(bk[:, 0:C], w3[:, 0, :], pw[:, 0, :], start=True, stop=False)
                        mm(bk[:, 0:C], w3[:, 1, :], pw[:, 2, :], start=False, stop=True)
                        mm(bk[:, C:2 * C], w3[:, 1, :], pw[:, 3, :], start=True, stop=False)
                        mm(bk[:, C:2 * C], w3[:, 2, :], pw[:, 1, :], start=False, stop=True).then_inc(S["projected"], 1)
                    end_phase(pe, MIX0 + 2 * hp)
                average(1)

                selv = sels[:, 0:15 * NW].rearrange("p (k w m) -> p k w m", k=3, w=WB)
                selev = sels[:, 15 * NW:21 * NW].rearrange("p (n m) -> p n m", m=NW)

                def combine(g):
                    pe.wait_ge(S["r_out"], g + 1)
                    if g >= 2:
                        pe.wait_ge(S["g_out"], g - 1)
                    dst = bank[4 + g % 2][0:NW, 0:NW]
                    for kj in range(3):
                        for wl in range(WB):
                            v = wl + 2 - kj
                            mm(dst, selv[0:120, kj, wl, :], rs[g % 2][0:120, :, v:v + 3], start=(kj == 0 and wl == 0), stop=False)
                    for n, (kj, a, _) in enumerate(EDGES):
                        v = a % 2 + 2 - kj
                        last = mm(dst, selev[0:48, n, :], res[g % 2][0:48, a // 2, :, v:v + 3], start=False, stop=(n == 5))
                    last.then_inc(S["g_done"], 1)

                pe.wait_ge(S["sels_loaded"], 16)
                for g in range(MG):
                    pe.wait_ge(S[f"fk_loaded{g % 2}"], 48 * (g // 2 + 1))
                    pe.wait_ge(S["fs_ready"], g + 1)
                    if g >= 2:
                        pe.wait_ge(S["r_out"], g - 1)
                    f, st = fk[g % 2], fs[g % 2]
                    for w in range(0, WM, WB):
                        mm(bank[g % 2][0:120, 0:216], st[0:HM, w:w + WB, :], f[0:HM, :, w:w + WB + 4],
                           start=(w == 0), stop=(w == WM - WB))
                    for side in range(2):
                        w = side * WM
                        last = mm(bank[2 + g % 2][0:48, 144 * side:144 * side + 144], st[0:HM, w:w + 2, :],
                                  f[0:HM, :, w:w + 6], start=True, stop=True)
                    last.then_inc(S["r_done"], 1)
                    if g:
                        combine(g - 1)
                combine(MG - 1)
                pe.wait_ge(S["gi_ready"], 1)
                for q in range(3):
                    g0, g1 = (0, 6, 12)[q], (6, 12, 16)[q]
                    last = mm(bank[5 + q][0:NW, 0:(g1 - g0) * NW], c_("ones")[0:NW, 0:NW], gif[:, g0 * NW:g1 * NW], start=True, stop=True)
                last.then_inc(S["sq_done"], 1)
                pe.wait_ge(S["best_ready"], 1)
                nc.tensor.transpose(bank[0][0:MG, 0:NW], best, c_("ident")[0:NW, 0:NW]).then_inc(S["bt_done"], 1)
                pe.wait_ge(S["offc_ready"], 1)
                mm(bank[1][:, 0:18], c_("rep", MG), offc, start=True, stop=True).then_inc(S["rep_done"], 1)
                end_phase(pe, GRAM)

                def add_up(n, k):
                    at_ = y_at(n, k)
                    r0, r1 = fold_rows(n, k // 3)
                    kj = k % 3
                    b0 = 4 * (n % 2)
                    if k == 0:
                        if n >= 2:
                            pe.wait_ge(S["taken"], n - 1)
                        for q in range(4):
                            kind = 0 if n == q == 0 else 2 if (n, q) == (NF - 1, 3) else 1
                            mm(bank[b0 + q][:, 0:384], ident_b[:, :], left_b[:, kind, :], start=True, stop=False, skip_group_check=True)
                    pe.wait_ge(S["g_ready"], at_)
                    for wgt, src in ((c_("ident"), zz[at_ % 4]), (ident_b[:, :], gg[at_ % 4])):
                        for q in range(4):
                            a, z = max(2 * q, r0), min(2 * q + 2, r1)
                            if a < z:
                                dst = bank[b0 + q][:, 0:384].rearrange("p (r w) -> p r w", w=C)[:, a - 2 * q:z - 2 * q, kj:kj + WM]
                                last = mm(dst, wgt, rows(src)[:, a:z, kj:kj + WM], start=False, stop=(k == 8), skip_group_check=True)
                    last.then_inc(S["summed"], 1)

                for n in range(0, NF, 2):
                    for k in range(9):
                        add_up(n, k)
                        add_up(n + 1, k)
                end_phase(pe, FOLD)
                end_image(pe)


def kernel(x, L0_conv_qkv_w, L0_conv_dw_w, L0_conv_proj_w, L0_conv_temperature):
    import concourse.bacc as bacc
    from concourse.bass_utils import run_bass_kernel_spmd

    x = np.ascontiguousarray(x)
    B = x.shape[0]
    nc = bacc.Bacc("TRN2", target_bir_lowering=False, num_devices=1)
    dw = np.ascontiguousarray(np.asarray(L0_conv_dw_w).reshape(9, 9, THIRD).transpose(2, 1, 0))
    temp = np.ascontiguousarray(np.repeat(np.asarray(L0_conv_temperature).reshape(2, 2).T, 64, axis=0))
    arrays = {"x": x, "qkv_w": np.ascontiguousarray(L0_conv_qkv_w), "dw_w": dw,
              "proj_w": np.ascontiguousarray(L0_conv_proj_w), "temp": temp, "cst": const_table()}
    args = [nc.dram_tensor(f"in_{k}", a.shape, F32, kind="ExternalInput").ap() for k, a in arrays.items()]
    out = nc.dram_tensor("out", x.shape, F32, kind="ExternalOutput").ap()
    motif_kernel(nc, *args, out, B)
    r = run_bass_kernel_spmd(nc, [{f"in_{k}": a for k, a in arrays.items()}], core_ids=[0])
    return r.results[0]["out"]
```
